# Optimizing a Trainium2 kernel written in Bass

```python
import numpy as np
import jax
import jax.numpy as jnp

def _softmax(x, axis=-1):
    return jax.nn.softmax(x, axis=axis)

def _gelu(x):
    return jax.nn.gelu(x, approximate=True)

def _silu(x):
    return jax.nn.silu(x)

def _sigmoid(x):
    return jax.nn.sigmoid(x)

def _layernorm(x, axis=-1, eps=1e-05):
    m = jnp.mean(x, axis=axis, keepdims=True)
    v = jnp.var(x, axis=axis, keepdims=True)
    return (x - m) / jnp.sqrt(v + eps)

def _scatter_add(tgt, idx, src, axis=0):
    return tgt.at[idx].add(src)

def _segment_sum(src, seg, n):
    return jax.ops.segment_sum(src, seg, n)
kernel_name = 'mk_xattn_ffn_d2_seqx_r4_9d0046'

def setup_inputs(seed: int=0):
    np.random.seed(seed)
    _w = jnp.asarray

    def _rec_inputs():
        import jax
        import jax.numpy as jnp
        _rk = jax.random.key(seed)
        x = 7.22e-05 + 1 * jax.random.normal(jax.random.fold_in(_rk, 1), (2, 512, 1024), jnp.float32)
        _lenS = 512 - jax.random.randint(jax.random.fold_in(_rk, 7), (2,), 0, max(1, 512 // 4) + 1, jnp.int32)
        _lenS2 = 1024 - jax.random.randint(jax.random.fold_in(_rk, 8), (2,), 0, max(1, 1024 // 4) + 1, jnp.int32)
        _ctx_4096P = jax.random.normal(jax.random.fold_in(_rk, 11), (2, 16, 1024), jnp.float32)
        _ctx_4096c = jax.random.dirichlet(jax.random.fold_in(_rk, 511), 0.3 * jnp.ones((16,), jnp.float32), (2, 1024))
        _ctx_4096t = jnp.einsum('bsk,bkd->bsd', _ctx_4096c, _ctx_4096P)
        _ctx_4096t = _ctx_4096t * jax.lax.rsqrt(jnp.mean(jnp.square(_ctx_4096t)) + 1e-12) * 0.953939
        ctx_4096 = 2.81802e-05 + 1.00001 * (_ctx_4096t + 0.3 * jax.random.normal(jax.random.fold_in(_rk, 611), (2, 1024, 1024), jnp.float32))
        return (x, ctx_4096)
    x, ctx_4096 = _rec_inputs()

    def _L0_xattn_setup():
        import jax, jax.numpy as jnp
        import numpy as np
        HIDDEN = 1024
        N_HEADS = 32
        N_KV_HEADS = 8
        HEAD_DIM = HIDDEN // N_HEADS
        N_REP = N_HEADS // N_KV_HEADS
        EPS = 1e-05

        def _rmsnorm(x, w):
            xf = x.astype(jnp.float32)
            var = jnp.mean(xf * xf, axis=-1, keepdims=True)
            return (xf * jax.lax.rsqrt(var + EPS)).astype(x.dtype) * w
        key = jax.random.key(seed)
        ks = jax.random.split(key, 7)
        B, Q, K = (2, 256, 512)
        scale = 0.02
        return {'hidden_states': jax.random.normal(ks[0], (B, Q, HIDDEN), jnp.float32), 'encoder_hidden_states': jax.random.normal(ks[1], (B, K, HIDDEN), jnp.float32), 'wq': jax.random.normal(ks[2], (N_HEADS * HEAD_DIM, HIDDEN), jnp.float32) * scale, 'wk': jax.random.normal(ks[3], (N_KV_HEADS * HEAD_DIM, HIDDEN), jnp.float32) * scale, 'wv': jax.random.normal(ks[4], (N_KV_HEADS * HEAD_DIM, HIDDEN), jnp.float32) * scale, 'wo': jax.random.normal(ks[5], (HIDDEN, N_HEADS * HEAD_DIM), jnp.float32) * scale, 'ln_w': jnp.ones((HIDDEN,), jnp.float32)}
    _L0_xattn_all = _L0_xattn_setup()
    _L0_xattn_in = {k: v for k, v in _L0_xattn_all.items() if k in ('wq', 'wk', 'wv', 'wo', 'ln_w')}
    del _L0_xattn_all

    def _L0_ffn_setup():
        import jax, jax.numpy as jnp
        import numpy as np
        R = 16
        NUM_EXPERTS = 8
        TOP_K = 2
        LORA_ALPHA = 32
        SCALING = LORA_ALPHA / R
        key = jax.random.key(seed)
        ks = jax.random.split(key, 6)
        d_in, d_out = (1024, 1024)
        x = jax.random.normal(ks[0], (4, 512, d_in), dtype=jnp.float32)
        W_base = jax.random.normal(ks[1], (d_out, d_in), dtype=jnp.float32) * 0.02
        b_base = jax.random.normal(ks[2], (d_out,), dtype=jnp.float32) * 0.02
        W_router = jax.random.normal(ks[3], (NUM_EXPERTS, d_in), dtype=jnp.float32) * 0.01
        A = jax.random.normal(ks[4], (NUM_EXPERTS, R, d_in), dtype=jnp.float32) * 0.02
        B = jax.random.normal(ks[5], (NUM_EXPERTS, d_out, R), dtype=jnp.float32) * 0.02
        return {'x': x, 'W_base': W_base, 'b_base': b_base, 'W_router': W_router, 'A': A, 'B': B}
    _L0_ffn_all = _L0_ffn_setup()
    _L0_ffn_in = {k: v for k, v in _L0_ffn_all.items() if k in ('W_base', 'b_base', 'W_router', 'A', 'B')}
    del _L0_ffn_all

    def _L1_xattn_setup():
        import jax, jax.numpy as jnp
        import numpy as np
        import math
        HIDDEN = 1024
        N_HEADS = 32
        HEAD_DIM = 128
        N_KV_HEADS = 4
        N_GROUPS = N_HEADS // N_KV_HEADS
        key = jax.random.key(seed)
        ks = jax.random.split(key, 6)
        B, NL, S = (8, 64, 1024)
        latents = jax.random.normal(ks[0], (B, NL, HIDDEN), dtype=jnp.float32)
        context = jax.random.normal(ks[1], (B, S, HIDDEN), dtype=jnp.float32)
        scale = 1.0 / math.sqrt(HIDDEN)
        Wq = jax.random.normal(ks[2], (HIDDEN, N_HEADS * HEAD_DIM), dtype=jnp.float32) * scale
        Wk = jax.random.normal(ks[3], (HIDDEN, N_KV_HEADS * HEAD_DIM), dtype=jnp.float32) * scale
        Wv = jax.random.normal(ks[4], (HIDDEN, N_KV_HEADS * HEAD_DIM), dtype=jnp.float32) * scale
        Wo = jax.random.normal(ks[5], (N_HEADS * HEAD_DIM, HIDDEN), dtype=jnp.float32) * scale
        return {'latents': latents, 'context': context, 'Wq': Wq, 'Wk': Wk, 'Wv': Wv, 'Wo': Wo}
    _L1_xattn_all = _L1_xattn_setup()
    _L1_xattn_in = {k: v for k, v in _L1_xattn_all.items() if k in ('Wq', 'Wk', 'Wv', 'Wo')}
    del _L1_xattn_all

    def _L1_ffn_setup():
        import jax, jax.numpy as jnp
        import numpy as np
        IN_F = 1024
        OUT_F = 1024
        RANK = 8
        NUM_EXPERTS = 64
        TOP_K = 16
        ROUTER_DIM = 16
        ALPHA = 32
        SCALING = ALPHA / TOP_K
        BOTTLENECK = NUM_EXPERTS * RANK
        key = jax.random.key(seed)
        ks = jax.random.split(key, 5)
        x = jax.random.normal(ks[0], (4, 1024, IN_F), dtype=jnp.float32)
        bound_a = float(np.sqrt(6.0 / IN_F))
        A_w = jax.random.uniform(ks[1], (BOTTLENECK, IN_F), jnp.float32, -bound_a, bound_a)
        B_w = jax.random.normal(ks[2], (OUT_F, BOTTLENECK), dtype=jnp.float32) * 0.02
        Wq_w = jax.random.normal(ks[3], (ROUTER_DIM, IN_F), dtype=jnp.float32) * 0.02
        keys = jax.random.normal(ks[4], (NUM_EXPERTS, ROUTER_DIM), dtype=jnp.float32) * 0.01
        return {'x': x, 'A_w': A_w, 'B_w': B_w, 'Wq_w': Wq_w, 'keys': keys}
    _L1_ffn_all = _L1_ffn_setup()
    _L1_ffn_in = {k: v for k, v in _L1_ffn_all.items() if k in ('A_w', 'B_w', 'Wq_w', 'keys')}
    del _L1_ffn_all
    return {'x': x, 'ctx_4096': ctx_4096, 'L0_xattn_wq': _L0_xattn_in['wq'], 'L0_xattn_wk': _L0_xattn_in['wk'], 'L0_xattn_wv': _L0_xattn_in['wv'], 'L0_xattn_wo': _L0_xattn_in['wo'], 'L0_xattn_ln_w': _L0_xattn_in['ln_w'], 'L0_ffn_W_base': _L0_ffn_in['W_base'], 'L0_ffn_b_base': _L0_ffn_in['b_base'], 'L0_ffn_W_router': _L0_ffn_in['W_router'], 'L0_ffn_A': _L0_ffn_in['A'], 'L0_ffn_B': _L0_ffn_in['B'], 'L1_xattn_Wq': _L1_xattn_in['Wq'], 'L1_xattn_Wk': _L1_xattn_in['Wk'], 'L1_xattn_Wv': _L1_xattn_in['Wv'], 'L1_xattn_Wo': _L1_xattn_in['Wo'], 'L1_ffn_A_w': _L1_ffn_in['A_w'], 'L1_ffn_B_w': _L1_ffn_in['B_w'], 'L1_ffn_Wq_w': _L1_ffn_in['Wq_w'], 'L1_ffn_keys': _L1_ffn_in['keys']}

def reference(x, ctx_4096, L0_xattn_wq, L0_xattn_wk, L0_xattn_wv, L0_xattn_wo, L0_xattn_ln_w, L0_ffn_W_base, L0_ffn_b_base, L0_ffn_W_router, L0_ffn_A, L0_ffn_B, L1_xattn_Wq, L1_xattn_Wk, L1_xattn_Wv, L1_xattn_Wo, L1_ffn_A_w, L1_ffn_B_w, L1_ffn_Wq_w, L1_ffn_keys):
    import jax
    import jax.numpy as jnp

    def _L0_xattn_ref(hidden_states, encoder_hidden_states, wq, wk, wv, wo, ln_w):
        import jax, jax.numpy as jnp
        import numpy as np
        HIDDEN = 1024
        N_HEADS = 32
        N_KV_HEADS = 8
        HEAD_DIM = HIDDEN // N_HEADS
        N_REP = N_HEADS // N_KV_HEADS
        EPS = 1e-05

        def _rmsnorm(x, w):
            xf = x.astype(jnp.float32)
            var = jnp.mean(xf * xf, axis=-1, keepdims=True)
            return (xf * jax.lax.rsqrt(var + EPS)).astype(x.dtype) * w
        B, Qlen, _ = hidden_states.shape
        _, Klen, _ = encoder_hidden_states.shape
        x = _rmsnorm(hidden_states, ln_w)
        q = jnp.einsum('bqd,hd->bqh', x, wq).reshape(B, Qlen, N_HEADS, HEAD_DIM)
        k = jnp.einsum('bkd,hd->bkh', encoder_hidden_states, wk).reshape(B, Klen, N_KV_HEADS, HEAD_DIM)
        v = jnp.einsum('bkd,hd->bkh', encoder_hidden_states, wv).reshape(B, Klen, N_KV_HEADS, HEAD_DIM)
        q = q.transpose(0, 2, 1, 3)
        k = k.transpose(0, 2, 1, 3)
        v = v.transpose(0, 2, 1, 3)
        k = jnp.repeat(k, N_REP, axis=1)
        v = jnp.repeat(v, N_REP, axis=1)
        scores = jnp.einsum('bhqd,bhkd->bhqk', q, k) / np.sqrt(HEAD_DIM).astype(np.float32)
        attn = jax.nn.softmax(scores.astype(jnp.float32), axis=-1).astype(q.dtype)
        out = jnp.einsum('bhqk,bhkd->bhqd', attn, v)
        out = out.transpose(0, 2, 1, 3).reshape(B, Qlen, HIDDEN)
        return jnp.einsum('bqh,dh->bqd', out, wo)

    def _L0_ffn_ref(x, W_base, b_base, W_router, A, B):
        import jax, jax.numpy as jnp
        import numpy as np
        R = 16
        NUM_EXPERTS = 8
        TOP_K = 2
        LORA_ALPHA = 32
        SCALING = LORA_ALPHA / R
        orig_shape = x.shape
        d_in = x.shape[-1]
        x_flat = x.reshape(-1, d_in)
        logits = x_flat @ W_router.T
        probs = jax.nn.softmax(logits, axis=-1)
        topk_probs, topk_idx = jax.lax.top_k(probs, TOP_K)
        topk_probs = topk_probs / jnp.sum(topk_probs, axis=-1, keepdims=True)
        onehot = jax.nn.one_hot(topk_idx, NUM_EXPERTS, dtype=x.dtype)
        combine = jnp.einsum('nk,nke->ne', topk_probs, onehot)
        h = jnp.einsum('nd,erd->ner', x_flat, A)
        hw = h * combine[:, :, None]
        expert_out = jnp.einsum('ner,eor->no', hw, B) * SCALING
        base_out = x_flat @ W_base.T + b_base
        out = base_out + expert_out
        return out.reshape(*orig_shape[:-1], W_base.shape[0])

    def _L1_xattn_ref(latents, context, Wq, Wk, Wv, Wo):
        import jax, jax.numpy as jnp
        import numpy as np
        import math
        HIDDEN = 1024
        N_HEADS = 32
        HEAD_DIM = 128
        N_KV_HEADS = 4
        N_GROUPS = N_HEADS // N_KV_HEADS
        b, q_len, _ = latents.shape
        kv_len = q_len + context.shape[1]
        hidden_states = jnp.concatenate([context, latents], axis=1)
        q = (latents @ Wq).reshape(b, q_len, N_KV_HEADS, N_GROUPS, HEAD_DIM)
        k = (hidden_states @ Wk).reshape(b, kv_len, N_KV_HEADS, HEAD_DIM)
        v = (hidden_states @ Wv).reshape(b, kv_len, N_KV_HEADS, HEAD_DIM)
        scale = 1.0 / math.sqrt(HEAD_DIM)
        scores = jnp.einsum('bqhgd,bkhd->bhgqk', q, k) * scale
        attn = jax.nn.softmax(scores.astype(jnp.float32), axis=-1).astype(q.dtype)
        out = jnp.einsum('bhgqk,bkhd->bqhgd', attn, v)
        out = out.reshape(b, q_len, N_HEADS * HEAD_DIM)
        return out @ Wo

    def _L1_ffn_ref(x, A_w, B_w, Wq_w, keys):
        import jax, jax.numpy as jnp
        import numpy as np
        IN_F = 1024
        OUT_F = 1024
        RANK = 8
        NUM_EXPERTS = 64
        TOP_K = 16
        ROUTER_DIM = 16
        ALPHA = 32
        SCALING = ALPHA / TOP_K
        BOTTLENECK = NUM_EXPERTS * RANK
        q = jnp.einsum('bsd,rd->bsr', x, Wq_w)
        scores = jnp.einsum('bsr,er->bse', q, keys)
        top_vals, top_idx = jax.lax.top_k(scores, TOP_K)
        top_w = jax.nn.softmax(top_vals, axis=-1)
        gate = jnp.sum(jax.nn.one_hot(top_idx, NUM_EXPERTS, dtype=top_w.dtype) * top_w[..., None], axis=-2)
        z = jnp.einsum('bsd,nd->bsn', x, A_w)
        z = z.reshape(*z.shape[:-1], NUM_EXPERTS, RANK)
        z_gated = (z * gate[..., None]).reshape(*z.shape[:-2], BOTTLENECK)
        out = jnp.einsum('bsn,on->bso', z_gated, B_w) * SCALING
        return out
    x = x + _L0_xattn_ref(_layernorm(x, axis=-1), ctx_4096, L0_xattn_wq, L0_xattn_wk, L0_xattn_wv, L0_xattn_wo, L0_xattn_ln_w)
    x = x + _L0_ffn_ref(_layernorm(x, axis=-1), L0_ffn_W_base, L0_ffn_b_base, L0_ffn_W_router, L0_ffn_A, L0_ffn_B)
    x = x + _L1_xattn_ref(_layernorm(x, axis=-1), ctx_4096, L1_xattn_Wq, L1_xattn_Wk, L1_xattn_Wv, L1_xattn_Wo)
    x = x + _L1_ffn_ref(_layernorm(x, axis=-1), L1_ffn_A_w, L1_ffn_B_w, L1_ffn_Wq_w, L1_ffn_keys)
    return x

_drawn_inputs = setup_inputs


def setup_inputs(seed=0):
    import zlib

    import numpy as np

    out = dict(_drawn_inputs(seed))
    spreads = {'L0_xattn_ln_w': (1.0, 0.6)}
    factors = {'L0_ffn_b_base': 3.602}
    for name, (base, spread) in spreads.items():
        noise = np.random.default_rng([zlib.crc32(name.encode()), seed]).standard_normal(out[name].shape)
        drawn = base * np.exp(spread * noise) if base else spread * noise
        out[name] = jnp.asarray(drawn.astype(out[name].dtype))
    for name, factor in factors.items():
        out[name] = (out[name] * factor).astype(out[name].dtype)
    return out
```

```python
from contextlib import ExitStack

import concourse.bass as bass
from concourse import mybir

F32 = mybir.dt.float32
F32R = mybir.dt.float32r
ALU = mybir.AluOpType
ACT = mybir.ActivationFunctionType
X = mybir.AxisListType.X
ds = bass.ds

P = 128
B, T, D = 2, 512, 1024
S = 1024
DC = D // P
TT = T // P
H0, KV0, HD0 = 32, 8, 32
R0 = H0 // KV0
H1, KV1, HD1 = 32, 4, 128
R1 = H1 // KV1
S1 = S + T
C0, C1 = S // P, S1 // P
E0, RK0, TOP0, ALPHA0 = 8, 16, 2, 32
E1, RK1, TOP1, ALPHA1 = 64, 8, 16, 32
RD1 = 16
N1 = E1 * RK1
ZB = N1 // P
SCALE0 = 1.0 / float(HD0) ** 0.5
SCALE1 = 1.0 / float(HD1) ** 0.5
GAIN0 = ALPHA0 / RK0
GAIN1 = ALPHA1 / TOP1
EPS = 1e-5
LOWEST = -3.0e38

def cols_of(w):
    return 512 if w < G_WO0 or G_Z <= w < G_BW else D


G_KV0, G_K1, G_V1, G_WO0, G_A0, G_BASE, G_B0 = 0, 8, 16, 24, 32, 33, 41
G_KV1, G_WO1, G_Z, G_BW = 42, 50, 82, 90
NG = 94
NU = KV0 + H1
NTILE = 2 * H0 * TT
NCH0, NCH1 = H0 * C0, H1 * C1
NCHUNK = NCH0 + NCH1
A_KV0, A_K1, A_V1, A_WO0, A_BASE, A_KV1, A_WO1, A_BW = 0, 8, 16, 24, 32, 40, 48, 80
NACC = 88
X_WO0, X_B0, X_WO1, X_BW = 0, 8, 9, 41
NA = 45
NDONE = 7 * (NACC // 8)
NEV = 32
NST = 28
NDV = 35


def block_program(nc, x_in, ctxT, w_kv0, w_kv1, wq0, wo0, lnw, wbase, bbase, a0, b0, wr0,
                  wq1, wo1, aw, bw, wr1, keysT, out):
    ctx = ExitStack()
    with ctx:
        def sb(name, shape, dt, stack=ctx):
            return stack.enter_context(nc.sbuf_tensor(name, shape, dt))

        def sem(name):
            return ctx.enter_context(nc.semaphore(name))

        k0s = nc.dram_tensor("k0s", [B, 2, KV0 * HD0, S], F32).ap()
        k1s = nc.dram_tensor("k1s", [B, 2, KV1, P, S1], F32).ap()
        v1s = nc.dram_tensor("v1s", [B, 2, C1, P, KV1 * HD1], F32).ap()

        x = sb("x", [P, TT, D], F32)
        xh = sb("xh", [P, DC, T], F32R)
        xl = sb("xl", [P, DC, T], F32R)
        act = sb("act", [P, DC, T], F32)
        xn = act[:, :, :].rearrange("p (t a) n -> p t (a n)", t=TT)
        graw = sb("graw", [P, 2, D], F32)
        gh = sb("gh", [P, 2, D], F32R)
        gl = sb("gl", [P, 2, D], F32R)
        qraw = sb("qraw", [P, DC, P], F32)
        qwh = sb("qwh", [P, DC, P], F32R)
        qwl = sb("qwl", [P, DC, P], F32R)
        ah = sb("ah", [P, 2, T], F32R)
        al = sb("al", [P, 2, T], F32R)
        sgh, sgl = ah, al
        ident = sb("ident", [P, P], F32)
        lnw_sb = sb("lnw_sb", [P, DC], F32)
        wr0_raw = sb("wr0_raw", [P, DC, E0], F32)
        wr0h = sb("wr0h", [P, DC, E0], F32R)
        wr0l = sb("wr0l", [P, DC, E0], F32R)
        wr1_raw = sb("wr1_raw", [P, DC, RD1], F32)
        wr1h = sb("wr1h", [P, DC, RD1], F32R)
        wr1l = sb("wr1l", [P, DC, RD1], F32R)
        keys_sb = sb("keys_sb", [RD1, E1], F32)
        neghalf = sb("neghalf", [P, TT], F32)
        stats = sb("stats", [P, TT, 12], F32)
        mv = sb("mv", [P, TT, 2], F32)
        ve = sb("ve", [P, TT], F32)
        rstd = sb("rstd", [P, TT], F32)
        ssq = sb("ssq", [P, TT], F32)
        nmax = sb("nmax", [P, 2, TT], F32)
        rs = sb("rs", [P, 2, TT, R0], F32)
        rinv = sb("rinv", [P, 2, TT, R0], F32)
        pv = sb("pv", [P, TT, 14], F32)
        m8 = sb("m8", [P, TT, 8], F32)
        rp = sb("rp", [P, TT, 8], F32)
        mr = sb("mr", [P, TT, 14], F32)
        ex0 = sb("ex0", [P, TT, E0], F32)
        comb = sb("comb", [P, TT, E0], F32)
        t4 = sb("t4", [P, 4, TT], F32)

        with ExitStack() as part:
            v0h = sb("v0h", [P, C0, KV0 * HD0], F32R, part)
            v0l = sb("v0l", [P, C0, KV0 * HD0], F32R, part)
            with ExitStack() as inner:
                ch = sb("ch", [P, DC, S], F32R, inner)
                cl = sb("cl", [P, DC, S], F32R, inner)
                craw = sb("craw", [P, 2, S], F32, inner)
            with ExitStack() as inner:
                VW = 2 * P - HD0
                vph = sb("vph", [P, C0, VW], F32R, inner)
                vpl = sb("vpl", [P, C0, VW], F32R, inner)
                kp = sb("kp", [P, 2, S], F32R, inner)
                qp = sb("qp", [P, R0, T], F32R, inner)
                qh = sb("qh", [P, T], F32R, inner)
                ql = sb("ql", [P, T], F32R, inner)
                e0 = sb("e0", [P, 2 * TT, S], F32, inner)
                ph0 = sb("ph0", [P, 2, T], F32R, inner)
                pl0 = sb("pl0", [P, 2, T], F32R, inner)
                rb0 = sb("rb0", [P, T], F32, inner)
                rwide = sb("rwide", [P, TT, P], F32, inner)
        with ExitStack() as part:
            e1 = sb("e1", [P, 2 * TT, S1], F32, part)
            ph1 = sb("ph1", [P, 2, T], F32R, part)
            pl1 = sb("pl1", [P, 2, T], F32R, part)
            k1h = sb("k1h", [P, S1], F32R, part)
            k1l = sb("k1l", [P, S1], F32R, part)
            v1h = sb("v1h", [P, C1, P], F32R, part)
            v1l = sb("v1l", [P, C1, P], F32R, part)
            q1h = sb("q1h", [P, 2, T], F32R, part)
            q1l = sb("q1l", [P, 2, T], F32R, part)
            rb1 = sb("rb1", [P, T], F32, part)
        with ExitStack() as part:
            bias_sb = sb("bias_sb", [P, D], F32, part)
            gwide0 = sb("gwide0", [P, TT, P], F32, part)
        with ExitStack() as part:
            sc1 = sb("sc1", [P, TT, E1], F32, part)
            sc2 = sb("sc2", [P, TT, E1], F32, part)
            sc3 = sb("sc3", [P, TT, E1], F32, part)
            ex1 = sb("ex1", [P, TT, E1], F32, part)
            m16 = sb("m16", [P, TT, 16], F32, part)
            q16 = sb("q16", [P, TT, RD1], F32, part)
            q16T = sb("q16T", [RD1, T], F32, part)
            gwide1 = sb("gwide1", [P, TT, N1], F32, part)

        ps = ctx.enter_context(nc.psum_tensor("ps", [P, 8, 512], F32))
        TB, PVB, QB = 4, 6, 7
        RB0, RB1 = 7, 3

        const_dma = sem("const_dma")
        const_hi = sem("const_hi")
        const_ready = sem("const_ready")
        bias_landed = sem("bias_landed")
        bias_added = sem("bias_added")
        x_landed = sem("x_landed")
        out_stored = sem("out_stored")
        ctx_landed = [sem(f"ctx_landed{i}") for i in range(2)]
        ctx_hi = sem("ctx_hi")
        ctx_lo = sem("ctx_lo")
        g_landed = [sem(f"g_landed{i}") for i in range(2)]
        g_hi = sem("g_hi")
        g_lo = sem("g_lo")
        g_used = sem("g_used")
        q_landed = sem("q_landed")
        q_hi = sem("q_hi")
        q_lo = sem("q_lo")
        a_hi = sem("a_hi")
        a_lo = sem("a_lo")
        acc_done = sem("acc_done")
        ev_hi = sem("ev_hi")
        acc_evac = sem("acc_evac")
        st_done = [sem(f"st_done{i}") for i in range(2)]
        ln_dve = sem("ln_dve")
        ln_pool = sem("ln_pool")
        xn_ready = sem("xn_ready")
        xt_ready = sem("xt_ready")
        xt_hi = sem("xt_hi")
        xt_lo = sem("xt_lo")
        qt_done = sem("qt_done")
        qt_hi = sem("qt_hi")
        qt_lo = sem("qt_lo")
        q_packed = [sem(f"q_packed{j}") for j in range(R0)]
        k_packed = [sem(f"k_packed{i}") for i in range(2)]
        kv_landed = sem("kv_landed")
        vp_ready = sem("vp_ready")
        s_ready = sem("s_ready")
        mx_done = sem("mx_done")
        e_done = sem("e_done")
        rinv_done = sem("rinv_done")
        rwide_done = sem("rwide_done")
        rb_ready = sem("rb_ready")
        rb_done = sem("rb_done")
        t_ready = sem("t_ready")
        p_hi = sem("p_hi")
        p_lo = sem("p_lo")
        p_used = sem("p_used")
        act_done = sem("act_done")
        ff_pe = sem("ff_pe")
        ff_act = sem("ff_act")
        ff_dve = sem("ff_dve")
        dv = sem("dv")
        sp_steps = sem("sp_steps")
        pool_steps = sem("pool_steps")
        dve_steps = sem("dve_steps")
        pool_c = sem("pool_c")
        dve_c = sem("dve_c")

        block = ctx.enter_context(nc.Block())

        def G(b, w):
            return b * NG + (w + 1 + 2)

        def tile0(b, g, j, t):
            return b * NTILE + g * (R0 * TT) + (j * TT + t)

        def tile1(b, h, j, t):
            return b * NTILE + h * (R1 * TT) + (H0 * TT + j * TT + t)

        def chunk0(b, g, j, c):
            return b * NCHUNK + g * (R0 * C0) + (j * C0 + c)

        def chunk1(b, h, j, c):
            return b * NCHUNK + h * (R1 * C1) + (NCH0 + j * C1 + c)

        def unit0(b, g):
            return b * NU + g

        def unit1(b, h, j):
            return b * NU + h * R1 + (KV0 + j)

        NLN, NFP, NFA, NFD = 5, 6, 4, 8

        def wait_bank(eng, b, phase, k, w_last, ph_extra=0, w_extra=0):
            if k < 7:
                eng.wait_ge(acc_done, b * NDONE + ph_extra + (phase * 7 + k + 1))
            else:
                eng.wait_ge(g_used, G(b, w_last) + w_extra)

        def wait_stored(eng, b, i):
            eng.wait_ge(st_done[i % 2], b * (NST * 16) + (i // 2) * 32)

        @block.sync
        def _(sp):
            def wait(semaphore, value):
                sp.wait_ge(semaphore, value)
                sp.sem_inc(sp_steps, 1)

            sp.dma_start(lnw_sb[:, :], lnw).then_inc(const_dma, 16)
            sp.dma_start(wr0_raw[:, :, :], wr0.rearrange("(c p) e -> p c e", p=P)).then_inc(const_dma, 16)
            sp.dma_start(wr1_raw[:, :, :], wr1.rearrange("(c p) e -> p c e", p=P)).then_inc(const_dma, 16)
            sp.dma_start(keys_sb[:, :], keysT).then_inc(const_dma, 16)

            with sp.Fori(0, B) as b:
                def load_g(w, src, cols=D, extra=0):
                    wait(g_lo, b * NG + extra + (w + 1))
                    sp.dma_start(graw[:, w % 2, 0:cols], src).then_inc(g_landed[w % 2], 16)

                def load_q(u, src):
                    wait(q_lo, u + 1)
                    sp.dma_start(qraw[:, :, :], src).then_inc(q_landed, 16)

                def rows(w, c, lo=0, n=D):
                    return w[c * P:(c + 1) * P, lo:lo + n]

                sp.dma_start(x[:, :, :], x_in[ds(b, 1)].rearrange("a (t p) d -> p (a t) d", p=P)).then_inc(x_landed, 16)

                def wq0_tile(g):
                    return wq0.rearrange("(c p) n -> p c n", p=P)[:, :, ds(g * P, P)]

                def wq1_tile(n):
                    return wq1.rearrange("(c p) n -> p c n", p=P)[:, :, ds(n * P, P)]

                for c in range(DC):
                    if c >= 2:
                        wait(ctx_lo, b * DC + (c - 1))
                    sp.dma_start(craw[:, c % 2, :], ctxT[ds(b, 1), c * P:(c + 1) * P, :].rearrange("a p s -> p (a s)")).then_inc(ctx_landed[c % 2], 16)
                    load_g(G_KV0 + c, rows(w_kv0, c, 0, 512), 512)
                load_q(unit0(b, 0), wq0_tile(0))

                def store(i, acc, dst_h, dst_l):
                    wait(acc_evac, b * NACC + (acc + 2))
                    sp.dma_start(dst_h, sgh[:, i % 2, :].bitcast(F32)).then_inc(st_done[i % 2], 16)
                    sp.dma_start(dst_l, sgl[:, i % 2, :].bitcast(F32)).then_inc(st_done[i % 2], 16)

                def k0_dst(part, i):
                    return k0s[ds(b, 1), part, (i // 2) * P:(i // 2 + 1) * P, (i % 2) * T:(i % 2 + 1) * T].rearrange("a p s -> p (a s)")

                def k1_dst(part, h, s0):
                    return k1s[ds(b, 1), part, h, :, s0:s0 + T].rearrange("a p s -> p (a s)")

                def v1_dst(part, c):
                    return v1s[ds(b, 1), part, c].rearrange("a p n -> p (a n)")

                load_g(G_K1, rows(w_kv1, 0, 0, 512), 512)
                load_g(G_K1 + 1, rows(w_kv1, 1, 0, 512), 512)
                for i in range(4):
                    store(i, A_KV0 + i, k0_dst(0, i), k0_dst(1, i))
                for c in range(2, DC):
                    load_g(G_K1 + c, rows(w_kv1, c, 0, 512), 512)
                load_g(G_V1, rows(w_kv1, 0, 512, 512), 512)
                load_g(G_V1 + 1, rows(w_kv1, 1, 512, 512), 512)
                for i in range(8):
                    store(4 + i, A_K1 + i, k1_dst(0, i // 2, (i % 2) * T), k1_dst(1, i // 2, (i % 2) * T))
                    if i % 4 == 3:
                        load_g(G_V1 + 2 + i // 4, rows(w_kv1, 2 + i // 4, 512, 512), 512)
                for c in range(4, DC):
                    load_g(G_V1 + c, rows(w_kv1, c, 512, 512), 512)
                for i in range(8):
                    store(12 + i, A_V1 + i, v1_dst(0, i), v1_dst(1, i))

                def pack_k(g, par):
                    for r in range(4):
                        sp.dma_start(kp[r * HD0:(r + 1) * HD0, par, :].bitcast(F32),
                                     k0s[ds(b, 1), r // 2, ds(g * HD0, HD0), :].rearrange("a p s -> p (a s)")).then_inc(k_packed[par], 16)

                def pack_q(j):
                    for r in range(4):
                        sp.dma_start(qp[r * HD0:(r + 1) * HD0, j, :].bitcast(F32),
                                     (qh, ql)[r % 2][j * HD0:(j + 1) * HD0, :].bitcast(F32)).then_inc(q_packed[j], 16)

                load_g(G_WO0, rows(wo0, 0))
                load_g(G_WO0 + 1, rows(wo0, 1))
                load_q(unit0(b, 1), wq0_tile(1))
                wait(st_done[0], b * (NST * 16) + 32 * 10)
                wait(st_done[1], b * (NST * 16) + 32 * 10)
                wait(qt_lo, unit0(b, 0) + 2)
                pack_k(0, 0)
                for j in range(R0):
                    pack_q(j)

                def group0(g, par, more, more2):
                    if more2:
                        load_q(unit0(b, g) + 2, wq0_tile(g + 2))
                    if more:
                        wait(s_ready, tile0(b, g, 0, TT - 1) + 1)
                        pack_k(g + 1, 1 - par)
                        wait(qt_lo, unit0(b, g) + 3)
                        for j in range(R0):
                            wait(s_ready, tile0(b, g, j, TT - 1) + 1)
                            pack_q(j)

                with sp.Fori(0, KV0 // 2 - 1) as r:
                    group0(r * 2, 0, True, True)
                    group0(r * 2 + 1, 1, True, True)
                group0(KV0 - 2, 0, True, False)
                for c in range(2, DC):
                    load_g(G_WO0 + c, rows(wo0, c))

                wait(act_done, unit0(b, KV0 - 1) + 2)
                sp.dma_start(bias_sb[:, :], bbase.rearrange("(a d) -> a d", a=1).to_broadcast([P, D])).then_inc(bias_landed, 16)
                load_g(G_A0, a0.rearrange("(c p) n -> p c n", p=P))
                for c in range(DC):
                    load_g(G_BASE + c, rows(wbase, c))
                load_g(G_B0, b0)
                load_g(G_KV1, rows(w_kv1, 0))
                load_g(G_KV1 + 1, rows(w_kv1, 1))
                for c in range(2, DC):
                    load_g(G_KV1 + c, rows(w_kv1, c))
                for i in range(8):
                    if i < 4:
                        store(20 + i, A_KV1 + i, k1_dst(0, i, S), k1_dst(1, i, S))
                    else:
                        store(20 + i, A_KV1 + i, v1_dst(0, C0 + i - 4), v1_dst(1, C0 + i - 4))
                wait(st_done[0], b * (NST * 16) + NST * 16)
                wait(st_done[1], b * (NST * 16) + NST * 16)

                def load_k1(h):
                    sp.dma_start(k1h[:, :].bitcast(F32), k1s[ds(b, 1), 0, ds(h, 1)].rearrange("a h p s -> p (a h s)")).then_inc(kv_landed, 16)
                    sp.dma_start(k1l[:, :].bitcast(F32), k1s[ds(b, 1), 1, ds(h, 1)].rearrange("a h p s -> p (a h s)")).then_inc(kv_landed, 16)

                def load_v1(h):
                    for part, dst in ((0, v1h), (1, v1l)):
                        sp.dma_start(dst[:, :, :].bitcast(F32), v1s[ds(b, 1), part, :, :, ds(h * HD1, HD1)].rearrange("a c p n -> p (a c) n")).then_inc(kv_landed, 16)

                with sp.Fori(0, KV1) as h:
                    load_q(unit1(b, h, 0), wq1_tile(h * R1))
                    wait(s_ready, tile1(b, h, 0, 0))
                    load_k1(h)
                    wait(p_used, chunk1(b, h, 0, 0) + 2)
                    load_v1(h)
                    for j in range(1, R1):
                        load_q(unit1(b, h, j), wq1_tile(h * R1 + j))
                    for c in range(DC):
                        load_g(G_WO1 + c, wo1[ds(h * (R1 * HD1) + c * P, P), :], extra=h * DC)
                for c in range(DC):
                    load_g(G_Z + c, rows(aw, c, 0, N1), N1)
                for c in range(ZB):
                    load_g(G_BW + c, rows(bw, c))
                wait(acc_evac, b * NACC + (NACC + 1))
                sp.dma_start(out[ds(b, 1)].rearrange("a (t p) d -> p (a t) d", p=P), x[:, :, :]).then_inc(out_stored, 16)
                wait(out_stored, b * 16 + 16)

        @block.tensor
        def _(pe):
            def mm3(o, wh, wl, mh, ml, start, stop, check=True):
                pe.matmul(o, wh, mh, start=start, stop=False, skip_group_check=not check)
                pe.matmul(o, wh, ml, start=False, stop=False, skip_group_check=not check)
                return pe.matmul(o, wl, mh, start=False, stop=stop, skip_group_check=not check)

            pe.sem_inc(g_used, 2)
            pe.sem_inc(p_used, 2)
            pe.sem_inc(qt_done, 1)
            pe.wait_ge(const_ready, 3)

            with pe.Fori(0, B) as b:
                def wait_acc(n):
                    pe.wait_ge(acc_evac, b * NACC + (n + 1))

                def gemm(w0, extra, acc, chunks, before=None):
                    n = len(chunks)
                    for c in range(n):
                        s = (w0 + c) % 2
                        for wait in chunks[c][0]:
                            wait()
                        pe.wait_ge(g_lo, G(b, w0 + c) + extra)
                        first, last = c == 0, c == n - 1
                        for k in range(8):
                            if first and before is not None:
                                before(k)
                            for o, wh, wl, mh, ml, opens, check in chunks[c][1](c, s, k):
                                mm = mm3(o, wh, wl, mh, ml, first and opens, last, check)
                            if k == 7:
                                mm.then_inc(g_used, 1)
                            elif last:
                                mm.then_inc(acc_done, 1)

                def evacuated(n, extra=0):
                    def wait(k):
                        pe.wait_ge(acc_evac, b * NACC + extra + (n + k + 2))
                    return wait

                def kv0_bank(c, s, k):
                    if k < 4:
                        w = slice((k // 2) * P, (k // 2 + 1) * P)
                        m = slice((k % 2) * T, (k % 2 + 1) * T)
                        return [(ps[:, k, :], gh[:, s, w], gl[:, s, w], ch[:, c, m], cl[:, c, m], True, True)]
                    return [(ps[:, k, i * 256:(i + 1) * 256],
                             ch[:, c, (2 * k - 8 + i) * P:(2 * k - 7 + i) * P], cl[:, c, (2 * k - 8 + i) * P:(2 * k - 7 + i) * P],
                             gh[:, s, 256:512], gl[:, s, 256:512], i == 0, False) for i in range(2)]

                def ctx_chunk(c):
                    return [lambda: pe.wait_ge(ctx_lo, b * DC + (c + 1))]

                wait_acc(0)
                gemm(G_KV0, 0, A_KV0, [(ctx_chunk(c), kv0_bank) for c in range(DC)])

                def k1_bank(c, s, k):
                    w = slice((k // 2) * P, (k // 2 + 1) * P)
                    m = slice((k % 2) * T, (k % 2 + 1) * T)
                    return [(ps[:, k, :], gh[:, s, w], gl[:, s, w], ch[:, c, m], cl[:, c, m], True, True)]

                gemm(G_K1, 0, A_K1, [([], k1_bank)] * DC, evacuated(A_KV0))

                def v1_bank(c, s, k):
                    w = slice(k * P, (k + 1) * P)
                    return [(ps[:, k, :], ch[:, c, w], cl[:, c, w], gh[:, s, 0:512], gl[:, s, 0:512], True, True)]

                gemm(G_V1, 0, A_V1, [([], v1_bank)] * DC, evacuated(A_K1))

                def transpose_x(p, before=None):
                    for t in range(TT):
                        pe.wait_ge(xn_ready, b * (4 * TT) + (p * TT + t + 1))
                        for c in range(DC):
                            if t == 0 and before is not None:
                                before(c)
                            tr = pe.transpose(ps[:, c, t * P:(t + 1) * P], xn[:, t, c * P:(c + 1) * P], ident[:, :])
                            if t == TT - 1:
                                tr.then_inc(xt_ready, 1)

                def wait_xt(p):
                    pe.wait_ge(xt_lo, b * (4 * DC) + (p + 1) * DC)

                transpose_x(0, evacuated(A_V1))
                wait_xt(0)

                def q_project(u, cs):
                    if cs[0] == 0:
                        pe.wait_ge(q_lo, u + 2)
                        pe.wait_ge(qt_lo, u + 1)
                    for c in cs:
                        mm = mm3(ps[:, QB, :], qwh[:, c, :], qwl[:, c, :], xh[:, c, :], xl[:, c, :], c == 0, c == DC - 1)
                    if cs[-1] == DC - 1:
                        mm.then_inc(qt_done, 1)

                def scores0(g, par, j, t):
                    a = tile0(b, g, j, t)
                    pe.wait_ge(e_done, a + 1)
                    for half in range(2):
                        mm = pe.matmul(ps[:, 2 * (t % 2) + half, :], qp[:, j, t * P:(t + 1) * P],
                                       kp[:, par, half * 512:(half + 1) * 512], start=True, stop=True)
                    mm.then_inc(s_ready, 1)

                def packed(n, j, par, m):
                    pe.wait_ge(q_packed[j], n * 64 + 64)
                    if j == 0:
                        pe.wait_ge(k_packed[par], m * 64 + 64)

                def transpose_p(n, e, c, exps):
                    if c == 0:
                        pe.wait_ge(e_done, exps)
                    pe.wait_ge(p_lo, n + 1)
                    for t in range(TT):
                        tr = pe.transpose(ps[:, TB + c % 2, t * P:(t + 1) * P], e[:, t, c * P:(c + 1) * P], ident[:, :])
                    tr.then_inc(t_ready, 1)

                def pv0(g, j, c):
                    n = chunk0(b, g, j, c)
                    first, last = j == 0 and c == 0, j == R0 - 1 and c == C0 - 1
                    if first:
                        pe.wait_ge(vp_ready, b * KV0 + g + 1)
                        pe.wait_ge(act_done, unit0(b, g) + 1)
                    pe.wait_ge(p_lo, n + 3)
                    w = slice(P - HD0 - j * HD0, 2 * P - HD0 - j * HD0)
                    mm3(ps[:, PVB, :], vph[:, c, w], vpl[:, c, w], ph0[:, c % 2, :], pl0[:, c % 2, :],
                        first, last).then_inc(p_used, 1)

                def broadcast_rinv(bank, src, ready, count, u):
                    pe.wait_ge(ready, count)
                    pe.wait_ge(rb_done, u + 1)
                    for t in range(TT):
                        tr = pe.transpose(ps[:, bank, t * P:(t + 1) * P], src(t), ident[:, :])
                    tr.then_inc(rb_ready, 1)

                def group0(g, par, more, m):
                    pending = None
                    if more:
                        pe.wait_ge(rb_done, unit0(b, g) + 1)
                    for j in range(R0):
                        for t in range(TT):
                            if j < R0 - 1:
                                if t == 0:
                                    packed(b * KV0 + g, j + 1, par, m)
                                scores0(g, par, j + 1, t)
                            elif more:
                                if t == 0:
                                    packed(b * KV0 + g + 1, 0, 1 - par, m + par)
                                scores0(g + 1, 1 - par, 0, t)
                            for c in (2 * t, 2 * t + 1):
                                n = chunk0(b, g, j, c)
                                transpose_p(n, e0[:, (j % 2) * TT:(j % 2) * TT + TT, :], c, tile0(b, g, j, TT - 1) + 3)
                                if pending is not None:
                                    pv0(g, *pending)
                                pending = (j, c)
                                if j == 0 and more:
                                    q_project(unit0(b, g) + 1, [c])
                            if j == R0 - 1 and t == 1:
                                if more:
                                    pe.wait_ge(qt_lo, unit0(b, g) + 3)
                                broadcast_rinv(RB0, lambda i: rwide[:, i, :], rwide_done, b * KV0 + g + 1, unit0(b, g))
                    pv0(g, *pending)

                q_project(unit0(b, 0), list(range(DC)))
                packed(b * KV0, 0, 0, b * (KV0 // 2))
                for t in range(TT):
                    scores0(0, 0, 0, t)
                with pe.Fori(0, KV0 // 2 - 1) as r:
                    group0(r * 2, 0, True, b * (KV0 // 2) + r)
                    group0(r * 2 + 1, 1, True, b * (KV0 // 2) + r)
                group0(KV0 - 2, 0, True, b * (KV0 // 2) + KV0 // 2 - 1)
                group0(KV0 - 1, 1, False, b * (KV0 // 2) + KV0 // 2 - 1)

                def out_bank(sh, sl):
                    def bank(c, s, k):
                        w = slice((k // 2) * P, (k // 2 + 1) * P)
                        m = slice((k % 2) * 512, (k % 2 + 1) * 512)
                        return [(ps[:, k, :], sh(c)[:, w], sl(c)[:, w], gh[:, s, m], gl[:, s, m], True, True)]
                    return bank

                def split_act(i, extra=0):
                    return [lambda: pe.wait_ge(a_lo, b * NA + extra + (i + 1))]

                ring_bank = out_bank(lambda c: ah[:, c % 2, :], lambda c: al[:, c % 2, :])
                pe.wait_ge(act_done, unit0(b, KV0 - 1) + 2)
                gemm(G_WO0, 0, A_WO0, [(split_act(X_WO0 + c), ring_bank) for c in range(DC)])

                transpose_x(1)
                wait_xt(1)

                pe.wait_ge(g_lo, G(b, G_A0))
                wa = lambda w, c: w[:, G_A0 % 2, c * P:(c + 1) * P]
                for c in range(DC):
                    mm = mm3(ps[:, 0, :], wa(gh, c), wa(gl, c), xh[:, c, :], xl[:, c, :], c == 0, c == DC - 1)
                mm.then_inc(g_used, 1)

                def router(bank, wh, wl, n):
                    for t in range(TT):
                        w = slice(t * P, (t + 1) * P)
                        for c in range(DC):
                            mm = mm3(ps[:, bank, t * n:(t + 1) * n], xh[:, c, w], xl[:, c, w], wh[:, c, :], wl[:, c, :],
                                     c == 0, c == DC - 1)
                    mm.then_inc(ff_pe, 1)

                router(1, wr0h, wr0l, E0)
                pe.wait_ge(ff_dve, b * 8 + 2)
                for t in range(TT):
                    tr = pe.transpose(ps[:, 2, t * P:(t + 1) * P], gwide0[:, t, :], ident[:, :])
                tr.then_inc(ff_pe, 1)
                pe.wait_ge(ff_dve, b * 8 + 3)
                x_bank = out_bank(lambda c: xh[:, c, :], lambda c: xl[:, c, :])
                low_bank = out_bank(lambda c: ah[:, 0, :], lambda c: al[:, 0, :])
                gemm(G_BASE, 0, A_BASE, [([], x_bank)] * DC + [(split_act(X_B0), low_bank)])

                transpose_x(2)
                wait_xt(2)

                def kv1_bank(c, s, k):
                    if k < 4:
                        w = slice(k * P, (k + 1) * P)
                        return [(ps[:, k, :], gh[:, s, w], gl[:, s, w], xh[:, c, :], xl[:, c, :], True, True)]
                    w = slice((k - 4) * P, (k - 3) * P)
                    return [(ps[:, k, :], xh[:, c, w], xl[:, c, w], gh[:, s, 512:], gl[:, s, 512:], True, True)]

                gemm(G_KV1, 0, A_KV1, [([], kv1_bank)] * DC)

                with pe.Fori(0, KV1) as h:
                    def scores1(j, t):
                        a = tile1(b, h, j, t)
                        pe.wait_ge(e_done, a + 2)
                        if t == 0:
                            pe.wait_ge(qt_lo, unit1(b, h, j) + 2)
                        w = slice(t * P, (t + 1) * P)
                        for k in range(3):
                            m = slice(k * 512, (k + 1) * 512)
                            mm = mm3(ps[:, k, :], q1h[:, j % 2, w], q1l[:, j % 2, w], k1h[:, m], k1l[:, m], True, True)
                        mm.then_inc(s_ready, 1)

                    def pv1(j, c):
                        if c == 0:
                            pe.wait_ge(act_done, unit1(b, h, j) + 1)
                        pe.wait_ge(p_lo, chunk1(b, h, j, c) + 3)
                        mm3(ps[:, PVB, :], v1h[:, c, :], v1l[:, c, :], ph1[:, c % 2, :], pl1[:, c % 2, :],
                            c == 0, c == C1 - 1).then_inc(p_used, 1)

                    pe.wait_ge(acc_evac, b * NACC + h * 8 + (A_WO1 + 1))
                    q_project(unit1(b, h, 0), list(range(DC)))
                    pe.wait_ge(kv_landed, b * (KV1 * 64) + h * 64 + 64)
                    for t in range(TT):
                        scores1(0, t)
                        q_project(unit1(b, h, 1), [2 * t, 2 * t + 1])
                    pending = None
                    for j in range(R1):
                        for t in range(TT):
                            if j < R1 - 1:
                                scores1(j + 1, t)
                            for i in range(3):
                                c = 3 * t + i
                                transpose_p(chunk1(b, h, j, c), e1[:, (j % 2) * TT:(j % 2) * TT + TT, :], c, tile1(b, h, j, TT - 1) + 3)
                                if c < DC and j < R1 - 2:
                                    q_project(unit1(b, h, j + 2), [c])
                                if pending is not None:
                                    pv1(*pending)
                                pending = (j, c)
                            if t == 2:
                                broadcast_rinv(RB1, lambda i: rinv[:, j % 2, i, 0:1].to_broadcast([P, P]), rinv_done, unit1(b, h, j) + 1, unit1(b, h, j))
                    pv1(*pending)
                    pe.wait_ge(act_done, unit1(b, h, R1 - 1) + 2)
                    gemm(G_WO1, h * DC, A_WO1, [(split_act(X_WO1 + c, h * R1), ring_bank) for c in range(R1)])

                transpose_x(3)
                wait_xt(3)
                for c in range(DC):
                    s = (G_Z + c) % 2
                    pe.wait_ge(g_lo, G(b, G_Z + c))
                    for k in range(ZB):
                        w = slice(k * P, (k + 1) * P)
                        mm = mm3(ps[:, k, :], gh[:, s, w], gl[:, s, w], xh[:, c, :], xl[:, c, :], c == 0, c == DC - 1)
                    mm.then_inc(g_used, 1)
                router(4, wr1h, wr1l, RD1)
                pe.wait_ge(ff_dve, b * 8 + 4)
                for t in range(TT):
                    tr = pe.transpose(ps[0:RD1, 5, t * P:(t + 1) * P], q16[:, t, :], ident[:, :])
                tr.then_inc(ff_pe, 1)
                pe.wait_ge(ff_dve, b * 8 + 5)
                for t in range(TT):
                    mm = pe.matmul(ps[:, 6, t * E1:(t + 1) * E1], q16T[:, t * P:(t + 1) * P], keys_sb[:, :], start=True, stop=True)
                mm.then_inc(ff_pe, 1)
                pe.wait_ge(ff_act, b * 4 + 3)
                pe.wait_ge(ff_dve, b * 8 + 7)
                for k in range(ZB):
                    for t in range(TT):
                        tr = pe.transpose(ps[:, k, t * P:(t + 1) * P], gwide1[:, t, k * P:(k + 1) * P], ident[:, :])
                tr.then_inc(ff_pe, 1)
                pe.wait_ge(ff_dve, b * 8 + 8)
                gemm(G_BW, 0, A_BW, [(split_act(X_BW + c), ring_bank) for c in range(ZB)])

        @block.scalar
        def _(sc):
            def hi(o, i, scale=1.0):
                return sc.activation(o, i, ACT.Copy, scale=scale)

            sc.sem_inc(e_done, 2)
            sc.sem_inc(rb_done, 1)
            sc.wait_ge(const_dma, 16 * 4)
            hi(wr0h[:, :, :], wr0_raw[:, :, :]).then_inc(const_hi, 1)
            hi(wr1h[:, :, :], wr1_raw[:, :, :]).then_inc(const_hi, 1)

            with sc.Fori(0, B) as b:
                def g_split(w, extra=0, slots=0):
                    sc.wait_ge(g_landed[w % 2], b * (NG * 8) + slots + (w // 2 + 1) * 16)
                    sc.wait_ge(g_used, G(b, w - 2) + extra)
                    n = cols_of(w)
                    hi(gh[:, w % 2, 0:n], graw[:, w % 2, 0:n]).then_inc(g_hi, 1)

                def q_split(u):
                    sc.wait_ge(q_landed, u * 16 + 16)
                    sc.wait_ge(qt_done, u + 1)
                    hi(qwh[:, :, :], qraw[:, :, :]).then_inc(q_hi, 1)

                def a_split(c, w, extra=0):
                    sc.wait_ge(g_used, G(b, w - 2) + extra)
                    hi(ah[:, c % 2, :], act[:, c, :]).then_inc(a_hi, 1)

                def evac(k, o, phase, w_last):
                    wait_bank(sc, b, phase, k, w_last)
                    hi(o, ps[:, k, :]).then_inc(ev_hi, 1)

                def xt_split(p):
                    for c in range(DC):
                        sc.wait_ge(xt_ready, b * (4 * DC) + (p * DC + c + 1))
                        hi(xh[:, c, :], ps[:, c, :], lnw_sb[:, c:c + 1] if p == 0 else 1.0).then_inc(xt_hi, 1)

                for c in range(DC):
                    sc.wait_ge(ctx_landed[c % 2], b * (DC * 8) + (c // 2 + 1) * 16)
                    hi(ch[:, c, :], craw[:, c % 2, :]).then_inc(ctx_hi, 1)
                    g_split(G_KV0 + c)
                g_split(G_K1)
                for k in range(8):
                    if k in (2, 3):
                        wait_stored(sc, b, k)
                    evac(k, sgh[:, k % 2, :] if k < 4 else v0h[:, 2 * k - 8:2 * k - 6, :].rearrange("p a n -> p (a n)"), 0, G_K1 - 1)
                    if k == 3:
                        g_split(G_K1 + 1)
                for c in range(2, DC):
                    g_split(G_K1 + c)
                g_split(G_V1)
                for k in range(8):
                    wait_stored(sc, b, 4 + k)
                    evac(k, sgh[:, k % 2, :], 1, G_V1 - 1)
                    if k == 3:
                        g_split(G_V1 + 1)
                for c in range(2, DC):
                    g_split(G_V1 + c)
                q_split(unit0(b, 0))
                for k in range(8):
                    wait_stored(sc, b, 12 + k)
                    evac(k, sgh[:, k % 2, :], 2, G_WO0 - 1)
                xt_split(0)
                g_split(G_WO0)
                g_split(G_WO0 + 1)

                sc.wait_ge(st_done[0], b * (NST * 16) + 32 * 10)
                sc.wait_ge(st_done[1], b * (NST * 16) + 32 * 10)

                def q_evac(u, o, scale):
                    sc.wait_ge(qt_done, u + 2)
                    hi(o, ps[:, QB, :], scale).then_inc(qt_hi, 1)

                def exp0(g, par, j, t):
                    a = tile0(b, g, j, t)
                    sc.wait_ge(mx_done, a + 1)
                    sc.activation(e0[:, (j % 2) * TT + t, :], ps[:, 2 * (t % 2):2 * (t % 2) + 2, :].rearrange("p a n -> p (a n)"),
                                  ACT.Exp, bias=nmax[:, j % 2, t:t + 1], accum_out=rs[:, par, t, j:j + 1]).then_inc(e_done, 1)

                def p_split(n, c, o):
                    sc.wait_ge(t_ready, n + 1)
                    sc.wait_ge(p_used, n + 1)
                    hi(o[:, c % 2, :], ps[:, TB + c % 2, :]).then_inc(p_hi, 1)

                def copy_rb(u, o, bank):
                    sc.wait_ge(rb_ready, u + 1)
                    sc.wait_ge(act_done, u + 1)
                    sc.copy(o, ps[:, bank, :]).then_inc(rb_done, 1)

                def group0(g, par, more, more2):
                    for j in range(R0):
                        for t in range(TT):
                            if j == R0 - 1 and t == 2:
                                copy_rb(unit0(b, g), rb0[:, :], RB0)
                            p_split(chunk0(b, g, j, 2 * t), 2 * t, ph0)
                            if j < R0 - 1:
                                exp0(g, par, j + 1, t)
                            elif more:
                                exp0(g + 1, 1 - par, 0, t)
                            p_split(chunk0(b, g, j, 2 * t + 1), 2 * t + 1, ph0)
                            if j == 1 and t == 0 and more:
                                for i in range(R0):
                                    sc.wait_ge(q_packed[i], (b * KV0 + g) * 64 + 64)
                                q_evac(unit0(b, g) + 1, qh[:, :], SCALE0)
                            if j == 2 and t == 0 and more2:
                                q_split(unit0(b, g) + 2)

                q_evac(unit0(b, 0), qh[:, :], SCALE0)
                q_split(unit0(b, 1))
                for t in range(TT):
                    exp0(0, 0, 0, t)
                with sc.Fori(0, KV0 // 2 - 1) as r:
                    group0(r * 2, 0, True, True)
                    group0(r * 2 + 1, 1, True, True)
                group0(KV0 - 2, 0, True, False)
                group0(KV0 - 1, 1, False, False)

                for c in range(DC):
                    if c >= 2:
                        g_split(G_WO0 + c)
                    sc.wait_ge(act_done, unit0(b, c) + 2)
                    a_split(c, G_WO0 + c)
                g_split(G_A0)

                g_split(G_BASE)
                xt_split(1)
                sc.wait_ge(g_used, G(b, G_A0))
                sc.copy(act[:, 1, :], ps[:, 0, :]).then_inc(ff_act, 1)
                sc.wait_ge(ff_dve, b * NFD + 1)
                sc.activation(ex0[:, :, :], comb[:, :, :], ACT.Exp).then_inc(ff_act, 1)
                for c in range(1, DC):
                    g_split(G_BASE + c)
                g_split(G_B0)
                sc.wait_ge(ff_dve, b * NFD + 3)
                a_split(0, G_B0)

                g_split(G_KV1)
                g_split(G_KV1 + 1)
                xt_split(2)
                for c in range(2, DC):
                    g_split(G_KV1 + c)
                for k in range(8):
                    wait_stored(sc, b, 20 + k)
                    evac(k, sgh[:, k % 2, :], 5, G_WO1 - 1)
                sc.wait_ge(st_done[0], b * (NST * 16) + NST * 16)
                sc.wait_ge(st_done[1], b * (NST * 16) + NST * 16)

                with sc.Fori(0, KV1) as h:
                    def exp1(j, t):
                        sc.wait_ge(mx_done, tile1(b, h, j, t) + 1)
                        sc.activation(e1[:, (j % 2) * TT + t, :], ps[:, 0:3, :].rearrange("p a n -> p (a n)"),
                                      ACT.Exp, bias=nmax[:, j % 2, t:t + 1], accum_out=rs[:, j % 2, t, 0:1]).then_inc(e_done, 1)

                    q_split(unit1(b, h, 0))
                    q_evac(unit1(b, h, 0), q1h[:, 0, :], SCALE1)
                    q_split(unit1(b, h, 1))
                    for t in range(TT):
                        exp1(0, t)
                    q_evac(unit1(b, h, 1), q1h[:, 1, :], SCALE1)
                    q_split(unit1(b, h, 2))
                    for j in range(R1):
                        for t in range(TT):
                            if t == TT - 1:
                                copy_rb(unit1(b, h, j), rb1[:, :], RB1)
                            p_split(chunk1(b, h, j, 3 * t), 3 * t, ph1)
                            if j < R1 - 1:
                                exp1(j + 1, t)
                            for i in (1, 2):
                                p_split(chunk1(b, h, j, 3 * t + i), 3 * t + i, ph1)
                            if t == 2 and j < R1 - 2:
                                q_evac(unit1(b, h, j + 2), q1h[:, j % 2, :], SCALE1)
                            if t == 3 and j < R1 - 3:
                                q_split(unit1(b, h, j + 3))
                            if j == R1 - 1 and t < 2:
                                g_split(G_WO1 + t, h * DC, h * (DC * 8))
                    for c in range(R1):
                        if c >= 2:
                            g_split(G_WO1 + c, h * DC, h * (DC * 8))
                        sc.wait_ge(act_done, unit1(b, h, c) + 2)
                        a_split(c, G_WO1 + c, h * DC)

                g_split(G_Z)
                g_split(G_Z + 1)
                xt_split(3)
                for c in range(2, DC):
                    g_split(G_Z + c)
                g_split(G_BW)
                sc.wait_ge(g_used, G(b, G_BW - 1))
                for k in range(ZB):
                    cp = sc.copy(act[:, ZB + k, :], ps[:, k, :])
                cp.then_inc(ff_act, 1)
                g_split(G_BW + 1)
                sc.wait_ge(ff_dve, b * NFD + 6)
                sc.activation(ex1[:, :, :], sc3[:, :, :], ACT.Exp).then_inc(ff_act, 1)
                sc.wait_ge(ff_dve, b * NFD + 8)
                for c in range(ZB):
                    if c >= 2:
                        g_split(G_BW + c)
                    a_split(c, G_BW + c)

        @block.gpsimd
        def _(po):
            po.sem_inc(g_lo, 2)
            po.sem_inc(q_lo, 1)
            po.memset(neghalf[:, :], -0.5).then_inc(pool_c, 1)
            po.memset(ident[:, :], 0.0).then_inc(pool_c, 1)
            po.wait_ge(pool_c, 2)
            po.affine_select(out=ident[:, :], in_=ident[:, :], compare_op=ALU.not_equal, fill=1.0, base=0,
                             pattern=[[-1, P]], channel_multiplier=1).then_inc(const_ready, 1)

            with po.Fori(0, B) as b:
                def lo(o, i, h):
                    return po.tensor_tensor(o, i, h.bitcast(F32), ALU.subtract)

                def g_split(w, extra=0):
                    po.wait_ge(g_hi, b * NG + extra + (w + 1))
                    n = cols_of(w)
                    s = w % 2
                    lo(gl[:, s, 0:n], graw[:, s, 0:n], gh[:, s, 0:n]).then_inc(g_lo, 1)

                def q_split(u):
                    po.wait_ge(q_hi, u + 1)
                    lo(qwl[:, :, :], qraw[:, :, :], qwh[:, :, :]).then_inc(q_lo, 1)

                def inv_root(i):
                    po.wait_ge(ln_dve, b * NLN + (i + 1))
                    po.tensor_tensor(rstd[:, :], ve[:, :], neghalf[:, :], ALU.pow).then_inc(ln_pool, 1)

                for c in range(DC):
                    po.wait_ge(ctx_hi, b * DC + (c + 1))
                    lo(cl[:, c, :], craw[:, c % 2, :], ch[:, c, :]).then_inc(ctx_lo, 1)
                    g_split(G_KV0 + c)
                    if c in (3, 5):
                        inv_root((c - 3) // 2)
                for w in range(G_K1, G_WO0):
                    g_split(w)
                q_split(unit0(b, 0))
                g_split(G_WO0)
                g_split(G_WO0 + 1)
                q_split(unit0(b, 1))

                def widen(g, par):
                    po.wait_ge(rinv_done, unit0(b, g) + 1)
                    po.wait_ge(rb_done, unit0(b, g) + 1)
                    po.sem_inc(pool_steps, 1)
                    po.tensor_copy(rwide[:, :, :].rearrange("p t (j d) -> p (t j) d", d=HD0),
                                   rinv[:, par].rearrange("p t j -> p (t j)").unsqueeze(2).to_broadcast([P, TT * R0, HD0])).then_inc(rwide_done, 1)

                with po.Fori(0, KV0 // 2 - 1) as r:
                    for par in range(2):
                        q_split(unit0(b, r * 2 + par) + 2)
                        widen(r * 2 + par, par)
                widen(KV0 - 2, 0)
                widen(KV0 - 1, 1)
                for c in range(2, DC):
                    g_split(G_WO0 + c)
                g_split(G_A0)
                inv_root(2)
                po.wait_ge(xn_ready, b * (4 * TT) + 2 * TT)
                po.wait_ge(bias_landed, b * 16 + 16)
                for t in range(TT):
                    add = po.tensor_tensor(x[:, t, :], x[:, t, :], bias_sb[:, :], ALU.add)
                add.then_inc(bias_added, 1)
                for c in range(DC):
                    g_split(G_BASE + c)
                g_split(G_B0)
                g_split(G_KV1)
                g_split(G_KV1 + 1)
                inv_root(3)
                for c in range(2, DC):
                    g_split(G_KV1 + c)
                with po.Fori(0, KV1) as h:
                    for j in range(R1):
                        q_split(unit1(b, h, j))
                    for c in range(R1):
                        g_split(G_WO1 + c, h * DC)
                g_split(G_Z)
                g_split(G_Z + 1)
                inv_root(4)
                for w in range(G_Z + 2, NG):
                    g_split(w)

        @block.vector
        def _(v):
            v.sem_inc(p_lo, 2)
            v.sem_inc(acc_evac, 1)
            v.sem_inc(act_done, 1)
            v.sem_inc(qt_lo, 1)
            for i in range(8 - TOP0):
                v.memset(pv[:, :, E0 + i:E0 + i + 1], -1.0 - i)
                pad = v.memset(rp[:, :, TOP0 + i:TOP0 + i + 1], -1.0 - i)
            pad.then_inc(dve_c, 1)
            v.wait_ge(dve_c, 1)
            v.wait_ge(const_hi, 2)
            v.tensor_tensor(wr0l[:, :, :], wr0_raw[:, :, :], wr0h[:, :, :].bitcast(F32), ALU.subtract).then_inc(const_ready, 1)
            v.tensor_tensor(wr1l[:, :, :], wr1_raw[:, :, :], wr1h[:, :, :].bitcast(F32), ALU.subtract).then_inc(const_ready, 1)

            with v.Fori(0, B) as b:
                links = [0]

                def link(ins):
                    links[0] += 1
                    ins.then_inc(dv, 1)
                    v.wait_ge(dv, b * NDV + links[0])
                    v.sem_inc(dve_steps, 1)

                def lo(o, i, h):
                    return v.tensor_tensor(o, i, h.bitcast(F32), ALU.subtract)

                def scaled_lo(o, i, scale, h):
                    return v.scalar_tensor_tensor(out=o, in0=i, scalar=scale, in1=h.bitcast(F32), op0=ALU.mult, op1=ALU.subtract)

                def row_stats(src):
                    for t in range(TT):
                        for i in range(2):
                            st = v.bn_stats(stats[:, t, 6 * i:6 * i + 6], src[:, t, 512 * i:512 * i + 512])
                    link(st)
                    for t in range(TT):
                        ag = v.bn_aggr(mv[:, t, :], stats[:, t, :])
                    link(ag)

                def norm(p):
                    row_stats(x)
                    v.tensor_scalar(ve[:, :], mv[:, :, 1], EPS, None, ALU.add).then_inc(ln_dve, 1)
                    v.wait_ge(ln_pool, b * NLN + (1 if p == 0 else p + 2))
                    for t in range(TT):
                        nm = v.tensor_scalar(xn[:, t, :], x[:, t, :], mv[:, t, 0:1], rstd[:, t:t + 1], ALU.subtract, ALU.mult)
                        if p > 0:
                            nm.then_inc(xn_ready, 1)
                    if p > 0:
                        return
                    link(nm)
                    row_stats(xn)
                    link(v.tensor_tensor(ve[:, :], mv[:, :, 0], mv[:, :, 0], ALU.mult))
                    link(v.tensor_tensor(ve[:, :], ve[:, :], mv[:, :, 1], ALU.add))
                    v.tensor_scalar(ve[:, :], ve[:, :], EPS, None, ALU.add).then_inc(ln_dve, 1)
                    v.wait_ge(ln_pool, b * NLN + 2)
                    for t in range(TT):
                        v.tensor_scalar(xn[:, t, :], xn[:, t, :], rstd[:, t:t + 1], None, ALU.mult).then_inc(xn_ready, 1)

                def xt_split(p):
                    for c in range(DC):
                        v.wait_ge(xt_hi, b * (4 * DC) + (p * DC + c + 1))
                        if p == 0:
                            ins = scaled_lo(xl[:, c, :], ps[:, c, :], lnw_sb[:, c:c + 1], xh[:, c, :])
                        else:
                            ins = lo(xl[:, c, :], ps[:, c, :], xh[:, c, :])
                        ins.then_inc(xt_lo, 1)

                def evac(k, i, o, h):
                    v.wait_ge(ev_hi, b * NEV + (i + 1))
                    lo(o, ps[:, k, :], h).then_inc(acc_evac, 1)

                def add_banks(phase, w_last, ph_extra=0, w_extra=0):
                    for k in range(8):
                        wait_bank(v, b, phase, k, w_last, ph_extra, w_extra)
                        xs = x[:, k // 2, (k % 2) * 512:(k % 2 + 1) * 512]
                        v.tensor_tensor(xs, ps[:, k, :], xs, ALU.add).then_inc(acc_evac, 1)

                def added(n):
                    v.wait_ge(acc_evac, b * NACC + (n + 1))

                def a_split(c, i, extra=0):
                    v.wait_ge(a_hi, b * NA + extra + (i + 1))
                    lo(al[:, c % 2, :], act[:, c, :], ah[:, c % 2, :]).then_inc(a_lo, 1)

                v.wait_ge(x_landed, b * 16 + 16)
                norm(0)
                for k in range(8):
                    if k < 4:
                        evac(k, k, sgl[:, k % 2, :], sgh[:, k % 2, :])
                    else:
                        w = slice(2 * k - 8, 2 * k - 6)
                        evac(k, k, v0l[:, w, :].rearrange("p a n -> p (a n)"), v0h[:, w, :].rearrange("p a n -> p (a n)"))
                for i in range(8, 24):
                    evac(i % 8, i, sgl[:, i % 2, :], sgh[:, i % 2, :])
                xt_split(0)

                v.wait_ge(st_done[0], b * (NST * 16) + 32 * 10)
                v.wait_ge(st_done[1], b * (NST * 16) + 32 * 10)
                v.memset(vph[:, :, :].bitcast(F32), 0.0)
                link(v.memset(vpl[:, :, :].bitcast(F32), 0.0))

                def lay_values(g):
                    v.wait_ge(p_used, chunk0(b, g, 0, 0) + 2)
                    o = slice(P - HD0, P)
                    v.tensor_copy(vph[:, :, o], v0h[:, :, ds(g * HD0, HD0)].bitcast(F32))
                    v.tensor_copy(vpl[:, :, o], v0l[:, :, ds(g * HD0, HD0)].bitcast(F32)).then_inc(vp_ready, 1)

                def q_evac(u, o, scale, h):
                    v.wait_ge(qt_hi, u + 1)
                    scaled_lo(o, ps[:, QB, :], scale, h).then_inc(qt_lo, 1)

                def max0(g, j, t):
                    v.wait_ge(s_ready, tile0(b, g, j, t) + 1)
                    v.tensor_reduce(nmax[:, j % 2, t:t + 1], ps[:, 2 * (t % 2):2 * (t % 2) + 2, :].rearrange("p a n -> p (a n)"),
                                    X, ALU.max, negate=True).then_inc(mx_done, 1)

                def p_split(n, c, o, h):
                    v.wait_ge(p_hi, n + 1)
                    lo(o[:, c % 2, :], ps[:, TB + c % 2, :], h[:, c % 2, :]).then_inc(p_lo, 1)

                def invert(u, o, i, exps):
                    v.wait_ge(e_done, exps)
                    v.reciprocal(o, i).then_inc(rinv_done, 1)

                def scale_out(u, o, rb, n):
                    v.wait_ge(p_used, n + 3)
                    v.wait_ge(rb_done, u + 2)
                    v.tensor_tensor(o, ps[:, PVB, :], rb, ALU.mult).then_inc(act_done, 1)

                def group0(g, par, more):
                    for j in range(R0):
                        for t in range(TT):
                            if j < R0 - 1:
                                max0(g, j + 1, t)
                            elif more:
                                max0(g + 1, 0, t)
                            if j == R0 - 1 and t == 0:
                                invert(unit0(b, g), rinv[:, par], rs[:, par], tile0(b, g, R0 - 1, TT - 1) + 3)
                            for c in (2 * t, 2 * t + 1):
                                p_split(chunk0(b, g, j, c), c, pl0, ph0)
                            if j == 1 and t == 0 and more:
                                q_evac(unit0(b, g) + 1, ql[:, :], SCALE0, qh[:, :])
                    scale_out(unit0(b, g), act[:, ds(g, 1), :].rearrange("p a n -> p (a n)"), rb0[:, :], chunk0(b, g, R0 - 1, C0 - 1))
                    if more:
                        lay_values(g + 1)

                q_evac(unit0(b, 0), ql[:, :], SCALE0, qh[:, :])
                lay_values(0)
                for t in range(TT):
                    max0(0, 0, t)
                with v.Fori(0, KV0 // 2 - 1) as r:
                    group0(r * 2, 0, True)
                    group0(r * 2 + 1, 1, True)
                group0(KV0 - 2, 0, True)
                group0(KV0 - 1, 1, False)

                for c in range(DC):
                    a_split(c, X_WO0 + c)
                add_banks(3, G_WO0 + 7)
                added(A_WO0 + 8)

                norm(1)
                xt_split(1)
                v.wait_ge(ff_pe, b * NFP + 1)
                link(v.tensor_copy(comb[:, :, :], ps[:, 1, 0:TT * E0].rearrange("p (t e) -> p t e", t=TT)))
                link(v.tensor_reduce(t4[:, 0, :], comb[:, :, :], X, ALU.max))
                v.tensor_tensor(comb[:, :, :], comb[:, :, :], t4[:, 0, :].unsqueeze(2).to_broadcast([P, TT, E0]), ALU.subtract).then_inc(ff_dve, 1)
                v.wait_ge(ff_act, b * NFA + 2)
                link(v.tensor_reduce(t4[:, 1, :], ex0[:, :, :], X, ALU.add))
                link(v.reciprocal(t4[:, 2, :], t4[:, 1, :]))
                link(v.tensor_tensor(pv[:, :, 0:E0], ex0[:, :, :], t4[:, 2, :].unsqueeze(2).to_broadcast([P, TT, E0]), ALU.mult))
                for t in range(TT):
                    ins = v.max(m8[:, t, :], pv[:, t, 0:E0])
                link(ins)
                v.tensor_tensor(t4[:, 3, :], m8[:, :, 0], m8[:, :, 1], ALU.add)
                link(v.tensor_copy(rp[:, :, 0:TOP0], m8[:, :, 0:TOP0]))
                for t in range(TT):
                    ins = v.match_replace(mr[:, t, :], rp[:, t, :], pv[:, t, :], -9.0)
                link(ins)
                v.reciprocal(t4[:, 0, :], t4[:, 3, :])
                link(v.tensor_tensor(ex0[:, :, :], mr[:, :, 0:E0], pv[:, :, 0:E0], ALU.not_equal))
                link(v.tensor_tensor(comb[:, :, :], ex0[:, :, :], pv[:, :, 0:E0], ALU.mult))
                link(v.scalar_tensor_tensor(out=comb[:, :, :], in0=comb[:, :, :], scalar=GAIN0, in1=t4[:, 0, :].unsqueeze(2).to_broadcast([P, TT, E0]),
                                            op0=ALU.mult, op1=ALU.mult))
                v.tensor_copy(gwide0[:, :, :].rearrange("p t (e r) -> p (t e) r", r=RK0),
                              comb[:, :, :].rearrange("p t e -> p (t e)").unsqueeze(2).to_broadcast([P, TT * E0, RK0])).then_inc(ff_dve, 1)
                v.wait_ge(ff_pe, b * NFP + 2)
                v.wait_ge(ff_act, b * NFA + 1)
                v.tensor_tensor(act[:, 0, :], ps[:, 2, :], act[:, 1, :], ALU.mult).then_inc(ff_dve, 1)
                a_split(0, X_B0)
                v.wait_ge(bias_added, b + 1)
                add_banks(4, G_B0)
                added(A_BASE + 8)

                norm(2)
                xt_split(2)
                for k in range(8):
                    evac(k, 24 + k, sgl[:, k % 2, :], sgh[:, k % 2, :])

                with v.Fori(0, KV1) as h:
                    def max1(j, t):
                        v.wait_ge(s_ready, tile1(b, h, j, t) + 1)
                        v.tensor_reduce(nmax[:, j % 2, t:t + 1], ps[:, 0:3, :].rearrange("p a n -> p (a n)"), X, ALU.max,
                                        negate=True).then_inc(mx_done, 1)

                    q_evac(unit1(b, h, 0), q1l[:, 0, :], SCALE1, q1h[:, 0, :])
                    for t in range(TT):
                        max1(0, t)
                    q_evac(unit1(b, h, 1), q1l[:, 1, :], SCALE1, q1h[:, 1, :])
                    for j in range(R1):
                        u = unit1(b, h, j)
                        for t in range(TT):
                            if j < R1 - 1:
                                max1(j + 1, t)
                            if t == 0:
                                invert(u, rinv[:, j % 2, :, 0], rs[:, j % 2, :, 0], tile1(b, h, j, TT - 1) + 3)
                            for i in range(3):
                                p_split(chunk1(b, h, j, 3 * t + i), 3 * t + i, pl1, ph1)
                                if t == 0 and i == 0 and j > 0:
                                    scale_out(u - 1, act[:, j - 1, :], rb1[:, :], chunk1(b, h, j - 1, C1 - 1))
                            if t == 2 and j < R1 - 2:
                                q_evac(u + 2, q1l[:, j % 2, :], SCALE1, q1h[:, j % 2, :])
                    scale_out(unit1(b, h, R1 - 1), act[:, R1 - 1, :], rb1[:, :], chunk1(b, h, R1 - 1, C1 - 1))
                    for c in range(R1):
                        a_split(c, X_WO1 + c, h * R1)
                    add_banks(6, G_WO1 + 7, h * 7, h * DC)

                added(A_WO1 + 8 * KV1)
                norm(3)
                xt_split(3)
                v.wait_ge(ff_pe, b * NFP + 3)
                v.tensor_copy(q16[:, :, :], ps[:, 4, 0:TT * RD1].rearrange("p (t e) -> p t e", t=TT)).then_inc(ff_dve, 1)
                v.wait_ge(ff_pe, b * NFP + 4)
                v.tensor_copy(q16T[:, :], ps[0:RD1, 5, :]).then_inc(ff_dve, 1)
                v.wait_ge(ff_pe, b * NFP + 5)
                link(v.tensor_copy(sc1[:, :, :], ps[:, 6, 0:TT * E1].rearrange("p (t e) -> p t e", t=TT)))
                for t in range(TT):
                    ins = v.max(m16[:, t, 0:8], sc1[:, t, :])
                link(ins)
                for t in range(TT):
                    ins = v.match_replace(sc2[:, t, :], m16[:, t, 0:8], sc1[:, t, :], LOWEST)
                link(ins)
                for t in range(TT):
                    ins = v.max(m16[:, t, 8:16], sc2[:, t, :])
                link(ins)
                for t in range(TT):
                    ins = v.match_replace(sc3[:, t, :], m16[:, t, 8:16], sc2[:, t, :], LOWEST)
                link(ins)
                link(v.tensor_tensor(sc2[:, :, :], sc3[:, :, :], sc1[:, :, :], ALU.not_equal))
                v.tensor_tensor(sc3[:, :, :], sc1[:, :, :], m16[:, :, 0:1].to_broadcast([P, TT, E1]), ALU.subtract).then_inc(ff_dve, 1)
                v.wait_ge(ff_act, b * NFA + 4)
                link(v.tensor_tensor(sc1[:, :, :], ex1[:, :, :], sc2[:, :, :], ALU.mult))
                link(v.tensor_reduce(t4[:, 0, :], sc1[:, :, :], X, ALU.add))
                link(v.reciprocal(t4[:, 1, :], t4[:, 0, :]))
                link(v.scalar_tensor_tensor(out=sc1[:, :, :], in0=sc1[:, :, :], scalar=GAIN1, in1=t4[:, 1, :].unsqueeze(2).to_broadcast([P, TT, E1]),
                                            op0=ALU.mult, op1=ALU.mult))
                v.tensor_copy(gwide1[:, :, :].rearrange("p t (e r) -> p (t e) r", r=RK1),
                              sc1[:, :, :].rearrange("p t e -> p (t e)").unsqueeze(2).to_broadcast([P, TT * E1, RK1])).then_inc(ff_dve, 1)
                v.wait_ge(ff_pe, b * NFP + 6)
                for k in range(ZB):
                    ins = v.tensor_tensor(act[:, k, :], ps[:, k, :], act[:, ZB + k, :], ALU.mult)
                ins.then_inc(ff_dve, 1)
                for c in range(ZB):
                    a_split(c, X_BW + c)
                add_banks(10, NG - 1)
                assert links[0] == NDV, links[0]


def _layout(np, a):
    t = lambda w: np.ascontiguousarray(w.T)
    return {
        "x_in": a["x"],
        "ctxT": np.ascontiguousarray(a["ctx_4096"].transpose(0, 2, 1)),
        "w_kv0": np.concatenate([a["L0_xattn_wk"].T, a["L0_xattn_wv"].T], axis=1),
        "w_kv1": np.concatenate([a["L1_xattn_Wk"], a["L1_xattn_Wv"]], axis=1),
        "wq0": t(a["L0_xattn_wq"]),
        "wo0": t(a["L0_xattn_wo"]),
        "lnw": t(a["L0_xattn_ln_w"].reshape(DC, P)),
        "wbase": t(a["L0_ffn_W_base"]),
        "bbase": a["L0_ffn_b_base"],
        "a0": t(a["L0_ffn_A"].reshape(E0 * RK0, D)),
        "b0": np.ascontiguousarray(a["L0_ffn_B"].transpose(0, 2, 1)).reshape(E0 * RK0, D),
        "wr0": t(a["L0_ffn_W_router"]),
        "wq1": a["L1_xattn_Wq"],
        "wo1": a["L1_xattn_Wo"],
        "aw": t(a["L1_ffn_A_w"]),
        "bw": t(a["L1_ffn_B_w"]),
        "wr1": t(a["L1_ffn_Wq_w"]),
        "keysT": t(a["L1_ffn_keys"]),
    }


def kernel(**inputs):
    import numpy as _np
    import concourse.bacc as _bacc
    from concourse import mybir as _mybir
    from concourse.bass_utils import run_bass_kernel_spmd as _run

    nc = _bacc.Bacc("TRN2", target_bir_lowering=False, num_devices=1)
    arrays, args = {}, []
    for name, a in _layout(_np, {k: _np.asarray(v) for k, v in inputs.items()}).items():
        a = _np.ascontiguousarray(a)
        arrays[f"in_{name}_dram"] = a
        args.append(nc.dram_tensor(f"in_{name}_dram", a.shape, _mybir.dt.from_np(a.dtype), kind="ExternalInput").ap())
    args.append(nc.dram_tensor("out_0_dram", (B, T, D), _mybir.dt.float32, kind="ExternalOutput").ap())
    block_program(nc, *args)
    r = _run(nc, [arrays], core_ids=[0])
    return r.results[0]["out_0_dram"]
```

```python
from contextlib import ExitStack

import concourse.bass as bass
from concourse import mybir

F32 = mybir.dt.float32
F32R = mybir.dt.float32r
ALU = mybir.AluOpType
ACT = mybir.ActivationFunctionType
X = mybir.AxisListType.X
ds = bass.ds

P = 128
B, T, D = 2, 512, 1024
S = 1024
DC = D // P
TT = T // P
H0, KV0, HD0 = 32, 8, 32
R0 = H0 // KV0
H1, KV1, HD1 = 32, 4, 128
R1 = H1 // KV1
S1 = S + T
C0, C1 = S // P, S1 // P
E0, RK0, TOP0, ALPHA0 = 8, 16, 2, 32
E1, RK1, TOP1, ALPHA1 = 64, 8, 16, 32
RD1 = 16
N1 = E1 * RK1
ZB = N1 // P
SCALE0 = 1.0 / float(HD0) ** 0.5
SCALE1 = 1.0 / float(HD1) ** 0.5
GAIN0 = ALPHA0 / RK0
GAIN1 = ALPHA1 / TOP1
EPS = 1e-5
LOWEST = -3.0e38

def cols_of(w):
    return 512 if w < G_Q0 or G_Z <= w < G_BW else D


G_KV0, G_K1, G_V1, G_Q0, G_WO0, G_A0, G_BASE, G_B0 = 0, 8, 16, 24, 32, 40, 41, 49
G_KV1, G_WO1, G_Z, G_BW = 50, 58, 90, 98
NG = 102
NU = KV0 + H1
NTILE = 2 * H0 * TT
NCH0, NCH1 = H0 * C0, H1 * C1
NCHUNK = NCH0 + NCH1
A_KV0, A_K1, A_V1, A_Q0, A_WO0, A_BASE, A_KV1, A_WO1, A_BW = 0, 8, 16, 24, 32, 40, 48, 56, 88
NACC = 96
X_WO0, X_B0, X_WO1, X_BW = 0, 8, 9, 41
NA = 45
NDONE = 7 * 11
NEV = 40
SLOT_X, SLOT_S, SLOT_C, SLOT_A, NSLOT = 0, 8, 10, 12, 16
STAGE = ([SLOT_X + i for i in range(8)] + [SLOT_X + i for i in range(4)]
         + [SLOT_S, SLOT_S + 1, SLOT_C, SLOT_C + 1] * 2
         + [SLOT_A + i for i in range(4)] + [SLOT_S, SLOT_S + 1, SLOT_A, SLOT_A + 1])
NST = len(STAGE)
ST_K0, ST_K1, ST_V1, ST_KV1 = 0, 4, 12, 20
PT0, PT1 = 4, 3
NPT = 3
NUSED = 4
KVL = 8 * 16
LAG0, LAG1 = 3, 2
NDV = 35


def block_program(nc, x_in, ctxT, w_kv0, w_kv1, wq0, wo0, lnw, wbase, bbase, a0, b0, wr0,
                  wq1, wo1, aw, bw, wr1, keysT, out):
    ctx = ExitStack()
    with ctx:
        def sb(name, shape, dt, stack=ctx):
            return stack.enter_context(nc.sbuf_tensor(name, shape, dt))

        def sem(name):
            return ctx.enter_context(nc.semaphore(name))

        k0s = nc.dram_tensor("k0s", [B, 2, KV0 * HD0, S], F32).ap()
        k1s = nc.dram_tensor("k1s", [B, 2, KV1, P, S1], F32).ap()
        v1s = nc.dram_tensor("v1s", [B, 2, C1, P, KV1 * HD1], F32).ap()

        x = sb("x", [P, TT, D], F32)
        act = sb("act", [P, DC, T], F32)
        xn = act[:, :, :].rearrange("p (t a) n -> p t (a n)", t=TT)
        graw = sb("graw", [P, 2, D], F32)
        gh = sb("gh", [P, 2, D], F32R)
        gl = sb("gl", [P, 2, D], F32R)
        qraw = sb("qraw", [P, DC, P], F32)
        qwh = sb("qwh", [P, DC, P], F32R)
        qwl = sb("qwl", [P, DC, P], F32R)
        ah = sb("ah", [P, 2, T], F32R)
        al = sb("al", [P, 2, T], F32R)
        sgh, sgl = ah, al
        ident = sb("ident", [P, P], F32)
        lnw_sb = sb("lnw_sb", [P, DC], F32)
        wr0_raw = sb("wr0_raw", [P, DC, E0], F32)
        wr0h = sb("wr0h", [P, DC, E0], F32R)
        wr0l = sb("wr0l", [P, DC, E0], F32R)
        wr1_raw = sb("wr1_raw", [P, DC, RD1], F32)
        wr1h = sb("wr1h", [P, DC, RD1], F32R)
        wr1l = sb("wr1l", [P, DC, RD1], F32R)
        keys_sb = sb("keys_sb", [RD1, E1], F32)
        neghalf = sb("neghalf", [P, TT], F32)
        stats = sb("stats", [P, TT, 12], F32)
        mv = sb("mv", [P, TT, 2], F32)
        ve = sb("ve", [P, TT], F32)
        rstd = sb("rstd", [P, TT], F32)
        ssq = sb("ssq", [P, TT], F32)
        nmax = sb("nmax", [P, 2, TT], F32)
        rs = sb("rs", [P, 2, TT, R0], F32)
        rinv = sb("rinv", [P, 2, TT, R0], F32)
        pv = sb("pv", [P, TT, 14], F32)
        m8 = sb("m8", [P, TT, 8], F32)
        rp = sb("rp", [P, TT, 8], F32)
        mr = sb("mr", [P, TT, 14], F32)
        ex0 = sb("ex0", [P, TT, E0], F32)
        comb = sb("comb", [P, TT, E0], F32)
        t4 = sb("t4", [P, 4, TT], F32)

        with ExitStack() as part:
            e0 = sb("e0", [P, 2 * TT, S], F32, part)
        xh = sb("xh", [P, DC, T], F32R)
        xl = sb("xl", [P, DC, T], F32R)
        with ExitStack() as part:
            v0h = sb("v0h", [P, C0, KV0 * HD0], F32R, part)
            v0l = sb("v0l", [P, C0, KV0 * HD0], F32R, part)
            with ExitStack() as inner:
                ch = sb("ch", [P, DC, S], F32R, inner)
                cl = sb("cl", [P, DC, S], F32R, inner)
                craw = sb("craw", [P, 2, S], F32, inner)
            with ExitStack() as inner:
                VW = 2 * P - HD0
                vph = sb("vph", [P, C0, VW], F32R, inner)
                vpl = sb("vpl", [P, C0, VW], F32R, inner)
                kp = sb("kp", [P, 2, S], F32R, inner)
                qp = sb("qp", [P, R0, T], F32R, inner)
                qh = sb("qh", [P, KV0, T], F32R, inner)
                ql = sb("ql", [P, KV0, T], F32R, inner)
                ph0 = sb("ph0", [P, PT0, T], F32R, inner)
                pl0 = sb("pl0", [P, PT0, T], F32R, inner)
                rb0 = sb("rb0", [P, T], F32, inner)
                rwide = sb("rwide", [P, TT, P], F32, inner)
        with ExitStack() as part:
            e1 = sb("e1", [P, 2 * TT, S1], F32, part)
            ph1 = sb("ph1", [P, PT1, T], F32R, part)
            pl1 = sb("pl1", [P, PT1, T], F32R, part)
            k1h = sb("k1h", [P, S1], F32R, part)
            k1l = sb("k1l", [P, S1], F32R, part)
            v1h = sb("v1h", [P, C1, P], F32R, part)
            v1l = sb("v1l", [P, C1, P], F32R, part)
            q1h = sb("q1h", [P, 2, T], F32R, part)
            q1l = sb("q1l", [P, 2, T], F32R, part)
            rb1 = sb("rb1", [P, T], F32, part)
        with ExitStack() as part:
            bias_sb = sb("bias_sb", [P, D], F32, part)
            gwide0 = sb("gwide0", [P, TT, P], F32, part)
        with ExitStack() as part:
            sc1 = sb("sc1", [P, TT, E1], F32, part)
            sc2 = sb("sc2", [P, TT, E1], F32, part)
            sc3 = sb("sc3", [P, TT, E1], F32, part)
            ex1 = sb("ex1", [P, TT, E1], F32, part)
            m16 = sb("m16", [P, TT, 16], F32, part)
            q16 = sb("q16", [P, TT, RD1], F32, part)
            q16T = sb("q16T", [RD1, T], F32, part)
            gwide1 = sb("gwide1", [P, TT, N1], F32, part)

        ps = ctx.enter_context(nc.psum_tensor("ps", [P, 8, 512], F32))
        TB0, TB1 = (4, 5, 7), (3, 4, 5)
        PVB, QB = 6, 7
        s_bank = lambda j, t: 3 * (t % 2) if j == 0 else 0
        q_bank = lambda j: QB if j > 0 else TB1[0]

        const_dma = sem("const_dma")
        const_hi = sem("const_hi")
        const_ready = sem("const_ready")
        bias_landed = sem("bias_landed")
        bias_added = sem("bias_added")
        x_landed = sem("x_landed")
        out_stored = sem("out_stored")
        ctx_landed = [sem(f"ctx_landed{i}") for i in range(2)]
        ctx_hi = sem("ctx_hi")
        ctx_lo = sem("ctx_lo")
        g_landed = [sem(f"g_landed{i}") for i in range(2)]
        g_hi = sem("g_hi")
        g_lo = sem("g_lo")
        g_used = sem("g_used")
        q_landed = sem("q_landed")
        q_hi = sem("q_hi")
        q_lo = sem("q_lo")
        a_hi = sem("a_hi")
        a_lo = sem("a_lo")
        acc_done = sem("acc_done")
        ev_hi = sem("ev_hi")
        acc_evac = sem("acc_evac")
        st_done = [sem(f"st_done{i}") for i in range(NSLOT)]
        ln_dve = sem("ln_dve")
        ln_pool = sem("ln_pool")
        xn_ready = sem("xn_ready")
        xt_ready = sem("xt_ready")
        xt_hi = sem("xt_hi")
        xt_lo = sem("xt_lo")
        qt_done = sem("qt_done")
        qt_hi = sem("qt_hi")
        qt_lo = sem("qt_lo")
        q_packed = [sem(f"q_packed{j}") for j in range(R0)]
        k_packed = [sem(f"k_packed{i}") for i in range(2)]
        kv_landed = sem("kv_landed")
        vp_ready = sem("vp_ready")
        s_ready = sem("s_ready")
        mx_done = sem("mx_done")
        e_done = sem("e_done")
        rinv_done = sem("rinv_done")
        rwide_done = sem("rwide_done")
        rb_ready = sem("rb_ready")
        rb_done = sem("rb_done")
        t_ready = sem("t_ready")
        p_hi = sem("p_hi")
        p_lo = sem("p_lo")
        p_used = sem("p_used")
        act_done = sem("act_done")
        ff_pe = sem("ff_pe")
        ff_act = sem("ff_act")
        ff_dve = sem("ff_dve")
        dv = sem("dv")
        sp_steps = sem("sp_steps")
        pool_steps = sem("pool_steps")
        dve_steps = sem("dve_steps")
        pool_c = sem("pool_c")
        dve_c = sem("dve_c")

        block = ctx.enter_context(nc.Block())

        def G(b, w):
            return b * NG + (w + 1 + 2)

        def tile0(b, g, j, t):
            return b * NTILE + g * (R0 * TT) + (j * TT + t)

        def tile1(b, h, j, t):
            return b * NTILE + h * (R1 * TT) + (H0 * TT + j * TT + t)

        def chunk0(b, g, j, c):
            return b * NCHUNK + g * (R0 * C0) + (j * C0 + c)

        def chunk1(b, h, j, c):
            return b * NCHUNK + h * (R1 * C1) + (NCH0 + j * C1 + c)

        def place0(j, c):
            return j * C0 + c + (1 if j == R0 - 1 and c >= 4 else 0)

        RB0 = TB0[(place0(R0 - 1, 3) + 1) % NPT]

        def unit0(b, g):
            return b * NU + g

        def unit1(b, h, j):
            return b * NU + h * R1 + (KV0 + j)

        def head1(b, h, j):
            return b * H1 + h * R1 + j

        NLN, NFP, NFA, NFD = 5, 6, 4, 8

        def wait_bank(eng, b, phase, k, w_last, ph_extra=0, w_extra=0):
            if k < 7:
                eng.wait_ge(acc_done, b * NDONE + ph_extra + (phase * 7 + k + 1))
            else:
                eng.wait_ge(g_used, G(b, w_last) + w_extra)

        def stored(b, i):
            slot = STAGE[i]
            return st_done[slot], b * (STAGE.count(slot) * 32) + STAGE[:i + 1].count(slot) * 32

        def wait_slot(eng, b, i):
            if STAGE[i] in STAGE[:i]:
                semaphore, count = stored(b, i)
                eng.wait_ge(semaphore, count - 32)

        def stage(i):
            slot = STAGE[i]
            if slot < SLOT_S:
                return xh[:, slot, :], xl[:, slot, :]
            if slot < SLOT_C:
                return sgh[:, slot - SLOT_S, :], sgl[:, slot - SLOT_S, :]
            if slot < SLOT_A:
                k = slot - SLOT_C
                return craw[:, k, 0:T].bitcast(F32R), craw[:, k, T:2 * T].bitcast(F32R)
            k = 2 * (slot - SLOT_A)
            return act[:, k, :].bitcast(F32R), act[:, k + 1, :].bitcast(F32R)

        @block.sync
        def _(sp):
            def wait(semaphore, value):
                sp.wait_ge(semaphore, value)
                sp.sem_inc(sp_steps, 1)

            sp.dma_start(lnw_sb[:, :], lnw).then_inc(const_dma, 16)
            sp.dma_start(wr0_raw[:, :, :], wr0.rearrange("(c p) e -> p c e", p=P)).then_inc(const_dma, 16)
            sp.dma_start(wr1_raw[:, :, :], wr1.rearrange("(c p) e -> p c e", p=P)).then_inc(const_dma, 16)
            sp.dma_start(keys_sb[:, :], keysT).then_inc(const_dma, 16)

            sp.sem_inc(out_stored, 16)
            with sp.Fori(0, B) as b:
                def load_g(w, src, cols=D, extra=0):
                    wait(g_lo, b * NG + extra + (w + 1))
                    sp.dma_start(graw[:, w % 2, 0:cols], src).then_inc(g_landed[w % 2], 16)

                def load_q(u, src):
                    wait(q_lo, u + 1)
                    sp.dma_start(qraw[:, :, :], src).then_inc(q_landed, 16)

                def rows(w, c, lo=0, n=D):
                    return w[c * P:(c + 1) * P, lo:lo + n]

                def wq0_tile(g):
                    return wq0.rearrange("(c p) n -> p c n", p=P)[:, :, ds(g * P, P)]

                def wq1_tile(n):
                    return wq1.rearrange("(c p) n -> p c n", p=P)[:, :, ds(n * P, P)]

                for c in range(DC):
                    if c >= 2:
                        wait(ctx_lo, b * DC + (c - 1))
                    sp.dma_start(craw[:, c % 2, :], ctxT[ds(b, 1), c * P:(c + 1) * P, :].rearrange("a p s -> p (a s)")).then_inc(ctx_landed[c % 2], 16)
                    load_g(G_KV0 + c, rows(w_kv0, c, 0, 512), 512)
                    if c == 1:
                        wait(out_stored, b * 16 + 16)
                        sp.dma_start(x[:, :, :], x_in[ds(b, 1)].rearrange("a (t p) d -> p (a t) d", p=P)).then_inc(x_landed, 16)

                def store(i, acc, dst_h, dst_l):
                    wait(acc_evac, b * NACC + (acc + 2))
                    high, low = stage(i)
                    sp.dma_start(dst_h, high.bitcast(F32)).then_inc(st_done[STAGE[i]], 16)
                    sp.dma_start(dst_l, low.bitcast(F32)).then_inc(st_done[STAGE[i]], 16)

                def wait_stores(first, last):
                    for slot in sorted(set(STAGE[first:last])):
                        wait(*stored(b, max(i for i in range(first, last) if STAGE[i] == slot)))

                def k0_dst(part, i):
                    return k0s[ds(b, 1), part, (i // 2) * P:(i // 2 + 1) * P, (i % 2) * T:(i % 2 + 1) * T].rearrange("a p s -> p (a s)")

                def k1_dst(part, h, s0):
                    return k1s[ds(b, 1), part, h, :, s0:s0 + T].rearrange("a p s -> p (a s)")

                def v1_dst(part, c):
                    return v1s[ds(b, 1), part, c].rearrange("a p n -> p (a n)")

                load_g(G_K1, rows(w_kv1, 0, 0, 512), 512)
                load_g(G_K1 + 1, rows(w_kv1, 1, 0, 512), 512)
                for i in range(4):
                    store(ST_K0 + i, A_KV0 + i, k0_dst(0, i), k0_dst(1, i))
                for c in range(2, DC):
                    load_g(G_K1 + c, rows(w_kv1, c, 0, 512), 512)
                load_g(G_V1, rows(w_kv1, 0, 512, 512), 512)
                load_g(G_V1 + 1, rows(w_kv1, 1, 512, 512), 512)
                for i in range(8):
                    store(ST_K1 + i, A_K1 + i, k1_dst(0, i // 2, (i % 2) * T), k1_dst(1, i // 2, (i % 2) * T))
                    if i % 4 == 3:
                        load_g(G_V1 + 2 + i // 4, rows(w_kv1, 2 + i // 4, 512, 512), 512)
                for c in range(4, DC):
                    load_g(G_V1 + c, rows(w_kv1, c, 512, 512), 512)
                load_g(G_Q0, wq0_tile(0))
                load_g(G_Q0 + 1, wq0_tile(1))
                for i in range(8):
                    store(ST_V1 + i, A_V1 + i, v1_dst(0, i), v1_dst(1, i))
                    if i % 4 == 3:
                        load_g(G_Q0 + 2 + i // 4, wq0_tile(2 + i // 4))

                def pack_k(g, par):
                    for r in range(4):
                        sp.dma_start(kp[r * HD0:(r + 1) * HD0, par, :].bitcast(F32),
                                     k0s[ds(b, 1), r // 2, ds(g * HD0, HD0), :].rearrange("a p s -> p (a s)")).then_inc(k_packed[par], 16)

                def pack_q(g, j):
                    for r in range(4):
                        sp.dma_start(qp[r * HD0:(r + 1) * HD0, j, :].bitcast(F32),
                                     (qh, ql)[r % 2][j * HD0:(j + 1) * HD0, ds(g, 1), :].rearrange("p a n -> p (a n)").bitcast(F32)).then_inc(q_packed[j], 16)

                wait_stores(ST_K0, ST_K1)
                wait_stores(ST_V1, ST_KV1)
                pack_k(0, 0)
                wait(acc_evac, b * NACC + (A_Q0 + 2))
                for j in range(R0):
                    pack_q(0, j)
                for g in range(4, KV0):
                    load_g(G_Q0 + g, wq0_tile(g))
                load_g(G_WO0, rows(wo0, 0))
                load_g(G_WO0 + 1, rows(wo0, 1))
                wait(acc_evac, b * NACC + (A_Q0 + 9))

                def group0(g, par, more):
                    if more:
                        wait(s_ready, tile0(b, g, 0, TT - 1) + 1)
                        pack_k(g + 1, 1 - par)
                        for j in range(R0):
                            wait(s_ready, tile0(b, g, j, TT - 1) + 1)
                            pack_q(g + 1, j)

                with sp.Fori(0, KV0 // 2 - 1) as r:
                    group0(r * 2, 0, True)
                    group0(r * 2 + 1, 1, True)
                group0(KV0 - 2, 0, True)
                for c in range(2, DC):
                    load_g(G_WO0 + c, rows(wo0, c))

                wait(act_done, unit0(b, KV0 - 1) + 2)
                sp.dma_start(bias_sb[:, :], bbase.rearrange("(a d) -> a d", a=1).to_broadcast([P, D])).then_inc(bias_landed, 16)
                load_g(G_A0, a0.rearrange("(c p) n -> p c n", p=P))
                for c in range(DC):
                    load_g(G_BASE + c, rows(wbase, c))
                load_g(G_B0, b0)
                def load_k1(h, lo, hi):
                    for part, dst in ((0, k1h), (1, k1l)):
                        sp.dma_start(dst[:, lo:hi].bitcast(F32), k1s[ds(b, 1), part, ds(h, 1), :, lo:hi].rearrange("a h p s -> p (a h s)")).then_inc(kv_landed, 16)

                def load_v1(h, lo, hi):
                    for part, dst in ((0, v1h), (1, v1l)):
                        sp.dma_start(dst[:, lo:hi, :].bitcast(F32), v1s[ds(b, 1), part, lo:hi, :, ds(h * HD1, HD1)].rearrange("a c p n -> p (a c) n")).then_inc(kv_landed, 16)

                load_g(G_KV1, rows(w_kv1, 0))
                load_g(G_KV1 + 1, rows(w_kv1, 1))
                load_q(head1(b, 0, 0), wq1_tile(0))
                wait_stores(ST_K1, ST_V1)
                wait_stores(ST_V1, ST_KV1)
                load_k1(0, 0, S)
                load_v1(0, 0, C0)
                for c in range(2, DC):
                    load_g(G_KV1 + c, rows(w_kv1, c))
                for i in range(8):
                    if i < 4:
                        store(ST_KV1 + i, A_KV1 + i, k1_dst(0, i, S), k1_dst(1, i, S))
                    else:
                        store(ST_KV1 + i, A_KV1 + i, v1_dst(0, C0 + i - 4), v1_dst(1, C0 + i - 4))
                wait(*stored(b, ST_KV1))
                load_k1(0, S, S1)
                wait_stores(ST_KV1, NST)
                load_v1(0, C0, C1)

                def head_weights(h, more):
                    for j in range(1, R1):
                        load_q(head1(b, h, j), wq1_tile(h * R1 + j))
                    for c in range(DC):
                        if c == 2 and more:
                            load_q(head1(b, h + 1, 0), wq1_tile((h + 1) * R1))
                            wait(s_ready, tile1(b, h + 1, 0, 0))
                            load_k1(h + 1, 0, S)
                            load_k1(h + 1, S, S1)
                            wait(p_used, chunk1(b, h + 1, 0, 0) + NUSED)
                            load_v1(h + 1, 0, C0)
                            load_v1(h + 1, C0, C1)
                        load_g(G_WO1 + c, wo1[ds(h * (R1 * HD1) + c * P, P), :], extra=h * DC)

                with sp.Fori(0, KV1 - 1) as h:
                    head_weights(h, True)
                head_weights(KV1 - 1, False)
                for c in range(DC):
                    load_g(G_Z + c, rows(aw, c, 0, N1), N1)
                for c in range(ZB):
                    load_g(G_BW + c, rows(bw, c))
                wait(acc_evac, b * NACC + (NACC + 1))
                sp.dma_start(out[ds(b, 1)].rearrange("a (t p) d -> p (a t) d", p=P), x[:, :, :]).then_inc(out_stored, 16)
            sp.wait_ge(out_stored, (B + 1) * 16)

        @block.tensor
        def _(pe):
            def mm3(o, wh, wl, mh, ml, start, stop, check=True):
                pe.matmul(o, wh, mh, start=start, stop=False, skip_group_check=not check)
                pe.matmul(o, wh, ml, start=False, stop=False, skip_group_check=not check)
                return pe.matmul(o, wl, mh, start=False, stop=stop, skip_group_check=not check)

            pe.sem_inc(g_used, 2)
            pe.sem_inc(p_used, NUSED)
            pe.sem_inc(qt_done, 1)
            pe.wait_ge(const_ready, 3)

            with pe.Fori(0, B) as b:
                def wait_acc(n):
                    pe.wait_ge(acc_evac, b * NACC + (n + 1))

                def gemm(w0, extra, acc, chunks, before=None):
                    n = len(chunks)
                    for c in range(n):
                        s = (w0 + c) % 2
                        for wait in chunks[c][0]:
                            wait()
                        pe.wait_ge(g_lo, G(b, w0 + c) + extra)
                        first, last = c == 0, c == n - 1
                        for k in range(8):
                            if first and before is not None:
                                before(k)
                            for o, wh, wl, mh, ml, opens, check in chunks[c][1](c, s, k):
                                mm = mm3(o, wh, wl, mh, ml, first and opens, last, check)
                            if k == 7:
                                mm.then_inc(g_used, 1)
                            elif last:
                                mm.then_inc(acc_done, 1)

                def evacuated(n, extra=0):
                    def wait(k):
                        pe.wait_ge(acc_evac, b * NACC + extra + (n + k + 2))
                    return wait

                def kv0_bank(c, s, k):
                    if k < 4:
                        w = slice((k // 2) * P, (k // 2 + 1) * P)
                        m = slice((k % 2) * T, (k % 2 + 1) * T)
                        return [(ps[:, k, :], gh[:, s, w], gl[:, s, w], ch[:, c, m], cl[:, c, m], True, True)]
                    return [(ps[:, k, i * 256:(i + 1) * 256],
                             ch[:, c, (2 * k - 8 + i) * P:(2 * k - 7 + i) * P], cl[:, c, (2 * k - 8 + i) * P:(2 * k - 7 + i) * P],
                             gh[:, s, 256:512], gl[:, s, 256:512], i == 0, False) for i in range(2)]

                def ctx_chunk(c):
                    return [lambda: pe.wait_ge(ctx_lo, b * DC + (c + 1))]

                wait_acc(0)
                gemm(G_KV0, 0, A_KV0, [(ctx_chunk(c), kv0_bank) for c in range(DC)])

                def k1_bank(c, s, k):
                    w = slice((k // 2) * P, (k // 2 + 1) * P)
                    m = slice((k % 2) * T, (k % 2 + 1) * T)
                    return [(ps[:, k, :], gh[:, s, w], gl[:, s, w], ch[:, c, m], cl[:, c, m], True, True)]

                gemm(G_K1, 0, A_K1, [([], k1_bank)] * DC, evacuated(A_KV0))

                def v1_bank(c, s, k):
                    w = slice(k * P, (k + 1) * P)
                    return [(ps[:, k, :], ch[:, c, w], cl[:, c, w], gh[:, s, 0:512], gl[:, s, 0:512], True, True)]

                gemm(G_V1, 0, A_V1, [([], v1_bank)] * DC, evacuated(A_K1))

                def transpose_x(p, before=None):
                    for t in range(TT):
                        pe.wait_ge(xn_ready, b * (4 * TT) + (p * TT + t + 1))
                        for c in range(DC):
                            if t == 0 and before is not None:
                                before(c)
                            tr = pe.transpose(ps[:, c, t * P:(t + 1) * P], xn[:, t, c * P:(c + 1) * P], ident[:, :])
                            if t == TT - 1:
                                tr.then_inc(xt_ready, 1)

                def split_x(p):
                    def wait(c):
                        pe.wait_ge(xt_lo, b * (4 * DC) + (p * DC + c + 1))
                    return wait

                transpose_x(0, evacuated(A_V1))

                for g in range(KV0):
                    pe.wait_ge(g_lo, G(b, G_Q0 + g))
                    for c in range(DC):
                        if g == 0:
                            split_x(0)(c)
                        w = slice(c * P, (c + 1) * P)
                        mm = mm3(ps[:, g, :], gh[:, g % 2, w], gl[:, g % 2, w], xh[:, c, :], xl[:, c, :], c == 0, c == DC - 1)
                    mm.then_inc(g_used, 1)

                def q_project(h, j, cs):
                    if cs[0] == 0:
                        pe.wait_ge(q_lo, head1(b, h, j) + 2)
                        pe.wait_ge(qt_lo, head1(b, h, j) + 1)
                        if j >= 3:
                            pe.wait_ge(rb_done, unit1(b, h, j) - 1)
                    for c in cs:
                        mm = mm3(ps[:, q_bank(j), :], qwh[:, c, :], qwl[:, c, :], xh[:, c, :], xl[:, c, :], c == 0, c == DC - 1)
                    if cs[-1] == DC - 1:
                        mm.then_inc(qt_done, 1)

                def scores0(g, par, j, t):
                    a = tile0(b, g, j, t)
                    pe.wait_ge(e_done, a + 1)
                    for half in range(2):
                        mm = pe.matmul(ps[:, 2 * (t % 2) + half, :], qp[:, j, t * P:(t + 1) * P],
                                       kp[:, par, half * 512:(half + 1) * 512], start=True, stop=True)
                    mm.then_inc(s_ready, 1)

                def packed(n, j, par, m):
                    pe.wait_ge(q_packed[j], n * 64 + 64)
                    if j == 0:
                        pe.wait_ge(k_packed[par], m * 64 + 64)

                def transpose_p(bank, e, c, exps):
                    if c == 0:
                        pe.wait_ge(e_done, exps)
                    for t in range(TT):
                        tr = pe.transpose(ps[:, bank, t * P:(t + 1) * P], e[:, t, c * P:(c + 1) * P], ident[:, :])
                    tr.then_inc(t_ready, 1)

                def turned_free0(g, j, c):
                    last = j == R0 - 1
                    if last and c == 6:
                        pe.wait_ge(rb_done, unit0(b, g) + 2)
                    elif last and c in (4, 5):
                        pe.wait_ge(p_lo, chunk0(b, g, j, c) - 2 + (NPT + 1))
                    else:
                        pe.wait_ge(p_lo, chunk0(b, g, j, c) + 1)

                def pv0(g, j, c):
                    n = chunk0(b, g, j, c)
                    first, last = j == 0 and c == 0, j == R0 - 1 and c == C0 - 1
                    if first:
                        pe.wait_ge(vp_ready, b * KV0 + g + 1)
                        pe.wait_ge(act_done, unit0(b, g) + 1)
                    pe.wait_ge(p_lo, n + (1 + NPT))
                    w = slice(P - HD0 - j * HD0, 2 * P - HD0 - j * HD0)
                    mm3(ps[:, PVB, :], vph[:, c, w], vpl[:, c, w], ph0[:, c % PT0, :], pl0[:, c % PT0, :],
                        first, last).then_inc(p_used, 1)

                def broadcast_rinv(bank, src, ready, count, u):
                    pe.wait_ge(ready, count)
                    for t in range(TT):
                        tr = pe.transpose(ps[:, bank, t * P:(t + 1) * P], src(t), ident[:, :])
                    tr.then_inc(rb_ready, 1)

                def step0(g, par, j, t, more, m, pending):
                    if j < R0 - 1:
                        if t == 0:
                            packed(b * KV0 + g, j + 1, par, m)
                        scores0(g, par, j + 1, t)
                    elif more:
                        if t == 0:
                            packed(b * KV0 + g + 1, 0, 1 - par, m + par)
                        scores0(g + 1, 1 - par, 0, t)
                    for c in (2 * t, 2 * t + 1):
                        turned_free0(g, j, c)
                        transpose_p(TB0[place0(j, c) % NPT], e0[:, (j % 2) * TT:(j % 2) * TT + TT, :], c, tile0(b, g, j, TT - 1) + 3)
                        pending.append((g, j, c))
                        if len(pending) > LAG0:
                            pv0(*pending.pop(0))
                    if j == R0 - 1 and t == 1:
                        pe.wait_ge(p_lo, chunk0(b, g, j, 4) - 3 + (NPT + 1))
                        broadcast_rinv(RB0, lambda i: rwide[:, i, :], rwide_done, b * KV0 + g + 1, unit0(b, g))

                def group0(g, par, more, m):
                    pending = [(g, 0, 0), (g, 0, 1)]
                    for j in range(R0):
                        for t in range(TT):
                            if j > 0 or t > 0:
                                step0(g, par, j, t, more, m, pending)
                    if more:
                        step0(g + 1, 1 - par, 0, 0, True, m + par, pending)
                        while pending[0][1] == R0 - 1:
                            pv0(*pending.pop(0))
                    else:
                        for step in pending:
                            pv0(*step)

                wait_acc(A_Q0 + 8)
                packed(b * KV0, 0, 0, b * (KV0 // 2))
                for t in range(TT):
                    scores0(0, 0, 0, t)
                step0(0, 0, 0, 0, True, b * (KV0 // 2), [])
                with pe.Fori(0, KV0 // 2 - 1) as r:
                    group0(r * 2, 0, True, b * (KV0 // 2) + r)
                    group0(r * 2 + 1, 1, True, b * (KV0 // 2) + r)
                group0(KV0 - 2, 0, True, b * (KV0 // 2) + KV0 // 2 - 1)
                group0(KV0 - 1, 1, False, b * (KV0 // 2) + KV0 // 2 - 1)

                def out_bank(sh, sl):
                    def bank(c, s, k):
                        w = slice((k // 2) * P, (k // 2 + 1) * P)
                        m = slice((k % 2) * 512, (k % 2 + 1) * 512)
                        return [(ps[:, k, :], sh(c)[:, w], sl(c)[:, w], gh[:, s, m], gl[:, s, m], True, True)]
                    return bank

                def split_act(i, extra=0):
                    return [lambda: pe.wait_ge(a_lo, b * NA + extra + (i + 1))]

                ring_bank = out_bank(lambda c: ah[:, c % 2, :], lambda c: al[:, c % 2, :])
                def output0_read(k):
                    if k == PVB:
                        pe.wait_ge(act_done, unit0(b, KV0 - 1) + 2)
                gemm(G_WO0, 0, A_WO0, [(split_act(X_WO0 + c), ring_bank) for c in range(DC)], output0_read)

                transpose_x(1)

                pe.wait_ge(g_lo, G(b, G_A0))
                wa = lambda w, c: w[:, G_A0 % 2, c * P:(c + 1) * P]
                for c in range(DC):
                    split_x(1)(c)
                    mm = mm3(ps[:, 0, :], wa(gh, c), wa(gl, c), xh[:, c, :], xl[:, c, :], c == 0, c == DC - 1)
                mm.then_inc(g_used, 1)

                def router(bank, wh, wl, n):
                    for t in range(TT):
                        w = slice(t * P, (t + 1) * P)
                        for c in range(DC):
                            mm = mm3(ps[:, bank, t * n:(t + 1) * n], xh[:, c, w], xl[:, c, w], wh[:, c, :], wl[:, c, :],
                                     c == 0, c == DC - 1)
                    mm.then_inc(ff_pe, 1)

                router(1, wr0h, wr0l, E0)
                pe.wait_ge(ff_dve, b * 8 + 2)
                for t in range(TT):
                    tr = pe.transpose(ps[:, 2, t * P:(t + 1) * P], gwide0[:, t, :], ident[:, :])
                tr.then_inc(ff_pe, 1)
                pe.wait_ge(ff_dve, b * 8 + 3)
                x_bank = out_bank(lambda c: xh[:, c, :], lambda c: xl[:, c, :])
                low_bank = out_bank(lambda c: ah[:, 0, :], lambda c: al[:, 0, :])
                gemm(G_BASE, 0, A_BASE, [([], x_bank)] * DC + [(split_act(X_B0), low_bank)])

                transpose_x(2)

                def kv1_bank(c, s, k):
                    if k < 4:
                        w = slice(k * P, (k + 1) * P)
                        return [(ps[:, k, :], gh[:, s, w], gl[:, s, w], xh[:, c, :], xl[:, c, :], True, True)]
                    w = slice((k - 4) * P, (k - 3) * P)
                    return [(ps[:, k, :], xh[:, c, w], xl[:, c, w], gh[:, s, 512:], gl[:, s, 512:], True, True)]

                gemm(G_KV1, 0, A_KV1, [([], kv1_bank)] * DC, split_x(2))

                with pe.Fori(0, KV1) as h:
                    def scores1(j, t):
                        a = tile1(b, h, j, t)
                        pe.wait_ge(e_done, a + (2 if j > 0 else 1))
                        if t == 0:
                            pe.wait_ge(qt_lo, head1(b, h, j) + 2)
                        w = slice(t * P, (t + 1) * P)
                        for k in range(3):
                            m = slice(k * 512, (k + 1) * 512)
                            mm = mm3(ps[:, s_bank(j, t) + k, :], q1h[:, j % 2, w], q1l[:, j % 2, w], k1h[:, m], k1l[:, m], True, True)
                        mm.then_inc(s_ready, 1)

                    def pv1(j, c):
                        if c == 0:
                            pe.wait_ge(act_done, unit1(b, h, j) + 1)
                        pe.wait_ge(p_lo, chunk1(b, h, j, c) + (1 + NPT))
                        mm3(ps[:, PVB, :], v1h[:, c, :], v1l[:, c, :], ph1[:, c % PT1, :], pl1[:, c % PT1, :],
                            c == 0, c == C1 - 1).then_inc(p_used, 1)

                    pe.wait_ge(acc_evac, b * NACC + h * 8 + (A_WO1 - 3))
                    q_project(h, 0, list(range(DC)))
                    pe.wait_ge(kv_landed, b * (KV1 * KVL) + h * KVL + KVL)
                    pe.wait_ge(acc_evac, b * NACC + h * 8 + (A_WO1 + 1))
                    for t in range(TT):
                        scores1(0, t)
                        q_project(h, 1, [2 * t, 2 * t + 1])
                    pending = []
                    for j in range(R1):
                        for t in range(TT):
                            if j < R1 - 1:
                                scores1(j + 1, t)
                            for i in range(3):
                                c = 3 * t + i
                                pe.wait_ge(p_lo, chunk1(b, h, j, c) + 1)
                                transpose_p(TB1[c % NPT], e1[:, (j % 2) * TT:(j % 2) * TT + TT, :], c, tile1(b, h, j, TT - 1) + 3)
                                if 1 <= c <= DC and j < R1 - 2:
                                    q_project(h, j + 2, [c - 1])
                                pending.append((j, c))
                                while len(pending) > LAG1 or pending[0][0] < j:
                                    pv1(*pending.pop(0))
                            if t == 3:
                                if j < R1 - 2:
                                    pe.wait_ge(qt_lo, head1(b, h, j) + 4)
                                else:
                                    pe.wait_ge(rb_done, unit1(b, h, j) + 1)
                                broadcast_rinv(QB, lambda i: rinv[:, j % 2, i, 0:1].to_broadcast([P, P]), rinv_done, unit1(b, h, j) + 1, unit1(b, h, j))
                    for step in pending:
                        pv1(*step)

                    def output1_read(k):
                        if k == PVB:
                            pe.wait_ge(act_done, unit1(b, h, R1 - 1) + 2)
                    gemm(G_WO1, h * DC, A_WO1, [(split_act(X_WO1 + c, h * R1), ring_bank) for c in range(R1)], output1_read)

                transpose_x(3)
                for c in range(DC):
                    s = (G_Z + c) % 2
                    pe.wait_ge(g_lo, G(b, G_Z + c))
                    if c >= ZB:
                        split_x(3)(c)
                    for k in range(ZB):
                        if c == 0:
                            split_x(3)(k)
                        w = slice(k * P, (k + 1) * P)
                        mm = mm3(ps[:, k, :], gh[:, s, w], gl[:, s, w], xh[:, c, :], xl[:, c, :], c == 0, c == DC - 1)
                    mm.then_inc(g_used, 1)
                router(4, wr1h, wr1l, RD1)
                pe.wait_ge(ff_dve, b * 8 + 4)
                for t in range(TT):
                    tr = pe.transpose(ps[0:RD1, 5, t * P:(t + 1) * P], q16[:, t, :], ident[:, :])
                tr.then_inc(ff_pe, 1)
                pe.wait_ge(ff_dve, b * 8 + 5)
                for t in range(TT):
                    mm = pe.matmul(ps[:, 6, t * E1:(t + 1) * E1], q16T[:, t * P:(t + 1) * P], keys_sb[:, :], start=True, stop=True)
                mm.then_inc(ff_pe, 1)
                pe.wait_ge(ff_act, b * 4 + 3)
                pe.wait_ge(ff_dve, b * 8 + 7)
                for k in range(ZB):
                    for t in range(TT):
                        tr = pe.transpose(ps[:, k, t * P:(t + 1) * P], gwide1[:, t, k * P:(k + 1) * P], ident[:, :])
                tr.then_inc(ff_pe, 1)
                pe.wait_ge(ff_dve, b * 8 + 8)
                gemm(G_BW, 0, A_BW, [(split_act(X_BW + c), ring_bank) for c in range(ZB)])

        @block.scalar
        def _(sc):
            def hi(o, i, scale=1.0):
                return sc.activation(o, i, ACT.Copy, scale=scale)

            sc.sem_inc(e_done, 2)
            sc.sem_inc(rb_done, 1)
            sc.wait_ge(const_dma, 16 * 4)
            hi(wr0h[:, :, :], wr0_raw[:, :, :]).then_inc(const_hi, 1)
            hi(wr1h[:, :, :], wr1_raw[:, :, :]).then_inc(const_hi, 1)

            with sc.Fori(0, B) as b:
                def g_split(w, extra=0, slots=0):
                    sc.wait_ge(g_landed[w % 2], b * (NG * 8) + slots + (w // 2 + 1) * 16)
                    sc.wait_ge(g_used, G(b, w - 2) + extra)
                    n = cols_of(w)
                    hi(gh[:, w % 2, 0:n], graw[:, w % 2, 0:n]).then_inc(g_hi, 1)

                def q_split(u):
                    sc.wait_ge(q_landed, u * 16 + 16)
                    sc.wait_ge(qt_done, u + 1)
                    hi(qwh[:, :, :], qraw[:, :, :]).then_inc(q_hi, 1)

                def a_split(c, w, extra=0):
                    sc.wait_ge(g_used, G(b, w - 2) + extra)
                    hi(ah[:, c % 2, :], act[:, c, :]).then_inc(a_hi, 1)

                def evac(k, o, phase, w_last):
                    wait_bank(sc, b, phase, k, w_last)
                    hi(o, ps[:, k, :]).then_inc(ev_hi, 1)

                def xt_split(p):
                    for c in range(DC):
                        sc.wait_ge(xt_ready, b * (4 * DC) + (p * DC + c + 1))
                        hi(xh[:, c, :], ps[:, c, :], lnw_sb[:, c:c + 1] if p == 0 else 1.0).then_inc(xt_hi, 1)

                for c in range(DC):
                    sc.wait_ge(ctx_landed[c % 2], b * (DC * 8) + (c // 2 + 1) * 16)
                    hi(ch[:, c, :], craw[:, c % 2, :]).then_inc(ctx_hi, 1)
                    g_split(G_KV0 + c)
                g_split(G_K1)
                for k in range(8):
                    evac(k, stage(ST_K0 + k)[0] if k < 4 else v0h[:, 2 * k - 8:2 * k - 6, :].rearrange("p a n -> p (a n)"), 0, G_K1 - 1)
                    if k == 3:
                        g_split(G_K1 + 1)
                for c in range(2, DC):
                    g_split(G_K1 + c)
                g_split(G_V1)
                for k in range(8):
                    wait_slot(sc, b, ST_K1 + k)
                    evac(k, stage(ST_K1 + k)[0], 1, G_V1 - 1)
                    if k == 3:
                        g_split(G_V1 + 1)
                for c in range(2, DC):
                    g_split(G_V1 + c)
                g_split(G_Q0)
                for k in range(8):
                    wait_slot(sc, b, ST_V1 + k)
                    evac(k, stage(ST_V1 + k)[0], 2, G_Q0 - 1)
                    if k == 3:
                        g_split(G_Q0 + 1)
                for i in range(ST_K1, ST_V1):
                    sc.wait_ge(*stored(b, i))
                xt_split(0)
                for i in range(ST_KV1 - 2, ST_KV1):
                    sc.wait_ge(*stored(b, i))
                for g in range(KV0):
                    sc.wait_ge(g_used, G(b, G_Q0 + g))
                    hi(qh[:, g, :], ps[:, g, :], SCALE0).then_inc(ev_hi, 1)
                    g_split(G_Q0 + g + 2)

                def q_evac(h, j, o, scale):
                    sc.wait_ge(qt_done, head1(b, h, j) + 2)
                    hi(o, ps[:, q_bank(j), :], scale).then_inc(qt_hi, 1)

                def exp0(g, par, j, t):
                    a = tile0(b, g, j, t)
                    sc.wait_ge(mx_done, a + 1)
                    sc.activation(e0[:, (j % 2) * TT + t, :], ps[:, 2 * (t % 2):2 * (t % 2) + 2, :].rearrange("p a n -> p (a n)"),
                                  ACT.Exp, bias=nmax[:, j % 2, t:t + 1], accum_out=rs[:, par, t, j:j + 1]).then_inc(e_done, 1)

                def p_split(n, bank, o, slot, slots):
                    sc.wait_ge(t_ready, n + 1)
                    sc.wait_ge(p_used, n + (1 + NUSED - slots))
                    hi(o[:, slot, :], ps[:, bank, :]).then_inc(p_hi, 1)

                def p_split0(g, j, c):
                    p_split(chunk0(b, g, j, c), TB0[place0(j, c) % NPT], ph0, c % PT0, PT0)

                def copy_rb(u, o, bank):
                    sc.wait_ge(rb_ready, u + 1)
                    sc.wait_ge(act_done, u + 1)
                    sc.copy(o, ps[:, bank, :]).then_inc(rb_done, 1)

                def group0(g, par, more):
                    for j in range(R0):
                        for t in range(TT):
                            if j == R0 - 1 and t == 2:
                                copy_rb(unit0(b, g), rb0[:, :], RB0)
                            p_split0(g, j, 2 * t)
                            p_split0(g, j, 2 * t + 1)
                            if not more and j == R0 - 1 and t < 2:
                                a_split(t, G_WO0 + t)
                            if j < R0 - 1:
                                exp0(g, par, j + 1, t)
                            elif more:
                                exp0(g + 1, 1 - par, 0, t)

                for t in range(TT):
                    exp0(0, 0, 0, t)
                with sc.Fori(0, KV0 // 2 - 1) as r:
                    group0(r * 2, 0, True)
                    group0(r * 2 + 1, 1, True)
                group0(KV0 - 2, 0, True)
                group0(KV0 - 1, 1, False)

                for c in range(2, DC):
                    g_split(G_WO0 + c)
                    sc.wait_ge(act_done, unit0(b, c) + 2)
                    a_split(c, G_WO0 + c)
                g_split(G_A0)

                g_split(G_BASE)
                xt_split(1)
                sc.wait_ge(g_used, G(b, G_A0))
                sc.copy(act[:, 1, :], ps[:, 0, :]).then_inc(ff_act, 1)
                sc.wait_ge(ff_dve, b * NFD + 1)
                sc.activation(ex0[:, :, :], comb[:, :, :], ACT.Exp).then_inc(ff_act, 1)
                for c in range(1, DC):
                    g_split(G_BASE + c)
                g_split(G_B0)
                sc.wait_ge(ff_dve, b * NFD + 3)
                a_split(0, G_B0)

                g_split(G_KV1)
                g_split(G_KV1 + 1)
                xt_split(2)
                for c in range(2, DC):
                    g_split(G_KV1 + c)
                for k in range(8):
                    wait_slot(sc, b, ST_KV1 + k)
                    evac(k, stage(ST_KV1 + k)[0], 5, G_WO1 - 1)
                with sc.Fori(0, KV1) as h:
                    def exp1(j, t):
                        sc.wait_ge(mx_done, tile1(b, h, j, t) + 1)
                        k = s_bank(j, t)
                        sc.activation(e1[:, (j % 2) * TT + t, :], ps[:, k:k + 3, :].rearrange("p a n -> p (a n)"),
                                      ACT.Exp, bias=nmax[:, j % 2, t:t + 1], accum_out=rs[:, j % 2, t, 0:1]).then_inc(e_done, 1)

                    def p_split1(j, c):
                        p_split(chunk1(b, h, j, c), TB1[c % NPT], ph1, c % PT1, PT1)

                    q_split(head1(b, h, 0))
                    q_evac(h, 0, q1h[:, 0, :], SCALE1)
                    q_split(head1(b, h, 1))
                    for t in range(TT):
                        exp1(0, t)
                    q_evac(h, 1, q1h[:, 1, :], SCALE1)
                    q_split(head1(b, h, 2))
                    for j in range(R1):
                        for t in range(TT):
                            for i in range(3):
                                if i == 2 and j < R1 - 1:
                                    exp1(j + 1, t)
                                p_split1(j, 3 * t + i)
                                if t == 3 and i == 0 and j < R1 - 3:
                                    q_split(head1(b, h, j + 3))
                            if t == 2 and j < R1 - 2:
                                q_evac(h, j + 2, q1h[:, j % 2, :], SCALE1)
                            if t == TT - 1:
                                copy_rb(unit1(b, h, j), rb1[:, :], QB)
                            if j == R1 - 1 and t < 2:
                                g_split(G_WO1 + t, h * DC, h * (DC * 8))
                                sc.wait_ge(*stored(b, ST_KV1 + 4 + t))
                                sc.wait_ge(act_done, unit1(b, h, t) + 2)
                                a_split(t, G_WO1 + t, h * DC)
                    for c in range(2, R1):
                        g_split(G_WO1 + c, h * DC, h * (DC * 8))
                        sc.wait_ge(act_done, unit1(b, h, c) + 2)
                        a_split(c, G_WO1 + c, h * DC)

                g_split(G_Z)
                g_split(G_Z + 1)
                xt_split(3)
                for c in range(2, DC):
                    g_split(G_Z + c)
                g_split(G_BW)
                sc.wait_ge(g_used, G(b, G_BW - 1))
                for k in range(ZB):
                    cp = sc.copy(act[:, ZB + k, :], ps[:, k, :])
                cp.then_inc(ff_act, 1)
                g_split(G_BW + 1)
                sc.wait_ge(ff_dve, b * NFD + 6)
                sc.activation(ex1[:, :, :], sc3[:, :, :], ACT.Exp).then_inc(ff_act, 1)
                sc.wait_ge(ff_dve, b * NFD + 8)
                for c in range(ZB):
                    if c >= 2:
                        g_split(G_BW + c)
                    a_split(c, G_BW + c)

        @block.gpsimd
        def _(po):
            po.sem_inc(g_lo, 2)
            po.sem_inc(q_lo, 1)
            po.memset(neghalf[:, :], -0.5).then_inc(pool_c, 1)
            po.memset(ident[:, :], 0.0).then_inc(pool_c, 1)
            po.wait_ge(pool_c, 2)
            po.affine_select(out=ident[:, :], in_=ident[:, :], compare_op=ALU.not_equal, fill=1.0, base=0,
                             pattern=[[-1, P]], channel_multiplier=1).then_inc(const_ready, 1)

            with po.Fori(0, B) as b:
                def lo(o, i, h):
                    return po.tensor_tensor(o, i, h.bitcast(F32), ALU.subtract)

                def g_split(w, extra=0):
                    po.wait_ge(g_hi, b * NG + extra + (w + 1))
                    n = cols_of(w)
                    s = w % 2
                    lo(gl[:, s, 0:n], graw[:, s, 0:n], gh[:, s, 0:n]).then_inc(g_lo, 1)

                def q_split(u):
                    po.wait_ge(q_hi, u + 1)
                    lo(qwl[:, :, :], qraw[:, :, :], qwh[:, :, :]).then_inc(q_lo, 1)

                def inv_root(i):
                    po.wait_ge(ln_dve, b * NLN + (i + 1))
                    po.tensor_tensor(rstd[:, :], ve[:, :], neghalf[:, :], ALU.pow).then_inc(ln_pool, 1)

                for c in range(DC):
                    po.wait_ge(ctx_hi, b * DC + (c + 1))
                    lo(cl[:, c, :], craw[:, c % 2, :], ch[:, c, :]).then_inc(ctx_lo, 1)
                    g_split(G_KV0 + c)
                    if c in (3, 5):
                        inv_root((c - 3) // 2)
                for w in range(G_K1, G_WO0 + 2):
                    g_split(w)

                def widen(g, par):
                    po.wait_ge(rinv_done, unit0(b, g) + 1)
                    po.wait_ge(rb_done, unit0(b, g) + 1)
                    po.sem_inc(pool_steps, 1)
                    po.tensor_copy(rwide[:, :, :].rearrange("p t (j d) -> p (t j) d", d=HD0),
                                   rinv[:, par].rearrange("p t j -> p (t j)").unsqueeze(2).to_broadcast([P, TT * R0, HD0])).then_inc(rwide_done, 1)

                with po.Fori(0, KV0 // 2) as r:
                    for par in range(2):
                        widen(r * 2 + par, par)
                for c in range(2, DC):
                    g_split(G_WO0 + c)
                g_split(G_A0)
                inv_root(2)
                po.wait_ge(xn_ready, b * (4 * TT) + 2 * TT)
                po.wait_ge(bias_landed, b * 16 + 16)
                for t in range(TT):
                    add = po.tensor_tensor(x[:, t, :], x[:, t, :], bias_sb[:, :], ALU.add)
                add.then_inc(bias_added, 1)
                for c in range(DC):
                    g_split(G_BASE + c)
                g_split(G_B0)
                g_split(G_KV1)
                g_split(G_KV1 + 1)
                inv_root(3)
                for c in range(2, DC):
                    g_split(G_KV1 + c)
                with po.Fori(0, KV1) as h:
                    for j in range(R1):
                        q_split(head1(b, h, j))
                    for c in range(R1):
                        g_split(G_WO1 + c, h * DC)
                g_split(G_Z)
                g_split(G_Z + 1)
                inv_root(4)
                for w in range(G_Z + 2, NG):
                    g_split(w)

        @block.vector
        def _(v):
            v.sem_inc(p_lo, NPT)
            v.sem_inc(acc_evac, 1)
            v.sem_inc(act_done, 1)
            v.sem_inc(qt_lo, 1)
            for i in range(8 - TOP0):
                v.memset(pv[:, :, E0 + i:E0 + i + 1], -1.0 - i)
                pad = v.memset(rp[:, :, TOP0 + i:TOP0 + i + 1], -1.0 - i)
            pad.then_inc(dve_c, 1)
            v.wait_ge(dve_c, 1)
            v.wait_ge(const_hi, 2)
            v.tensor_tensor(wr0l[:, :, :], wr0_raw[:, :, :], wr0h[:, :, :].bitcast(F32), ALU.subtract).then_inc(const_ready, 1)
            v.tensor_tensor(wr1l[:, :, :], wr1_raw[:, :, :], wr1h[:, :, :].bitcast(F32), ALU.subtract).then_inc(const_ready, 1)

            with v.Fori(0, B) as b:
                links = [0]

                def link(ins):
                    links[0] += 1
                    ins.then_inc(dv, 1)
                    v.wait_ge(dv, b * NDV + links[0])
                    v.sem_inc(dve_steps, 1)

                def lo(o, i, h):
                    return v.tensor_tensor(o, i, h.bitcast(F32), ALU.subtract)

                def scaled_lo(o, i, scale, h):
                    return v.scalar_tensor_tensor(out=o, in0=i, scalar=scale, in1=h.bitcast(F32), op0=ALU.mult, op1=ALU.subtract)

                def row_stats(src):
                    for t in range(TT):
                        for i in range(2):
                            st = v.bn_stats(stats[:, t, 6 * i:6 * i + 6], src[:, t, 512 * i:512 * i + 512])
                    link(st)
                    for t in range(TT):
                        ag = v.bn_aggr(mv[:, t, :], stats[:, t, :])
                    link(ag)

                def norm(p):
                    row_stats(x)
                    v.tensor_scalar(ve[:, :], mv[:, :, 1], EPS, None, ALU.add).then_inc(ln_dve, 1)
                    v.wait_ge(ln_pool, b * NLN + (1 if p == 0 else p + 2))
                    for t in range(TT):
                        nm = v.tensor_scalar(xn[:, t, :], x[:, t, :], mv[:, t, 0:1], rstd[:, t:t + 1], ALU.subtract, ALU.mult)
                        if p > 0:
                            nm.then_inc(xn_ready, 1)
                    if p > 0:
                        return
                    link(nm)
                    row_stats(xn)
                    link(v.tensor_tensor(ve[:, :], mv[:, :, 0], mv[:, :, 0], ALU.mult))
                    link(v.tensor_tensor(ve[:, :], ve[:, :], mv[:, :, 1], ALU.add))
                    v.tensor_scalar(ve[:, :], ve[:, :], EPS, None, ALU.add).then_inc(ln_dve, 1)
                    v.wait_ge(ln_pool, b * NLN + 2)
                    for t in range(TT):
                        v.tensor_scalar(xn[:, t, :], xn[:, t, :], rstd[:, t:t + 1], None, ALU.mult).then_inc(xn_ready, 1)

                def xt_split(p):
                    for c in range(DC):
                        v.wait_ge(xt_hi, b * (4 * DC) + (p * DC + c + 1))
                        if p == 0:
                            ins = scaled_lo(xl[:, c, :], ps[:, c, :], lnw_sb[:, c:c + 1], xh[:, c, :])
                        else:
                            ins = lo(xl[:, c, :], ps[:, c, :], xh[:, c, :])
                        ins.then_inc(xt_lo, 1)

                def evac(k, i, o, h):
                    v.wait_ge(ev_hi, b * NEV + (i + 1))
                    lo(o, ps[:, k, :], h).then_inc(acc_evac, 1)

                def add_banks(phase, w_last, ph_extra=0, w_extra=0):
                    for k in range(8):
                        wait_bank(v, b, phase, k, w_last, ph_extra, w_extra)
                        xs = x[:, k // 2, (k % 2) * 512:(k % 2 + 1) * 512]
                        v.tensor_tensor(xs, ps[:, k, :], xs, ALU.add).then_inc(acc_evac, 1)

                def added(n):
                    v.wait_ge(acc_evac, b * NACC + (n + 1))

                def a_split(c, i, extra=0):
                    v.wait_ge(a_hi, b * NA + extra + (i + 1))
                    lo(al[:, c % 2, :], act[:, c, :], ah[:, c % 2, :]).then_inc(a_lo, 1)

                v.wait_ge(x_landed, b * 16 + 16)
                norm(0)
                for k in range(8):
                    if k < 4:
                        evac(k, k, *reversed(stage(ST_K0 + k)))
                    else:
                        w = slice(2 * k - 8, 2 * k - 6)
                        evac(k, k, v0l[:, w, :].rearrange("p a n -> p (a n)"), v0h[:, w, :].rearrange("p a n -> p (a n)"))
                for i in range(8, 24):
                    evac(i % 8, i, *reversed(stage(ST_K1 + i - 8)))
                xt_split(0)
                for g in range(KV0):
                    v.wait_ge(ev_hi, b * NEV + (A_Q0 + g + 1))
                    scaled_lo(ql[:, g, :], ps[:, g, :], SCALE0, qh[:, g, :]).then_inc(acc_evac, 1)

                v.memset(vph[:, :, :].bitcast(F32), 0.0)
                link(v.memset(vpl[:, :, :].bitcast(F32), 0.0))

                def lay_values(g):
                    v.wait_ge(p_used, chunk0(b, g, 0, 0) + NUSED)
                    o = slice(P - HD0, P)
                    v.tensor_copy(vph[:, :, o], v0h[:, :, ds(g * HD0, HD0)].bitcast(F32))
                    v.tensor_copy(vpl[:, :, o], v0l[:, :, ds(g * HD0, HD0)].bitcast(F32)).then_inc(vp_ready, 1)

                def q_evac(i, j, o, scale, h):
                    v.wait_ge(qt_hi, i + 1)
                    scaled_lo(o, ps[:, q_bank(j), :], scale, h).then_inc(qt_lo, 1)

                def max0(g, j, t):
                    v.wait_ge(s_ready, tile0(b, g, j, t) + 1)
                    v.tensor_reduce(nmax[:, j % 2, t:t + 1], ps[:, 2 * (t % 2):2 * (t % 2) + 2, :].rearrange("p a n -> p (a n)"),
                                    X, ALU.max, negate=True).then_inc(mx_done, 1)

                def p_split(n, bank, o, h, slot):
                    v.wait_ge(p_hi, n + 1)
                    lo(o[:, slot, :], ps[:, bank, :], h[:, slot, :]).then_inc(p_lo, 1)

                def invert(u, o, i, exps):
                    v.wait_ge(e_done, exps)
                    v.reciprocal(o, i).then_inc(rinv_done, 1)

                def scale_out(u, o, rb, n):
                    v.wait_ge(p_used, n + (1 + NUSED))
                    v.wait_ge(rb_done, u + 2)
                    v.tensor_tensor(o, ps[:, PVB, :], rb, ALU.mult).then_inc(act_done, 1)

                def step0(g, par, j, t, more):
                    if j < R0 - 1:
                        max0(g, j + 1, t)
                    elif more:
                        max0(g + 1, 0, t)
                    if j == R0 - 1 and t == 0:
                        invert(unit0(b, g), rinv[:, par], rs[:, par], tile0(b, g, R0 - 1, TT - 1) + 3)
                    for c in (2 * t, 2 * t + 1):
                        p_split(chunk0(b, g, j, c), TB0[place0(j, c) % NPT], pl0, ph0, c % PT0)
                    if not more and j == R0 - 1 and t < 2:
                        a_split(t, X_WO0 + t)

                def group0(g, par, more):
                    for j in range(R0):
                        for t in range(TT):
                            if j > 0 or t > 0:
                                step0(g, par, j, t, more)
                    if more:
                        step0(g + 1, 1 - par, 0, 0, True)
                    scale_out(unit0(b, g), act[:, ds(g, 1), :].rearrange("p a n -> p (a n)"), rb0[:, :], chunk0(b, g, R0 - 1, C0 - 1))
                    if more:
                        lay_values(g + 1)

                lay_values(0)
                for t in range(TT):
                    max0(0, 0, t)
                step0(0, 0, 0, 0, True)
                with v.Fori(0, KV0 // 2 - 1) as r:
                    group0(r * 2, 0, True)
                    group0(r * 2 + 1, 1, True)
                group0(KV0 - 2, 0, True)
                group0(KV0 - 1, 1, False)

                for c in range(2, DC):
                    a_split(c, X_WO0 + c)
                add_banks(3, G_WO0 + 7)
                added(A_WO0 + 8)

                norm(1)
                xt_split(1)
                v.wait_ge(ff_pe, b * NFP + 1)
                link(v.tensor_copy(comb[:, :, :], ps[:, 1, 0:TT * E0].rearrange("p (t e) -> p t e", t=TT)))
                link(v.tensor_reduce(t4[:, 0, :], comb[:, :, :], X, ALU.max))
                v.tensor_tensor(comb[:, :, :], comb[:, :, :], t4[:, 0, :].unsqueeze(2).to_broadcast([P, TT, E0]), ALU.subtract).then_inc(ff_dve, 1)
                v.wait_ge(ff_act, b * NFA + 2)
                link(v.tensor_reduce(t4[:, 1, :], ex0[:, :, :], X, ALU.add))
                link(v.reciprocal(t4[:, 2, :], t4[:, 1, :]))
                link(v.tensor_tensor(pv[:, :, 0:E0], ex0[:, :, :], t4[:, 2, :].unsqueeze(2).to_broadcast([P, TT, E0]), ALU.mult))
                for t in range(TT):
                    ins = v.max(m8[:, t, :], pv[:, t, 0:E0])
                link(ins)
                v.tensor_tensor(t4[:, 3, :], m8[:, :, 0], m8[:, :, 1], ALU.add)
                link(v.tensor_copy(rp[:, :, 0:TOP0], m8[:, :, 0:TOP0]))
                for t in range(TT):
                    ins = v.match_replace(mr[:, t, :], rp[:, t, :], pv[:, t, :], -9.0)
                link(ins)
                v.reciprocal(t4[:, 0, :], t4[:, 3, :])
                link(v.tensor_tensor(ex0[:, :, :], mr[:, :, 0:E0], pv[:, :, 0:E0], ALU.not_equal))
                link(v.tensor_tensor(comb[:, :, :], ex0[:, :, :], pv[:, :, 0:E0], ALU.mult))
                link(v.scalar_tensor_tensor(out=comb[:, :, :], in0=comb[:, :, :], scalar=GAIN0, in1=t4[:, 0, :].unsqueeze(2).to_broadcast([P, TT, E0]),
                                            op0=ALU.mult, op1=ALU.mult))
                v.tensor_copy(gwide0[:, :, :].rearrange("p t (e r) -> p (t e) r", r=RK0),
                              comb[:, :, :].rearrange("p t e -> p (t e)").unsqueeze(2).to_broadcast([P, TT * E0, RK0])).then_inc(ff_dve, 1)
                v.wait_ge(ff_pe, b * NFP + 2)
                v.wait_ge(ff_act, b * NFA + 1)
                v.tensor_tensor(act[:, 0, :], ps[:, 2, :], act[:, 1, :], ALU.mult).then_inc(ff_dve, 1)
                a_split(0, X_B0)
                v.wait_ge(bias_added, b + 1)
                add_banks(4, G_B0)
                added(A_BASE + 8)

                norm(2)
                xt_split(2)
                for k in range(8):
                    evac(k, 32 + k, *reversed(stage(ST_KV1 + k)))

                with v.Fori(0, KV1) as h:
                    def max1(j, t):
                        v.wait_ge(s_ready, tile1(b, h, j, t) + 1)
                        v.tensor_reduce(nmax[:, j % 2, t:t + 1], ps[:, s_bank(j, t):s_bank(j, t) + 3, :].rearrange("p a n -> p (a n)"), X, ALU.max,
                                        negate=True).then_inc(mx_done, 1)

                    q_evac(head1(b, h, 0), 0, q1l[:, 0, :], SCALE1, q1h[:, 0, :])
                    for t in range(TT):
                        max1(0, t)
                    q_evac(head1(b, h, 1), 1, q1l[:, 1, :], SCALE1, q1h[:, 1, :])
                    for j in range(R1):
                        u = unit1(b, h, j)
                        for t in range(TT):
                            if j < R1 - 1:
                                max1(j + 1, t)
                            if t == 0:
                                invert(u, rinv[:, j % 2, :, 0], rs[:, j % 2, :, 0], tile1(b, h, j, TT - 1) + 3)
                            for i in range(3):
                                p_split(chunk1(b, h, j, 3 * t + i), TB1[i % NPT], pl1, ph1, i % PT1)
                                if t == 0 and i == 0 and j > 0:
                                    scale_out(u - 1, act[:, j - 1, :], rb1[:, :], chunk1(b, h, j - 1, C1 - 1))
                            if j == R1 - 1 and t < 2:
                                a_split(t, X_WO1 + t, h * R1)
                            if t == 2 and j < R1 - 2:
                                q_evac(head1(b, h, j) + 2, j + 2, q1l[:, j % 2, :], SCALE1, q1h[:, j % 2, :])
                    scale_out(unit1(b, h, R1 - 1), act[:, R1 - 1, :], rb1[:, :], chunk1(b, h, R1 - 1, C1 - 1))
                    for c in range(2, R1):
                        a_split(c, X_WO1 + c, h * R1)
                    add_banks(6, G_WO1 + 7, h * 7, h * DC)

                added(A_WO1 + 8 * KV1)
                norm(3)
                xt_split(3)
                v.wait_ge(ff_pe, b * NFP + 3)
                v.tensor_copy(q16[:, :, :], ps[:, 4, 0:TT * RD1].rearrange("p (t e) -> p t e", t=TT)).then_inc(ff_dve, 1)
                v.wait_ge(ff_pe, b * NFP + 4)
                v.tensor_copy(q16T[:, :], ps[0:RD1, 5, :]).then_inc(ff_dve, 1)
                v.wait_ge(ff_pe, b * NFP + 5)
                link(v.tensor_copy(sc1[:, :, :], ps[:, 6, 0:TT * E1].rearrange("p (t e) -> p t e", t=TT)))
                for t in range(TT):
                    ins = v.max(m16[:, t, 0:8], sc1[:, t, :])
                link(ins)
                for t in range(TT):
                    ins = v.match_replace(sc2[:, t, :], m16[:, t, 0:8], sc1[:, t, :], LOWEST)
                link(ins)
                for t in range(TT):
                    ins = v.max(m16[:, t, 8:16], sc2[:, t, :])
                link(ins)
                for t in range(TT):
                    ins = v.match_replace(sc3[:, t, :], m16[:, t, 8:16], sc2[:, t, :], LOWEST)
                link(ins)
                link(v.tensor_tensor(sc2[:, :, :], sc3[:, :, :], sc1[:, :, :], ALU.not_equal))
                v.tensor_tensor(sc3[:, :, :], sc1[:, :, :], m16[:, :, 0:1].to_broadcast([P, TT, E1]), ALU.subtract).then_inc(ff_dve, 1)
                v.wait_ge(ff_act, b * NFA + 4)
                link(v.tensor_tensor(sc1[:, :, :], ex1[:, :, :], sc2[:, :, :], ALU.mult))
                link(v.tensor_reduce(t4[:, 0, :], sc1[:, :, :], X, ALU.add))
                link(v.reciprocal(t4[:, 1, :], t4[:, 0, :]))
                link(v.scalar_tensor_tensor(out=sc1[:, :, :], in0=sc1[:, :, :], scalar=GAIN1, in1=t4[:, 1, :].unsqueeze(2).to_broadcast([P, TT, E1]),
                                            op0=ALU.mult, op1=ALU.mult))
                v.tensor_copy(gwide1[:, :, :].rearrange("p t (e r) -> p (t e) r", r=RK1),
                              sc1[:, :, :].rearrange("p t e -> p (t e)").unsqueeze(2).to_broadcast([P, TT * E1, RK1])).then_inc(ff_dve, 1)
                v.wait_ge(ff_pe, b * NFP + 6)
                for k in range(ZB):
                    ins = v.tensor_tensor(act[:, k, :], ps[:, k, :], act[:, ZB + k, :], ALU.mult)
                ins.then_inc(ff_dve, 1)
                for c in range(ZB):
                    a_split(c, X_BW + c)
                add_banks(10, NG - 1)
                assert links[0] == NDV, links[0]


def _layout(np, a):
    t = lambda w: np.ascontiguousarray(w.T)
    return {
        "x_in": a["x"],
        "ctxT": np.ascontiguousarray(a["ctx_4096"].transpose(0, 2, 1)),
        "w_kv0": np.concatenate([a["L0_xattn_wk"].T, a["L0_xattn_wv"].T], axis=1),
        "w_kv1": np.concatenate([a["L1_xattn_Wk"], a["L1_xattn_Wv"]], axis=1),
        "wq0": t(a["L0_xattn_wq"]),
        "wo0": t(a["L0_xattn_wo"]),
        "lnw": t(a["L0_xattn_ln_w"].reshape(DC, P)),
        "wbase": t(a["L0_ffn_W_base"]),
        "bbase": a["L0_ffn_b_base"],
        "a0": t(a["L0_ffn_A"].reshape(E0 * RK0, D)),
        "b0": np.ascontiguousarray(a["L0_ffn_B"].transpose(0, 2, 1)).reshape(E0 * RK0, D),
        "wr0": t(a["L0_ffn_W_router"]),
        "wq1": a["L1_xattn_Wq"],
        "wo1": a["L1_xattn_Wo"],
        "aw": t(a["L1_ffn_A_w"]),
        "bw": t(a["L1_ffn_B_w"]),
        "wr1": t(a["L1_ffn_Wq_w"]),
        "keysT": t(a["L1_ffn_keys"]),
    }


def kernel(**inputs):
    import numpy as _np
    import concourse.bacc as _bacc
    from concourse import mybir as _mybir
    from concourse.bass_utils import run_bass_kernel_spmd as _run

    nc = _bacc.Bacc("TRN2", target_bir_lowering=False, num_devices=1, dynamic_dma_scratch_size=1024)
    arrays, args = {}, []
    for name, a in _layout(_np, {k: _np.asarray(v) for k, v in inputs.items()}).items():
        a = _np.ascontiguousarray(a)
        arrays[f"in_{name}_dram"] = a
        args.append(nc.dram_tensor(f"in_{name}_dram", a.shape, _mybir.dt.from_np(a.dtype), kind="ExternalInput").ap())
    args.append(nc.dram_tensor("out_0_dram", (B, T, D), _mybir.dt.float32, kind="ExternalOutput").ap())
    block_program(nc, *args)
    r = _run(nc, [arrays], core_ids=[0])
    return r.results[0]["out_0_dram"]
```

```python
from contextlib import ExitStack

import concourse.bass as bass
from concourse import mybir

F32 = mybir.dt.float32
F32R = mybir.dt.float32r
ALU = mybir.AluOpType
ACT = mybir.ActivationFunctionType
X = mybir.AxisListType.X
ds = bass.ds

P = 128
B, T, D = 2, 512, 1024
S = 1024
DC = D // P
TT = T // P
H0, KV0, HD0 = 32, 8, 32
R0 = H0 // KV0
H1, KV1, HD1 = 32, 4, 128
R1 = H1 // KV1
S1 = S + T
C0, C1 = S // P, S1 // P
E0, RK0, TOP0, ALPHA0 = 8, 16, 2, 32
E1, RK1, TOP1, ALPHA1 = 64, 8, 16, 32
RD1 = 16
RC0 = 32
N1 = E1 * RK1
ZB = N1 // P
SCALE0 = 1.0 / float(HD0) ** 0.5
SCALE1 = 1.0 / float(HD1) ** 0.5
GAIN0 = ALPHA0 / RK0
GAIN1 = ALPHA1 / TOP1
EPS = 1e-5
LOWEST = -3.0e38

def cols_of(w):
    narrow = w < G_Q0 or G_K1 <= w < G_A0 or G_V1 <= w < G_KV1 or G_Z <= w < G_BW
    return 512 if narrow else D


G_KV0, G_Q0, G_WO0, G_K1, G_A0, G_BASE, G_B0, G_V1 = 0, 8, 16, 24, 32, 33, 41, 42
G_KV1, G_WO1, G_Z, G_BW = 50, 58, 90, 98
NG = 102
NU = KV0 + H1
NTILE = 2 * H0 * TT
NCH0, NCH1 = H0 * C0, H1 * C1
NCHUNK = NCH0 + NCH1
A_KV0, A_Q0, A_WO0, A_K1, A_BASE, A_V1, A_KV1, A_WO1, A_BW = 0, 8, 16, 24, 32, 40, 48, 56, 88
F_KV0, F_WO0, F_K1, F_BASE, F_V1, F_KV1, F_WO1, F_BW = 0, 1, 2, 3, 4, 5, 6, 10
V_KV0, V_Q0, V_K1, V_V1, V_KV1 = 0, 8, 16, 24, 32
NACC = 96
X_WO0, X_B0, X_WO1, X_BW = 0, 8, 9, 41
NA = 45
NDONE = 7 * 11
NEV = 40
SLOT_S, SLOT_C, SLOT_E, SLOT_V, SLOT_A, SLOT_F, NSLOT = 0, 2, 4, 6, 8, 12, 16
STAGE = ([SLOT_C, SLOT_C + 1, SLOT_E, SLOT_E + 1]
         + [SLOT_S, SLOT_S + 1, SLOT_E, SLOT_E + 1, SLOT_V, SLOT_V + 1, SLOT_C, SLOT_C + 1] * 2
         + [SLOT_A + i for i in range(4)] + [SLOT_F + i for i in range(4)])
NST = len(STAGE)
ST_K0, ST_K1, ST_V1, ST_KV1 = 0, 4, 12, 20
PT0, PT1 = 4, 3
NPT = 3
NUSED = 4
KVL = 8 * 16
LAG0, LAG1 = 3, 2
NDV = 35


def block_program(nc, x_in, ctxT, w_kv0, w_kv1, wq0, wo0, lnw, wbase, bbase, a0, b0, wr0,
                  wq1, wo1, aw, bw, wr1, keysT, out):
    ctx = ExitStack()
    with ctx:
        def sb(name, shape, dt, stack=ctx):
            return stack.enter_context(nc.sbuf_tensor(name, shape, dt))

        def sem(name):
            return ctx.enter_context(nc.semaphore(name))

        k0s = nc.dram_tensor("k0s", [B, 2, KV0 * HD0, S], F32).ap()
        k1s = nc.dram_tensor("k1s", [B, 2, KV1, P, S1], F32).ap()
        v1s = nc.dram_tensor("v1s", [B, 2, C1, P, KV1 * HD1], F32).ap()

        x = sb("x", [P, TT, D], F32)
        act = sb("act", [P, DC, T], F32)
        xn = act[:, :, :].rearrange("p (t a) n -> p t (a n)", t=TT)
        graw = sb("graw", [P, 2, D], F32)
        gh = sb("gh", [P, 2, D], F32R)
        gl = sb("gl", [P, 2, D], F32R)
        qraw = sb("qraw", [P, DC, P], F32)
        qwh = sb("qwh", [P, DC, P], F32R)
        qwl = sb("qwl", [P, DC, P], F32R)
        ah = sb("ah", [P, 2, T], F32R)
        al = sb("al", [P, 2, T], F32R)
        sgh, sgl = ah, al
        ident = sb("ident", [P, P], F32)
        lnw_sb = sb("lnw_sb", [P, DC], F32)
        wr0_raw = sb("wr0_raw", [P, DC, E0], F32)
        wr1_raw = sb("wr1_raw", [P, DC, RD1], F32)
        wrh = sb("wrh", [P, DC, P], F32R)
        wrl = sb("wrl", [P, DC, P], F32R)
        keys_sb = sb("keys_sb", [RD1, E1], F32)
        neghalf = sb("neghalf", [P, TT], F32)
        stats = sb("stats", [P, TT, 12], F32)
        mv = sb("mv", [P, TT, 2], F32)
        ve = sb("ve", [P, TT], F32)
        rstd = sb("rstd", [P, TT], F32)
        nmax = sb("nmax", [P, 2, TT], F32)
        rs = sb("rs", [P, 2, TT, R0], F32)
        rinv = sb("rinv", [P, 2, TT, R0], F32)
        pv = sb("pv", [P, TT, 14], F32)
        m8 = sb("m8", [P, TT, 8], F32)
        rp = sb("rp", [P, TT, 8], F32)
        mr = sb("mr", [P, TT, 14], F32)
        ex0 = sb("ex0", [P, TT, E0], F32)
        comb = sb("comb", [P, TT, E0], F32)
        t4 = sb("t4", [P, 4, TT], F32)

        with ExitStack() as part:
            e0 = sb("e0", [P, 2 * TT, S], F32, part)
        xh = sb("xh", [P, DC, T], F32R)
        xl = sb("xl", [P, DC, T], F32R)
        with ExitStack() as part:
            v0h = sb("v0h", [P, C0, KV0 * HD0], F32R, part)
            v0l = sb("v0l", [P, C0, KV0 * HD0], F32R, part)
            with ExitStack() as inner:
                ch = sb("ch", [P, DC, S], F32R, inner)
                cl = sb("cl", [P, DC, S], F32R, inner)
                craw = sb("craw", [P, 2, S], F32, inner)
                stx = sb("stx", [P, 4, T], F32R, inner)
            with ExitStack() as inner:
                VW = 2 * P - HD0
                vph = sb("vph", [P, C0, VW], F32R, inner)
                vpl = sb("vpl", [P, C0, VW], F32R, inner)
                kp = sb("kp", [P, 2, S], F32R, inner)
                qp = sb("qp", [P, R0, T], F32R, inner)
                qh = sb("qh", [P, KV0, T], F32R, inner)
                ql = sb("ql", [P, KV0, T], F32R, inner)
                ph0 = sb("ph0", [P, PT0, T], F32R, inner)
                pl0 = sb("pl0", [P, PT0, T], F32R, inner)
                rb0 = sb("rb0", [P, T], F32, inner)
                rwide = sb("rwide", [P, TT, P], F32, inner)
        with ExitStack() as part:
            e1 = sb("e1", [P, 2 * TT, S1], F32, part)
            ph1 = sb("ph1", [P, PT1, T], F32R, part)
            pl1 = sb("pl1", [P, PT1, T], F32R, part)
            k1h = sb("k1h", [P, S1], F32R, part)
            k1l = sb("k1l", [P, S1], F32R, part)
            v1h = sb("v1h", [P, C1, P], F32R, part)
            v1l = sb("v1l", [P, C1, P], F32R, part)
            q1h = sb("q1h", [P, 2, T], F32R, part)
            q1l = sb("q1l", [P, 2, T], F32R, part)
            rb1 = sb("rb1", [P, T], F32, part)
        with ExitStack() as part:
            bias_sb = sb("bias_sb", [P, D], F32, part)
            gwide0 = sb("gwide0", [P, TT, P], F32, part)
            logT = sb("logT", [P, T], F32, part)
        with ExitStack() as part:
            sc1 = sb("sc1", [P, TT, E1], F32, part)
            sc2 = sb("sc2", [P, TT, E1], F32, part)
            sc3 = sb("sc3", [P, TT, E1], F32, part)
            ex1 = sb("ex1", [P, TT, E1], F32, part)
            m16 = sb("m16", [P, TT, 16], F32, part)
            q16T = sb("q16T", [RD1, T], F32, part)
            gwide1 = sb("gwide1", [P, TT, N1], F32, part)

        ps = ctx.enter_context(nc.psum_tensor("ps", [P, 8, 512], F32))
        TB0, TB1 = (4, 5, 7), (3, 4, 5)
        PVB, QB = 6, 7
        s_bank = lambda j, t: 3 * (t % 2) if j == 0 else 0
        q_bank = lambda j: QB if j > 0 else TB1[0]

        const_dma = sem("const_dma")
        const_hi = sem("const_hi")
        const_ready = sem("const_ready")
        bias_landed = sem("bias_landed")
        bias_added = sem("bias_added")
        x_landed = sem("x_landed")
        out_stored = sem("out_stored")
        ctx_landed = [sem(f"ctx_landed{i}") for i in range(2)]
        ctx_hi = sem("ctx_hi")
        ctx_lo = sem("ctx_lo")
        g_landed = [sem(f"g_landed{i}") for i in range(2)]
        g_hi = sem("g_hi")
        g_lo = sem("g_lo")
        g_used = sem("g_used")
        q_landed = sem("q_landed")
        q_hi = sem("q_hi")
        q_lo = sem("q_lo")
        a_hi = sem("a_hi")
        a_lo = sem("a_lo")
        acc_done = sem("acc_done")
        ev_hi = sem("ev_hi")
        acc_evac = sem("acc_evac")
        st_done = [sem(f"st_done{i}") for i in range(NSLOT)]
        ln_dve = sem("ln_dve")
        ln_pool = sem("ln_pool")
        xn_ready = sem("xn_ready")
        xt_ready = sem("xt_ready")
        xt_hi = sem("xt_hi")
        xt_lo = sem("xt_lo")
        qt_done = sem("qt_done")
        qt_hi = sem("qt_hi")
        qt_lo = sem("qt_lo")
        q_packed = [sem(f"q_packed{j}") for j in range(R0)]
        k_packed = [sem(f"k_packed{i}") for i in range(2)]
        kv_landed = sem("kv_landed")
        vp_ready = sem("vp_ready")
        s_ready = sem("s_ready")
        mx_done = sem("mx_done")
        e_done = sem("e_done")
        rinv_done = sem("rinv_done")
        rwide_done = sem("rwide_done")
        rb_ready = sem("rb_ready")
        rb_done = sem("rb_done")
        t_ready = sem("t_ready")
        p_hi = sem("p_hi")
        p_lo = sem("p_lo")
        p_used = sem("p_used")
        act_done = sem("act_done")
        ff_pe = sem("ff_pe")
        ff_act = sem("ff_act")
        ff_dve = sem("ff_dve")
        dv = sem("dv")
        sp_steps = sem("sp_steps")
        pool_steps = sem("pool_steps")
        dve_steps = sem("dve_steps")
        pool_c = sem("pool_c")
        dve_c = sem("dve_c")

        block = ctx.enter_context(nc.Block())

        def G(b, w):
            return b * NG + (w + 1 + 2)

        def tile0(b, g, j, t):
            return b * NTILE + g * (R0 * TT) + (j * TT + t)

        def tile1(b, h, j, t):
            return b * NTILE + h * (R1 * TT) + (H0 * TT + j * TT + t)

        def chunk0(b, g, j, c):
            return b * NCHUNK + g * (R0 * C0) + (j * C0 + c)

        def chunk1(b, h, j, c):
            return b * NCHUNK + h * (R1 * C1) + (NCH0 + j * C1 + c)

        def place0(j, c):
            return j * C0 + c + (1 if j == R0 - 1 and c >= 4 else 0)

        RB0 = TB0[(place0(R0 - 1, 3) + 1) % NPT]

        def unit0(b, g):
            return b * NU + g

        def unit1(b, h, j):
            return b * NU + h * R1 + (KV0 + j)

        def head1(b, h, j):
            return b * H1 + h * R1 + j

        ROUTER, ROUTED, LOW0, GATE0, ZB0, GATE1 = 0, 5, 6, 7, 1, (0, 5, 6, 7)
        NLN, NFP, NFA, NFD = 5, 6, 4, 11

        def wait_bank(eng, b, phase, k, w_last, ph_extra=0, w_extra=0):
            if k < 7:
                eng.wait_ge(acc_done, b * NDONE + ph_extra + (phase * 7 + k + 1))
            else:
                eng.wait_ge(g_used, G(b, w_last) + w_extra)

        def stored(b, i):
            slot = STAGE[i]
            return st_done[slot], b * (STAGE.count(slot) * 32) + STAGE[:i + 1].count(slot) * 32

        def wait_slot(eng, b, i):
            if STAGE[i] in STAGE[:i]:
                semaphore, count = stored(b, i)
                eng.wait_ge(semaphore, count - 32)

        def stage(i):
            slot = STAGE[i]
            if slot < SLOT_C:
                return sgh[:, slot - SLOT_S, :], sgl[:, slot - SLOT_S, :]
            if slot < SLOT_E:
                k = slot - SLOT_C
                return craw[:, k, 0:T].bitcast(F32R), craw[:, k, T:2 * T].bitcast(F32R)
            if slot < SLOT_V:
                k = 2 * (slot - SLOT_E)
                return stx[:, k, :], stx[:, k + 1, :]
            if slot < SLOT_A:
                k = 2 * (slot - SLOT_V)
                room = v0l[:, :, :].rearrange("p (s a) n -> p s (a n)", s=4)
                return room[:, k, :], room[:, k + 1, :]
            if slot >= SLOT_F:
                k = slot - SLOT_F
                return e1[:, k, 0:T].bitcast(F32R), e1[:, k, T:2 * T].bitcast(F32R)
            k = 2 * (slot - SLOT_A)
            return act[:, k, :].bitcast(F32R), act[:, k + 1, :].bitcast(F32R)

        @block.sync
        def _(sp):
            def wait(semaphore, value):
                sp.wait_ge(semaphore, value)
                sp.sem_inc(sp_steps, 1)

            sp.dma_start(lnw_sb[:, :], lnw).then_inc(const_dma, 16)
            sp.dma_start(wr0_raw[:, :, :], wr0.rearrange("(c p) e -> p c e", p=P)).then_inc(const_dma, 16)
            sp.dma_start(wr1_raw[:, :, :], wr1.rearrange("(c p) e -> p c e", p=P)).then_inc(const_dma, 16)
            sp.dma_start(keys_sb[:, :], keysT).then_inc(const_dma, 16)

            sp.sem_inc(out_stored, 16)
            with sp.Fori(0, B) as b:
                def load_g(w, src, cols=D, extra=0):
                    wait(g_lo, b * NG + extra + (w + 1))
                    sp.dma_start(graw[:, w % 2, 0:cols], src).then_inc(g_landed[w % 2], 16)

                def load_q(u, src):
                    wait(q_lo, u + 1)
                    sp.dma_start(qraw[:, :, :], src).then_inc(q_landed, 16)

                def rows(w, c, lo=0, n=D):
                    return w[c * P:(c + 1) * P, lo:lo + n]

                def wq0_tile(g):
                    return wq0.rearrange("(c p) n -> p c n", p=P)[:, :, ds(g * P, P)]

                def wq1_tile(n):
                    return wq1.rearrange("(c p) n -> p c n", p=P)[:, :, ds(n * P, P)]

                def load_ctx(pas, c):
                    if c >= 2:
                        wait(ctx_lo, b * (2 * DC) + (pas * DC + c - 1))
                    sp.dma_start(craw[:, c % 2, :], ctxT[ds(b, 1), c * P:(c + 1) * P, :].rearrange("a p s -> p (a s)")).then_inc(ctx_landed[c % 2], 16)

                for c in range(DC):
                    load_g(G_KV0 + c, rows(w_kv0, c, 0, 512), 512)
                    load_ctx(0, c)
                    if c == 1:
                        wait(out_stored, b * (TT * 16) + 16)
                        sp.dma_start(x[:, :, :], x_in[ds(b, 1)].rearrange("a (t p) d -> p (a t) d", p=P)).then_inc(x_landed, 16)

                def store(i, acc, dst_h, dst_l):
                    wait(acc_evac, b * NACC + (acc + 2))
                    high, low = stage(i)
                    sp.dma_start(dst_h, high.bitcast(F32)).then_inc(st_done[STAGE[i]], 16)
                    sp.dma_start(dst_l, low.bitcast(F32)).then_inc(st_done[STAGE[i]], 16)

                def wait_stores(first, last):
                    for slot in sorted(set(STAGE[first:last])):
                        wait(*stored(b, max(i for i in range(first, last) if STAGE[i] == slot)))

                def k0_dst(part, i):
                    return k0s[ds(b, 1), part, (i // 2) * P:(i // 2 + 1) * P, (i % 2) * T:(i % 2 + 1) * T].rearrange("a p s -> p (a s)")

                def k1_dst(part, h, s0):
                    return k1s[ds(b, 1), part, h, :, s0:s0 + T].rearrange("a p s -> p (a s)")

                def v1_dst(part, c):
                    return v1s[ds(b, 1), part, c].rearrange("a p n -> p (a n)")

                load_g(G_Q0, wq0_tile(0))
                load_g(G_Q0 + 1, wq0_tile(1))
                for i in range(4):
                    store(ST_K0 + i, A_KV0 + i, k0_dst(0, i), k0_dst(1, i))
                load_g(G_Q0 + 2, wq0_tile(2))
                load_g(G_Q0 + 3, wq0_tile(3))

                def pack_k(g, par):
                    for r in range(4):
                        sp.dma_start(kp[r * HD0:(r + 1) * HD0, par, :].bitcast(F32),
                                     k0s[ds(b, 1), r // 2, ds(g * HD0, HD0), :].rearrange("a p s -> p (a s)")).then_inc(k_packed[par], 16)

                def pack_q(g, j):
                    for r in range(4):
                        sp.dma_start(qp[r * HD0:(r + 1) * HD0, j, :].bitcast(F32),
                                     (qh, ql)[r % 2][j * HD0:(j + 1) * HD0, ds(g, 1), :].rearrange("p a n -> p (a n)").bitcast(F32)).then_inc(q_packed[j], 16)

                wait_stores(ST_K0, ST_K1)
                wait(acc_evac, b * NACC + (A_KV0 + 9))
                pack_k(0, 0)
                wait(acc_evac, b * NACC + (A_Q0 + 2))
                for j in range(R0):
                    pack_q(0, j)
                    load_g(G_Q0 + 4 + j, wq0_tile(4 + j))
                load_g(G_WO0, rows(wo0, 0))
                load_g(G_WO0 + 1, rows(wo0, 1))
                wait(acc_evac, b * NACC + (A_Q0 + 9))

                def group0(g, par, more):
                    if more:
                        wait(s_ready, tile0(b, g, 0, TT - 1) + 1)
                        pack_k(g + 1, 1 - par)
                        for j in range(R0):
                            wait(s_ready, tile0(b, g, j, TT - 1) + 1)
                            pack_q(g + 1, j)

                with sp.Fori(0, KV0 // 2 - 1) as r:
                    group0(r * 2, 0, True)
                    group0(r * 2 + 1, 1, True)
                group0(KV0 - 2, 0, True)
                load_g(G_WO0 + 2, rows(wo0, 2))
                load_g(G_WO0 + 3, rows(wo0, 3))

                wait(act_done, unit0(b, KV0 - 1) + 2)
                load_ctx(1, 0)
                load_ctx(1, 1)
                sp.dma_start(bias_sb[:, :], bbase.rearrange("(a d) -> a d", a=1).to_broadcast([P, D])).then_inc(bias_landed, 16)
                for c in range(4, DC):
                    load_g(G_WO0 + c, rows(wo0, c))
                    load_ctx(1, c - 2)
                load_ctx(1, 6)
                load_g(G_K1, rows(w_kv1, 0, 0, 512), 512)
                load_ctx(1, 7)
                for c in range(1, DC):
                    load_g(G_K1 + c, rows(w_kv1, c, 0, 512), 512)
                load_g(G_A0, a0.rearrange("(c p) n -> p c n", p=P))
                load_g(G_BASE, rows(wbase, 0))
                for i in range(8):
                    store(ST_K1 + i, A_K1 + i, k1_dst(0, i // 2, (i % 2) * T), k1_dst(1, i // 2, (i % 2) * T))
                    if i == 3:
                        load_g(G_BASE + 1, rows(wbase, 1))
                for c in range(2, DC):
                    load_g(G_BASE + c, rows(wbase, c))
                load_g(G_B0, b0)
                for c in range(DC):
                    load_g(G_V1 + c, rows(w_kv1, c, 512, 512), 512)
                def load_k1(h, lo, hi):
                    for part, dst in ((0, k1h), (1, k1l)):
                        sp.dma_start(dst[:, lo:hi].bitcast(F32), k1s[ds(b, 1), part, ds(h, 1), :, lo:hi].rearrange("a h p s -> p (a h s)")).then_inc(kv_landed, 16)

                def load_v1(h, lo, hi):
                    for part, dst in ((0, v1h), (1, v1l)):
                        sp.dma_start(dst[:, lo:hi, :].bitcast(F32), v1s[ds(b, 1), part, lo:hi, :, ds(h * HD1, HD1)].rearrange("a c p n -> p (a c) n")).then_inc(kv_landed, 16)

                load_g(G_KV1, rows(w_kv1, 0))
                load_g(G_KV1 + 1, rows(w_kv1, 1))
                for i in range(8):
                    store(ST_V1 + i, A_V1 + i, v1_dst(0, i), v1_dst(1, i))
                load_g(G_KV1 + 2, rows(w_kv1, 2))
                load_g(G_KV1 + 3, rows(w_kv1, 3))
                load_q(head1(b, 0, 0), wq1_tile(0))
                wait_stores(ST_V1, ST_KV1)
                load_k1(0, 0, S)
                load_v1(0, 0, C0)
                for c in range(4, DC):
                    load_g(G_KV1 + c, rows(w_kv1, c))
                for i in range(8):
                    if i < 4:
                        store(ST_KV1 + i, A_KV1 + i, k1_dst(0, i, S), k1_dst(1, i, S))
                    else:
                        store(ST_KV1 + i, A_KV1 + i, v1_dst(0, C0 + i - 4), v1_dst(1, C0 + i - 4))
                wait(*stored(b, ST_KV1))
                load_k1(0, S, S1)
                wait_stores(ST_KV1, NST)
                load_v1(0, C0, C1)

                def head_weights(h, more):
                    for j in range(1, R1):
                        load_q(head1(b, h, j), wq1_tile(h * R1 + j))
                    for c in range(DC):
                        if c == 4 and more:
                            load_q(head1(b, h + 1, 0), wq1_tile((h + 1) * R1))
                            wait(s_ready, tile1(b, h + 1, 0, 0))
                            load_k1(h + 1, 0, S)
                            load_k1(h + 1, S, S1)
                            wait(p_used, chunk1(b, h + 1, 0, 0) + NUSED)
                            load_v1(h + 1, 0, C0)
                            load_v1(h + 1, C0, C1)
                        load_g(G_WO1 + c, wo1[ds(h * (R1 * HD1) + c * P, P), :], extra=h * DC)

                with sp.Fori(0, KV1 - 1) as h:
                    head_weights(h, True)
                head_weights(KV1 - 1, False)
                for c in range(DC):
                    load_g(G_Z + c, rows(aw, c, 0, N1), N1)
                for c in range(ZB):
                    load_g(G_BW + c, rows(bw, c))
                for t in range(TT):
                    wait(acc_evac, b * NACC + (A_BW + 2 * t + 3))
                    sp.dma_start(out[ds(b, 1), t * P:(t + 1) * P].rearrange("a p d -> p (a d)"), x[:, t, :]).then_inc(out_stored, 16)

            sp.wait_ge(out_stored, B * (TT * 16) + 16)

        @block.tensor
        def _(pe):
            def mm3(o, wh, wl, mh, ml, start, stop, check=True):
                pe.matmul(o, wh, mh, start=start, stop=False, skip_group_check=not check)
                pe.matmul(o, wh, ml, start=False, stop=False, skip_group_check=not check)
                return pe.matmul(o, wl, mh, start=False, stop=stop, skip_group_check=not check)

            pe.sem_inc(g_used, 2)
            pe.sem_inc(p_used, NUSED)
            pe.sem_inc(qt_done, 1)
            pe.wait_ge(const_ready, 3)

            with pe.Fori(0, B) as b:
                def wait_acc(n):
                    pe.wait_ge(acc_evac, b * NACC + (n + 1))

                def gemm(w0, extra, acc, chunks, before=None):
                    n = len(chunks)
                    for c in range(n):
                        s = (w0 + c) % 2
                        for wait in chunks[c][0]:
                            wait()
                        pe.wait_ge(g_lo, G(b, w0 + c) + extra)
                        first, last = c == 0, c == n - 1
                        for k in range(8):
                            if first and before is not None:
                                before(k)
                            for o, wh, wl, mh, ml, opens, check in chunks[c][1](c, s, k):
                                mm = mm3(o, wh, wl, mh, ml, first and opens, last, check)
                            if k == 7:
                                mm.then_inc(g_used, 1)
                            elif last:
                                mm.then_inc(acc_done, 1)

                def evacuated(n, extra=0):
                    def wait(k):
                        pe.wait_ge(acc_evac, b * NACC + extra + (n + k + 2))
                    return wait

                def kv0_bank(c, s, k):
                    if k < 4:
                        w = slice((k // 2) * P, (k // 2 + 1) * P)
                        m = slice((k % 2) * T, (k % 2 + 1) * T)
                        return [(ps[:, k, :], gh[:, s, w], gl[:, s, w], ch[:, c, m], cl[:, c, m], True, True)]
                    return [(ps[:, k, i * 256:(i + 1) * 256],
                             ch[:, c, (2 * k - 8 + i) * P:(2 * k - 7 + i) * P], cl[:, c, (2 * k - 8 + i) * P:(2 * k - 7 + i) * P],
                             gh[:, s, 256:512], gl[:, s, 256:512], i == 0, False) for i in range(2)]

                def ctx_chunk(pas, c):
                    return [lambda: pe.wait_ge(ctx_lo, b * (2 * DC) + (pas * DC + c + 1))]

                wait_acc(0)
                gemm(G_KV0, 0, A_KV0, [(ctx_chunk(0, c), kv0_bank) for c in range(DC)])

                def transpose_x(p, before=None):
                    for t in range(TT):
                        pe.wait_ge(xn_ready, b * (4 * TT) + (p * TT + t + 1))
                        for c in range(DC):
                            if t == 0 and before is not None:
                                before(c)
                            tr = pe.transpose(ps[:, c, t * P:(t + 1) * P], xn[:, t, c * P:(c + 1) * P], ident[:, :])
                            if t == TT - 1:
                                tr.then_inc(xt_ready, 1)

                def split_x(p):
                    def wait(c):
                        pe.wait_ge(xt_lo, b * (4 * DC) + (p * DC + c + 1))
                    return wait

                transpose_x(0, evacuated(A_KV0))

                for g in range(KV0):
                    pe.wait_ge(g_lo, G(b, G_Q0 + g))
                    for c in range(DC):
                        if g == 0:
                            split_x(0)(c)
                        w = slice(c * P, (c + 1) * P)
                        mm = mm3(ps[:, g, :], gh[:, g % 2, w], gl[:, g % 2, w], xh[:, c, :], xl[:, c, :], c == 0, c == DC - 1)
                    mm.then_inc(g_used, 1)

                def q_project(h, j, cs):
                    if cs[0] == 0:
                        pe.wait_ge(q_lo, head1(b, h, j) + 2)
                        pe.wait_ge(qt_lo, head1(b, h, j) + 1)
                        if j >= 3:
                            pe.wait_ge(rb_done, unit1(b, h, j) - 1)
                    for c in cs:
                        mm = mm3(ps[:, q_bank(j), :], qwh[:, c, :], qwl[:, c, :], xh[:, c, :], xl[:, c, :], c == 0, c == DC - 1)
                    if cs[-1] == DC - 1:
                        mm.then_inc(qt_done, 1)

                def scores0(g, par, j, t):
                    a = tile0(b, g, j, t)
                    pe.wait_ge(e_done, a + 1)
                    for half in range(2):
                        mm = pe.matmul(ps[:, 2 * (t % 2) + half, :], qp[:, j, t * P:(t + 1) * P],
                                       kp[:, par, half * 512:(half + 1) * 512], start=True, stop=True)
                    mm.then_inc(s_ready, 1)

                def packed(n, j, par, m):
                    pe.wait_ge(q_packed[j], n * 64 + 64)
                    if j == 0:
                        pe.wait_ge(k_packed[par], m * 64 + 64)

                def transpose_p(bank, e, c, exps):
                    if c == 0:
                        pe.wait_ge(e_done, exps)
                    for t in range(TT):
                        tr = pe.transpose(ps[:, bank, t * P:(t + 1) * P], e[:, t, c * P:(c + 1) * P], ident[:, :])
                    tr.then_inc(t_ready, 1)

                def turned_free0(g, j, c):
                    last = j == R0 - 1
                    if last and c == 6:
                        pe.wait_ge(rb_done, unit0(b, g) + 2)
                    elif last and c in (4, 5):
                        pe.wait_ge(p_lo, chunk0(b, g, j, c) - 2 + (NPT + 1))
                    else:
                        pe.wait_ge(p_lo, chunk0(b, g, j, c) + 1)

                def pv0(g, j, c):
                    n = chunk0(b, g, j, c)
                    first, last = j == 0 and c == 0, j == R0 - 1 and c == C0 - 1
                    if first:
                        pe.wait_ge(vp_ready, b * KV0 + g + 1)
                        pe.wait_ge(act_done, unit0(b, g) + 1)
                    pe.wait_ge(p_lo, n + (1 + NPT))
                    w = slice(P - HD0 - j * HD0, 2 * P - HD0 - j * HD0)
                    mm3(ps[:, PVB, :], vph[:, c, w], vpl[:, c, w], ph0[:, c % PT0, :], pl0[:, c % PT0, :],
                        first, last).then_inc(p_used, 1)

                def broadcast_rinv(bank, src, ready, count, u):
                    pe.wait_ge(ready, count)
                    for t in range(TT):
                        tr = pe.transpose(ps[:, bank, t * P:(t + 1) * P], src(t), ident[:, :])
                    tr.then_inc(rb_ready, 1)

                def step0(g, par, j, t, more, m, pending):
                    if j < R0 - 1:
                        if t == 0:
                            packed(b * KV0 + g, j + 1, par, m)
                        scores0(g, par, j + 1, t)
                    elif more:
                        if t == 0:
                            packed(b * KV0 + g + 1, 0, 1 - par, m + par)
                        scores0(g + 1, 1 - par, 0, t)
                    for c in (2 * t, 2 * t + 1):
                        if c == 0 and len(pending) == LAG0:
                            pv0(*pending.pop(0))
                        turned_free0(g, j, c)
                        transpose_p(TB0[place0(j, c) % NPT], e0[:, (j % 2) * TT:(j % 2) * TT + TT, :], c, tile0(b, g, j, TT - 1) + 3)
                        pending.append((g, j, c))
                        if len(pending) > LAG0:
                            pv0(*pending.pop(0))
                    if j == R0 - 1 and t == 1:
                        pe.wait_ge(p_lo, chunk0(b, g, j, 4) - 3 + (NPT + 1))
                        broadcast_rinv(RB0, lambda i: rwide[:, i, :], rwide_done, b * KV0 + g + 1, unit0(b, g))

                def group0(g, par, more, m):
                    pending = [(g, 0, 0), (g, 0, 1)]
                    for j in range(R0):
                        for t in range(TT):
                            if j > 0 or t > 0:
                                step0(g, par, j, t, more, m, pending)
                    if more:
                        step0(g + 1, 1 - par, 0, 0, True, m + par, pending)
                        while pending[0][1] == R0 - 1:
                            pv0(*pending.pop(0))
                    else:
                        for step in pending:
                            pv0(*step)

                wait_acc(A_Q0 + 8)
                packed(b * KV0, 0, 0, b * (KV0 // 2))
                for t in range(TT):
                    scores0(0, 0, 0, t)
                step0(0, 0, 0, 0, True, b * (KV0 // 2), [])
                with pe.Fori(0, KV0 // 2 - 1) as r:
                    group0(r * 2, 0, True, b * (KV0 // 2) + r)
                    group0(r * 2 + 1, 1, True, b * (KV0 // 2) + r)
                group0(KV0 - 2, 0, True, b * (KV0 // 2) + KV0 // 2 - 1)
                group0(KV0 - 1, 1, False, b * (KV0 // 2) + KV0 // 2 - 1)

                def out_bank(sh, sl):
                    def bank(c, s, k):
                        w = slice((k // 2) * P, (k // 2 + 1) * P)
                        m = slice((k % 2) * 512, (k % 2 + 1) * 512)
                        return [(ps[:, k, :], sh(c)[:, w], sl(c)[:, w], gh[:, s, m], gl[:, s, m], True, True)]
                    return bank

                def split_act(i, extra=0):
                    return [lambda: pe.wait_ge(a_lo, b * NA + extra + (i + 1))]

                ring_bank = out_bank(lambda c: ah[:, c % 2, :], lambda c: al[:, c % 2, :])
                def output0_read(k):
                    if k == PVB:
                        pe.wait_ge(act_done, unit0(b, KV0 - 1) + 2)
                gemm(G_WO0, 0, A_WO0, [(split_act(X_WO0 + c), ring_bank) for c in range(DC)], output0_read)

                def k1_bank(c, s, k):
                    w = slice((k // 2) * P, (k // 2 + 1) * P)
                    m = slice((k % 2) * T, (k % 2 + 1) * T)
                    return [(ps[:, k, :], gh[:, s, w], gl[:, s, w], ch[:, c, m], cl[:, c, m], True, True)]

                gemm(G_K1, 0, A_K1, [(ctx_chunk(1, c), k1_bank) for c in range(DC)], evacuated(A_WO0))

                transpose_x(1, evacuated(A_K1))

                def router(p):
                    for c in range(DC):
                        split_x(p)(c)
                        mm = mm3(ps[:, ROUTER, :], wrh[:, c, :], wrl[:, c, :], xh[:, c, :], xl[:, c, :], c == 0, c == DC - 1)
                    mm.then_inc(ff_pe, 1)

                router(1)
                pe.wait_ge(g_lo, G(b, G_A0))
                wa = lambda w, c: w[:, G_A0 % 2, c * P:(c + 1) * P]
                for c in range(DC):
                    mm = mm3(ps[:, LOW0, :], wa(gh, c), wa(gl, c), xh[:, c, :], xl[:, c, :], c == 0, c == DC - 1)
                    if c == 1:
                        pe.wait_ge(ff_dve, b * NFD + 1)
                        for t in range(TT):
                            tr = pe.transpose(ps[:, ROUTED, t * P:(t + 1) * P], logT[:, t * P:(t + 1) * P], ident[:, :])
                        tr.then_inc(ff_pe, 1)
                mm.then_inc(g_used, 1)

                def banks0_read(k):
                    if k == ROUTED:
                        pe.wait_ge(ff_dve, b * NFD + 2)
                    if k == LOW0:
                        pe.wait_ge(ff_act, b * NFA + 2)
                    if k == GATE0:
                        pe.wait_ge(ff_dve, b * NFD + 3)
                        for t in range(TT):
                            tr = pe.transpose(ps[:, GATE0, t * P:(t + 1) * P], gwide0[:, t, :], ident[:, :])
                        tr.then_inc(ff_pe, 1)
                        pe.wait_ge(ff_dve, b * NFD + 4)

                x_bank = out_bank(lambda c: xh[:, c, :], lambda c: xl[:, c, :])
                low_bank = out_bank(lambda c: ah[:, 0, :], lambda c: al[:, 0, :])
                gemm(G_BASE, 0, A_BASE, [([], x_bank)] * DC + [(split_act(X_B0), low_bank)], banks0_read)

                def v1_bank(c, s, k):
                    w = slice(k * P, (k + 1) * P)
                    return [(ps[:, k, :], ch[:, c, w], cl[:, c, w], gh[:, s, 0:512], gl[:, s, 0:512], True, True)]

                gemm(G_V1, 0, A_V1, [([], v1_bank)] * DC, evacuated(A_BASE))

                transpose_x(2, evacuated(A_V1))

                def kv1_bank(c, s, k):
                    if k < 4:
                        w = slice(k * P, (k + 1) * P)
                        return [(ps[:, k, :], gh[:, s, w], gl[:, s, w], xh[:, c, :], xl[:, c, :], True, True)]
                    w = slice((k - 4) * P, (k - 3) * P)
                    return [(ps[:, k, :], xh[:, c, w], xl[:, c, w], gh[:, s, 512:], gl[:, s, 512:], True, True)]

                gemm(G_KV1, 0, A_KV1, [([], kv1_bank)] * DC, split_x(2))

                with pe.Fori(0, KV1) as h:
                    def scores1(j, t):
                        a = tile1(b, h, j, t)
                        pe.wait_ge(e_done, a + (2 if j > 0 else 1))
                        if t == 0:
                            pe.wait_ge(qt_lo, head1(b, h, j) + 2)
                        w = slice(t * P, (t + 1) * P)
                        for k in range(3):
                            m = slice(k * 512, (k + 1) * 512)
                            mm = mm3(ps[:, s_bank(j, t) + k, :], q1h[:, j % 2, w], q1l[:, j % 2, w], k1h[:, m], k1l[:, m], True, True)
                        mm.then_inc(s_ready, 1)

                    def pv1(j, c):
                        if c == 0:
                            pe.wait_ge(act_done, unit1(b, h, j) + 1)
                        pe.wait_ge(p_lo, chunk1(b, h, j, c) + (1 + NPT))
                        mm3(ps[:, PVB, :], v1h[:, c, :], v1l[:, c, :], ph1[:, c % PT1, :], pl1[:, c % PT1, :],
                            c == 0, c == C1 - 1).then_inc(p_used, 1)

                    pe.wait_ge(acc_evac, b * NACC + h * 8 + (A_WO1 - 3))
                    q_project(h, 0, list(range(DC)))
                    pe.wait_ge(kv_landed, b * (KV1 * KVL) + h * KVL + KVL)
                    pe.wait_ge(acc_evac, b * NACC + h * 8 + (A_WO1 + 1))
                    scores1(0, 0)
                    scores1(0, 1)
                    q_project(h, 1, [0, 1])
                    scores1(0, 2)
                    q_project(h, 1, [2, 3])
                    scores1(0, 3)
                    q_project(h, 1, [4, 5, 6, 7])
                    q_steps = [{3: [0, 1], 4: [2], 5: [3], 6: [4, 5], 7: [6], 8: [7]}, {c: [c - 1] for c in range(1, DC + 1)}]
                    pending = []
                    for j in range(R1):
                        for t in range(TT):
                            ahead = 2 if j == 0 and t == 0 else 0
                            for i in range(3):
                                if i == ahead and j < R1 - 1:
                                    scores1(j + 1, t)
                                c = 3 * t + i
                                pe.wait_ge(p_lo, chunk1(b, h, j, c) + 1)
                                transpose_p(TB1[c % NPT], e1[:, (j % 2) * TT:(j % 2) * TT + TT, :], c, tile1(b, h, j, TT - 1) + 3)
                                if c in q_steps[j > 0] and j < R1 - 2:
                                    q_project(h, j + 2, q_steps[j > 0][c])
                                pending.append((j, c))
                                while len(pending) > LAG1 or pending[0][0] < j:
                                    pv1(*pending.pop(0))
                            if t == 3:
                                if j < R1 - 2:
                                    pe.wait_ge(qt_lo, head1(b, h, j) + 4)
                                else:
                                    pe.wait_ge(rb_done, unit1(b, h, j) + 1)
                                broadcast_rinv(QB, lambda i: rinv[:, j % 2, i, 0:1].to_broadcast([P, P]), rinv_done, unit1(b, h, j) + 1, unit1(b, h, j))
                    for step in pending:
                        pv1(*step)

                    def output1_read(k):
                        if k == PVB:
                            pe.wait_ge(act_done, unit1(b, h, R1 - 1) + 2)
                    gemm(G_WO1, h * DC, A_WO1, [(split_act(X_WO1 + c, h * R1), ring_bank) for c in range(R1)], output1_read)

                transpose_x(3)
                router(3)
                for c in range(DC):
                    s = (G_Z + c) % 2
                    pe.wait_ge(g_lo, G(b, G_Z + c))
                    for k in range(ZB):
                        w = slice(k * P, (k + 1) * P)
                        mm = mm3(ps[:, ZB0 + k, :], gh[:, s, w], gl[:, s, w], xh[:, c, :], xl[:, c, :], c == 0, c == DC - 1)
                    mm.then_inc(g_used, 1)
                    if c == 0:
                        pe.wait_ge(ff_dve, b * NFD + 5)
                        for t in range(TT):
                            mm = pe.matmul(ps[:, ROUTED, t * E1:(t + 1) * E1], q16T[:, t * P:(t + 1) * P], keys_sb[:, :], start=True, stop=True)
                        mm.then_inc(ff_pe, 1)
                    if c == 4:
                        pe.wait_ge(ff_dve, b * NFD + 7)
                        for k in range(ZB):
                            for t in range(TT):
                                tr = pe.transpose(ps[:, GATE1[k], t * P:(t + 1) * P], gwide1[:, t, k * P:(k + 1) * P], ident[:, :])
                        tr.then_inc(ff_pe, 1)

                def banks1_read(k):
                    pe.wait_ge(ff_dve, b * NFD + (8 + (k - ZB0) if ZB0 <= k < ZB0 + ZB else 8))
                gemm(G_BW, 0, A_BW, [(split_act(X_BW + c), ring_bank) for c in range(ZB)], banks1_read)

        @block.scalar
        def _(sc):
            def hi(o, i, scale=1.0):
                return sc.activation(o, i, ACT.Copy, scale=scale)

            sc.sem_inc(e_done, 2)
            sc.sem_inc(rb_done, 1)
            sc.wait_ge(const_dma, 16 * 4)
            sc.wait_ge(dve_c, 3)
            hi(wrh[:, :, RC0:RC0 + E0], wr0_raw[:, :, :]).then_inc(const_hi, 1)
            hi(wrh[:, :, 0:RD1], wr1_raw[:, :, :]).then_inc(const_hi, 1)

            with sc.Fori(0, B) as b:
                def g_split(w, extra=0, slots=0):
                    sc.wait_ge(g_landed[w % 2], b * (NG * 8) + slots + (w // 2 + 1) * 16)
                    sc.wait_ge(g_used, G(b, w - 2) + extra)
                    n = cols_of(w)
                    hi(gh[:, w % 2, 0:n], graw[:, w % 2, 0:n]).then_inc(g_hi, 1)

                def q_split(u):
                    sc.wait_ge(q_landed, u * 16 + 16)
                    sc.wait_ge(qt_done, u + 1)
                    hi(qwh[:, :, :], qraw[:, :, :]).then_inc(q_hi, 1)

                def a_split(c, w, extra=0):
                    sc.wait_ge(g_used, G(b, w - 2) + extra)
                    hi(ah[:, c % 2, :], act[:, c, :]).then_inc(a_hi, 1)

                def evac(k, o, phase, w_last):
                    wait_bank(sc, b, phase, k, w_last)
                    hi(o, ps[:, k, :]).then_inc(ev_hi, 1)

                def xt_split(p):
                    for c in range(DC):
                        sc.wait_ge(xt_ready, b * (4 * DC) + (p * DC + c + 1))
                        hi(xh[:, c, :], ps[:, c, :], lnw_sb[:, c:c + 1] if p == 0 else 1.0).then_inc(xt_hi, 1)

                def ctx_split(pas, c):
                    sc.wait_ge(ctx_landed[c % 2], b * (2 * DC * 8) + (pas * DC // 2 + c // 2 + 1) * 16)
                    hi(ch[:, c, :], craw[:, c % 2, :]).then_inc(ctx_hi, 1)

                for c in range(DC):
                    g_split(G_KV0 + c)
                    ctx_split(0, c)
                g_split(G_Q0)
                for k in range(8):
                    evac(k, stage(ST_K0 + k)[0] if k < 4 else v0h[:, 2 * k - 8:2 * k - 6, :].rearrange("p a n -> p (a n)"), F_KV0, G_KV0 + 7)
                g_split(G_Q0 + 1)
                xt_split(0)
                for i in range(ST_K0, ST_K1):
                    sc.wait_ge(*stored(b, i))
                for g in range(KV0):
                    sc.wait_ge(g_used, G(b, G_Q0 + g))
                    hi(qh[:, g, :], ps[:, g, :], SCALE0).then_inc(ev_hi, 1)
                    g_split(G_Q0 + g + 2)

                def q_evac(h, j, o, scale):
                    sc.wait_ge(qt_done, head1(b, h, j) + 2)
                    hi(o, ps[:, q_bank(j), :], scale).then_inc(qt_hi, 1)

                def exp0(g, par, j, t):
                    a = tile0(b, g, j, t)
                    sc.wait_ge(mx_done, a + 1)
                    sc.activation(e0[:, (j % 2) * TT + t, :], ps[:, 2 * (t % 2):2 * (t % 2) + 2, :].rearrange("p a n -> p (a n)"),
                                  ACT.Exp, bias=nmax[:, j % 2, t:t + 1], accum_out=rs[:, par, t, j:j + 1]).then_inc(e_done, 1)

                def p_split(n, bank, o, slot, slots):
                    sc.wait_ge(t_ready, n + 1)
                    sc.wait_ge(p_used, n + (1 + NUSED - slots))
                    hi(o[:, slot, :], ps[:, bank, :]).then_inc(p_hi, 1)

                def p_split0(g, j, c):
                    p_split(chunk0(b, g, j, c), TB0[place0(j, c) % NPT], ph0, c % PT0, PT0)

                def copy_rb(u, o, bank):
                    sc.wait_ge(rb_ready, u + 1)
                    sc.wait_ge(act_done, u + 1)
                    sc.copy(o, ps[:, bank, :]).then_inc(rb_done, 1)

                def group0(g, par, more):
                    for j in range(R0):
                        for t in range(TT):
                            if j == R0 - 1 and t == 2:
                                copy_rb(unit0(b, g), rb0[:, :], RB0)
                            p_split0(g, j, 2 * t)
                            p_split0(g, j, 2 * t + 1)
                            if not more and j == R0 - 1 and t < 2:
                                a_split(t, G_WO0 + t)
                            if j < R0 - 1:
                                exp0(g, par, j + 1, t)
                            elif more:
                                exp0(g + 1, 1 - par, 0, t)

                for t in range(TT):
                    exp0(0, 0, 0, t)
                with sc.Fori(0, KV0 // 2 - 1) as r:
                    group0(r * 2, 0, True)
                    group0(r * 2 + 1, 1, True)
                group0(KV0 - 2, 0, True)
                group0(KV0 - 1, 1, False)

                for c in range(2, DC):
                    g_split(G_WO0 + c)
                    sc.wait_ge(act_done, unit0(b, c) + 2)
                    a_split(c, G_WO0 + c)
                    if c == 2:
                        sc.wait_ge(act_done, unit0(b, KV0 - 1) + 2)
                    ctx_split(1, c - 2)
                ctx_split(1, 6)
                g_split(G_K1)
                ctx_split(1, 7)
                for c in range(1, DC):
                    g_split(G_K1 + c)

                g_split(G_A0)
                for k in range(8):
                    wait_slot(sc, b, ST_K1 + k)
                    evac(k, stage(ST_K1 + k)[0], F_K1, G_K1 + 7)
                g_split(G_BASE)
                xt_split(1)
                sc.wait_ge(ff_dve, b * NFD + 2)
                sc.activation(ex0[:, :, :], comb[:, :, :], ACT.Exp).then_inc(ff_act, 1)
                sc.wait_ge(g_used, G(b, G_A0))
                sc.copy(act[:, 1, :], ps[:, LOW0, :]).then_inc(ff_act, 1)
                for c in range(1, DC):
                    g_split(G_BASE + c)
                g_split(G_B0)
                sc.wait_ge(ff_dve, b * NFD + 4)
                sc.wait_ge(*stored(b, ST_K1))
                a_split(0, G_B0)

                for c in range(DC):
                    g_split(G_V1 + c)
                g_split(G_KV1)
                for k in range(8):
                    wait_slot(sc, b, ST_V1 + k)
                    evac(k, stage(ST_V1 + k)[0], F_V1, G_V1 + 7)
                g_split(G_KV1 + 1)
                xt_split(2)
                for c in range(2, DC):
                    g_split(G_KV1 + c)
                for k in range(8):
                    wait_slot(sc, b, ST_KV1 + k)
                    evac(k, stage(ST_KV1 + k)[0], F_KV1, G_KV1 + 7)
                with sc.Fori(0, KV1) as h:
                    def exp1(j, t):
                        sc.wait_ge(mx_done, tile1(b, h, j, t) + 1)
                        k = s_bank(j, t)
                        sc.activation(e1[:, (j % 2) * TT + t, :], ps[:, k:k + 3, :].rearrange("p a n -> p (a n)"),
                                      ACT.Exp, bias=nmax[:, j % 2, t:t + 1], accum_out=rs[:, j % 2, t, 0:1]).then_inc(e_done, 1)

                    def p_split1(j, c):
                        p_split(chunk1(b, h, j, c), TB1[c % NPT], ph1, c % PT1, PT1)

                    q_split(head1(b, h, 0))
                    q_evac(h, 0, q1h[:, 0, :], SCALE1)
                    q_split(head1(b, h, 1))
                    for t in range(TT):
                        exp1(0, t)
                    q_evac(h, 1, q1h[:, 1, :], SCALE1)
                    q_split(head1(b, h, 2))
                    for j in range(R1):
                        for t in range(TT):
                            for i in range(3):
                                if i == 2 and j < R1 - 1:
                                    exp1(j + 1, t)
                                p_split1(j, 3 * t + i)
                                if t == 3 and i == 0 and j < R1 - 3:
                                    q_split(head1(b, h, j + 3))
                            if t == 2 and j < R1 - 2:
                                q_evac(h, j + 2, q1h[:, j % 2, :], SCALE1)
                            if t == TT - 1:
                                copy_rb(unit1(b, h, j), rb1[:, :], QB)
                            if j == R1 - 1 and t < 2:
                                g_split(G_WO1 + t, h * DC, h * (DC * 8))
                                sc.wait_ge(act_done, unit1(b, h, t) + 2)
                                a_split(t, G_WO1 + t, h * DC)
                    for c in range(2, R1):
                        g_split(G_WO1 + c, h * DC, h * (DC * 8))
                        sc.wait_ge(act_done, unit1(b, h, c) + 2)
                        a_split(c, G_WO1 + c, h * DC)

                g_split(G_Z)
                g_split(G_Z + 1)
                xt_split(3)
                for c in range(2, DC):
                    g_split(G_Z + c)
                    if c == 4:
                        sc.wait_ge(ff_dve, b * NFD + 6)
                        sc.activation(ex1[:, :, :], sc3[:, :, :], ACT.Exp).then_inc(ff_act, 1)
                    if c == 6:
                        sc.wait_ge(ff_pe, b * NFP + 6)
                        for k in range(ZB):
                            cp = sc.copy(act[:, ZB + k, :], ps[:, GATE1[k], :])
                        cp.then_inc(ff_act, 1)
                g_split(G_BW)
                for c in range(ZB):
                    if c >= 1:
                        g_split(G_BW + c)
                    sc.wait_ge(ff_dve, b * NFD + 8 + c)
                    a_split(c, G_BW + c)

        @block.gpsimd
        def _(po):
            po.sem_inc(g_lo, 2)
            po.sem_inc(q_lo, 1)
            po.memset(neghalf[:, :], -0.5).then_inc(pool_c, 1)
            po.memset(ident[:, :], 0.0).then_inc(pool_c, 1)
            po.wait_ge(pool_c, 2)
            po.affine_select(out=ident[:, :], in_=ident[:, :], compare_op=ALU.not_equal, fill=1.0, base=0,
                             pattern=[[-1, P]], channel_multiplier=1).then_inc(const_ready, 1)

            with po.Fori(0, B) as b:
                def lo(o, i, h):
                    return po.tensor_tensor(o, i, h.bitcast(F32), ALU.subtract)

                def g_split(w, extra=0):
                    po.wait_ge(g_hi, b * NG + extra + (w + 1))
                    n = cols_of(w)
                    s = w % 2
                    lo(gl[:, s, 0:n], graw[:, s, 0:n], gh[:, s, 0:n]).then_inc(g_lo, 1)

                def q_split(u):
                    po.wait_ge(q_hi, u + 1)
                    lo(qwl[:, :, :], qraw[:, :, :], qwh[:, :, :]).then_inc(q_lo, 1)

                def inv_root(i):
                    po.wait_ge(ln_dve, b * NLN + (i + 1))
                    po.tensor_tensor(rstd[:, :], ve[:, :], neghalf[:, :], ALU.pow).then_inc(ln_pool, 1)

                def ctx_split(pas, c):
                    po.wait_ge(ctx_hi, b * (2 * DC) + (pas * DC + c + 1))
                    lo(cl[:, c, :], craw[:, c % 2, :], ch[:, c, :]).then_inc(ctx_lo, 1)

                for c in range(DC):
                    g_split(G_KV0 + c)
                    ctx_split(0, c)
                    if c in (3, 5):
                        inv_root((c - 3) // 2)
                for w in range(G_Q0, G_WO0 + 2):
                    g_split(w)

                def widen(g, par):
                    po.wait_ge(rinv_done, unit0(b, g) + 1)
                    po.wait_ge(rb_done, unit0(b, g) + 1)
                    po.sem_inc(pool_steps, 1)
                    po.tensor_copy(rwide[:, :, :].rearrange("p t (j d) -> p (t j) d", d=HD0),
                                   rinv[:, par].rearrange("p t j -> p (t j)").unsqueeze(2).to_broadcast([P, TT * R0, HD0])).then_inc(rwide_done, 1)

                with po.Fori(0, KV0 // 2) as r:
                    for par in range(2):
                        widen(r * 2 + par, par)
                for c in range(2, DC):
                    g_split(G_WO0 + c)
                    ctx_split(1, c - 2)
                ctx_split(1, 6)
                g_split(G_K1)
                ctx_split(1, 7)
                for c in range(1, DC):
                    g_split(G_K1 + c)
                    if c == 3:
                        inv_root(2)
                po.wait_ge(xn_ready, b * (4 * TT) + 2 * TT)
                po.wait_ge(bias_landed, b * 16 + 16)
                for t in range(TT):
                    add = po.tensor_tensor(x[:, t, :], x[:, t, :], bias_sb[:, :], ALU.add)
                add.then_inc(bias_added, 1)
                for w in range(G_A0, G_KV1 + 8):
                    g_split(w)
                    if w == G_V1 + 3:
                        inv_root(3)
                with po.Fori(0, KV1) as h:
                    for j in range(R1):
                        q_split(head1(b, h, j))
                    for c in range(R1):
                        g_split(G_WO1 + c, h * DC)
                g_split(G_Z)
                g_split(G_Z + 1)
                inv_root(4)
                for w in range(G_Z + 2, NG):
                    g_split(w)

        @block.vector
        def _(v):
            v.sem_inc(p_lo, NPT)
            v.sem_inc(acc_evac, 1)
            v.sem_inc(act_done, 1)
            v.sem_inc(qt_lo, 1)
            v.memset(wrh[:, :, :].bitcast(F32), 0.0).then_inc(dve_c, 1)
            v.memset(wrl[:, :, :].bitcast(F32), 0.0).then_inc(dve_c, 1)
            for i in range(8 - TOP0):
                v.memset(pv[:, :, E0 + i:E0 + i + 1], -1.0 - i)
                pad = v.memset(rp[:, :, TOP0 + i:TOP0 + i + 1], -1.0 - i)
            pad.then_inc(dve_c, 1)
            v.wait_ge(dve_c, 3)
            v.wait_ge(const_hi, 2)
            w0, w1 = slice(RC0, RC0 + E0), slice(0, RD1)
            v.tensor_tensor(wrl[:, :, w0], wr0_raw[:, :, :], wrh[:, :, w0].bitcast(F32), ALU.subtract).then_inc(const_ready, 1)
            v.tensor_tensor(wrl[:, :, w1], wr1_raw[:, :, :], wrh[:, :, w1].bitcast(F32), ALU.subtract).then_inc(const_ready, 1)

            with v.Fori(0, B) as b:
                links = [0]

                def link(ins):
                    links[0] += 1
                    ins.then_inc(dv, 1)
                    v.wait_ge(dv, b * NDV + links[0])
                    v.sem_inc(dve_steps, 1)

                def lo(o, i, h):
                    return v.tensor_tensor(o, i, h.bitcast(F32), ALU.subtract)

                def scaled_lo(o, i, scale, h):
                    return v.scalar_tensor_tensor(out=o, in0=i, scalar=scale, in1=h.bitcast(F32), op0=ALU.mult, op1=ALU.subtract)

                def row_stats(src):
                    for t in range(TT):
                        for i in range(2):
                            st = v.bn_stats(stats[:, t, 6 * i:6 * i + 6], src[:, t, 512 * i:512 * i + 512])
                    link(st)
                    for t in range(TT):
                        ag = v.bn_aggr(mv[:, t, :], stats[:, t, :])
                    link(ag)

                def norm(p):
                    row_stats(x)
                    v.tensor_scalar(ve[:, :], mv[:, :, 1], EPS, None, ALU.add).then_inc(ln_dve, 1)
                    v.wait_ge(ln_pool, b * NLN + (1 if p == 0 else p + 2))
                    for t in range(TT):
                        nm = v.tensor_scalar(xn[:, t, :], x[:, t, :], mv[:, t, 0:1], rstd[:, t:t + 1], ALU.subtract, ALU.mult)
                        if p > 0:
                            nm.then_inc(xn_ready, 1)
                    if p > 0:
                        return
                    link(nm)
                    row_stats(xn)
                    link(v.tensor_tensor(ve[:, :], mv[:, :, 0], mv[:, :, 0], ALU.mult))
                    link(v.tensor_tensor(ve[:, :], ve[:, :], mv[:, :, 1], ALU.add))
                    v.tensor_scalar(ve[:, :], ve[:, :], EPS, None, ALU.add).then_inc(ln_dve, 1)
                    v.wait_ge(ln_pool, b * NLN + 2)
                    for t in range(TT):
                        v.tensor_scalar(xn[:, t, :], xn[:, t, :], rstd[:, t:t + 1], None, ALU.mult).then_inc(xn_ready, 1)

                def xt_split(p):
                    for c in range(DC):
                        v.wait_ge(xt_hi, b * (4 * DC) + (p * DC + c + 1))
                        if p == 0:
                            ins = scaled_lo(xl[:, c, :], ps[:, c, :], lnw_sb[:, c:c + 1], xh[:, c, :])
                        else:
                            ins = lo(xl[:, c, :], ps[:, c, :], xh[:, c, :])
                        ins.then_inc(xt_lo, 1)

                def evac(k, i, o, h):
                    v.wait_ge(ev_hi, b * NEV + (i + 1))
                    lo(o, ps[:, k, :], h).then_inc(acc_evac, 1)

                def add_banks(phase, w_last, ph_extra=0, w_extra=0):
                    for k in range(8):
                        wait_bank(v, b, phase, k, w_last, ph_extra, w_extra)
                        xs = x[:, k // 2, (k % 2) * 512:(k % 2 + 1) * 512]
                        v.tensor_tensor(xs, ps[:, k, :], xs, ALU.add).then_inc(acc_evac, 1)

                def added(n):
                    v.wait_ge(acc_evac, b * NACC + (n + 1))

                def a_split(c, i, extra=0):
                    v.wait_ge(a_hi, b * NA + extra + (i + 1))
                    lo(al[:, c % 2, :], act[:, c, :], ah[:, c % 2, :]).then_inc(a_lo, 1)

                v.wait_ge(x_landed, b * 16 + 16)
                norm(0)
                for k in range(8):
                    if k < 4:
                        evac(k, k, *reversed(stage(ST_K0 + k)))
                    else:
                        w = slice(2 * k - 8, 2 * k - 6)
                        evac(k, k, v0l[:, w, :].rearrange("p a n -> p (a n)"), v0h[:, w, :].rearrange("p a n -> p (a n)"))
                xt_split(0)
                def lay_values(g):
                    v.wait_ge(p_used, chunk0(b, g, 0, 0) + NUSED)
                    o = slice(P - HD0, P)
                    v.tensor_copy(vph[:, :, o], v0h[:, :, ds(g * HD0, HD0)].bitcast(F32))
                    v.tensor_copy(vpl[:, :, o], v0l[:, :, ds(g * HD0, HD0)].bitcast(F32)).then_inc(vp_ready, 1)

                for g in range(KV0):
                    if g == 1:
                        v.memset(vph[:, :, :].bitcast(F32), 0.0)
                    if g == 2:
                        link(v.memset(vpl[:, :, :].bitcast(F32), 0.0))
                        lay_values(0)
                    v.wait_ge(ev_hi, b * NEV + (V_Q0 + g + 1))
                    scaled_lo(ql[:, g, :], ps[:, g, :], SCALE0, qh[:, g, :]).then_inc(acc_evac, 1)

                def q_evac(i, j, o, scale, h):
                    v.wait_ge(qt_hi, i + 1)
                    scaled_lo(o, ps[:, q_bank(j), :], scale, h).then_inc(qt_lo, 1)

                def max0(g, j, t):
                    v.wait_ge(s_ready, tile0(b, g, j, t) + 1)
                    v.tensor_reduce(nmax[:, j % 2, t:t + 1], ps[:, 2 * (t % 2):2 * (t % 2) + 2, :].rearrange("p a n -> p (a n)"),
                                    X, ALU.max, negate=True).then_inc(mx_done, 1)

                def p_split(n, bank, o, h, slot):
                    v.wait_ge(p_hi, n + 1)
                    lo(o[:, slot, :], ps[:, bank, :], h[:, slot, :]).then_inc(p_lo, 1)

                def invert(u, o, i, exps):
                    v.wait_ge(e_done, exps)
                    v.reciprocal(o, i).then_inc(rinv_done, 1)

                def scale_out(u, o, rb, n):
                    v.wait_ge(p_used, n + (1 + NUSED))
                    v.wait_ge(rb_done, u + 2)
                    v.tensor_tensor(o, ps[:, PVB, :], rb, ALU.mult).then_inc(act_done, 1)

                def step0(g, par, j, t, more):
                    if j < R0 - 1:
                        max0(g, j + 1, t)
                    elif more:
                        max0(g + 1, 0, t)
                    if j == R0 - 1 and t == 0:
                        invert(unit0(b, g), rinv[:, par], rs[:, par], tile0(b, g, R0 - 1, TT - 1) + 3)
                    for c in (2 * t, 2 * t + 1):
                        p_split(chunk0(b, g, j, c), TB0[place0(j, c) % NPT], pl0, ph0, c % PT0)
                    if not more and j == R0 - 1 and t < 2:
                        a_split(t, X_WO0 + t)

                def group0(g, par, more):
                    for j in range(R0):
                        for t in range(TT):
                            if j > 0 or t > 0:
                                step0(g, par, j, t, more)
                    if more:
                        step0(g + 1, 1 - par, 0, 0, True)
                    scale_out(unit0(b, g), act[:, ds(g, 1), :].rearrange("p a n -> p (a n)"), rb0[:, :], chunk0(b, g, R0 - 1, C0 - 1))
                    if more:
                        lay_values(g + 1)

                for t in range(TT):
                    max0(0, 0, t)
                step0(0, 0, 0, 0, True)
                with v.Fori(0, KV0 // 2 - 1) as r:
                    group0(r * 2, 0, True)
                    group0(r * 2 + 1, 1, True)
                group0(KV0 - 2, 0, True)
                group0(KV0 - 1, 1, False)

                for c in range(2, DC):
                    a_split(c, X_WO0 + c)
                add_banks(F_WO0, G_WO0 + 7)
                added(A_WO0 + 8)

                norm(1)
                for k in range(8):
                    evac(k, V_K1 + k, *reversed(stage(ST_K1 + k)))
                xt_split(1)
                v.wait_ge(ff_pe, b * NFP + 1)
                v.tensor_copy(logT[:, :], ps[:, ROUTER, :]).then_inc(ff_dve, 1)
                v.wait_ge(ff_pe, b * NFP + 2)
                link(v.tensor_copy(comb[:, :, :], ps[:, ROUTED, :].rearrange("p (t e) -> p t e", t=TT)[:, :, RC0:RC0 + E0]))
                link(v.tensor_reduce(t4[:, 0, :], comb[:, :, :], X, ALU.max))
                v.tensor_tensor(comb[:, :, :], comb[:, :, :], t4[:, 0, :].unsqueeze(2).to_broadcast([P, TT, E0]), ALU.subtract).then_inc(ff_dve, 1)
                v.wait_ge(ff_act, b * NFA + 1)
                link(v.tensor_reduce(t4[:, 1, :], ex0[:, :, :], X, ALU.add))
                link(v.reciprocal(t4[:, 2, :], t4[:, 1, :]))
                link(v.tensor_tensor(pv[:, :, 0:E0], ex0[:, :, :], t4[:, 2, :].unsqueeze(2).to_broadcast([P, TT, E0]), ALU.mult))
                for t in range(TT):
                    ins = v.max(m8[:, t, :], pv[:, t, 0:E0])
                link(ins)
                v.tensor_tensor(t4[:, 3, :], m8[:, :, 0], m8[:, :, 1], ALU.add)
                link(v.tensor_copy(rp[:, :, 0:TOP0], m8[:, :, 0:TOP0]))
                for t in range(TT):
                    ins = v.match_replace(mr[:, t, :], rp[:, t, :], pv[:, t, :], -9.0)
                link(ins)
                v.reciprocal(t4[:, 0, :], t4[:, 3, :])
                link(v.tensor_tensor(ex0[:, :, :], mr[:, :, 0:E0], pv[:, :, 0:E0], ALU.not_equal))
                link(v.tensor_tensor(comb[:, :, :], ex0[:, :, :], pv[:, :, 0:E0], ALU.mult))
                link(v.scalar_tensor_tensor(out=comb[:, :, :], in0=comb[:, :, :], scalar=GAIN0, in1=t4[:, 0, :].unsqueeze(2).to_broadcast([P, TT, E0]),
                                            op0=ALU.mult, op1=ALU.mult))
                v.tensor_copy(gwide0[:, :, :].rearrange("p t (e r) -> p (t e) r", r=RK0),
                              comb[:, :, :].rearrange("p t e -> p (t e)").unsqueeze(2).to_broadcast([P, TT * E0, RK0])).then_inc(ff_dve, 1)
                v.wait_ge(ff_pe, b * NFP + 3)
                v.wait_ge(ff_act, b * NFA + 2)
                v.tensor_tensor(act[:, 0, :], ps[:, GATE0, :], act[:, 1, :], ALU.mult).then_inc(ff_dve, 1)
                a_split(0, X_B0)
                v.wait_ge(bias_added, b + 1)
                add_banks(F_BASE, G_B0)
                added(A_BASE + 8)

                norm(2)
                for k in range(8):
                    evac(k, V_V1 + k, *reversed(stage(ST_V1 + k)))
                xt_split(2)
                for k in range(8):
                    evac(k, V_KV1 + k, *reversed(stage(ST_KV1 + k)))

                with v.Fori(0, KV1) as h:
                    def max1(j, t):
                        v.wait_ge(s_ready, tile1(b, h, j, t) + 1)
                        v.tensor_reduce(nmax[:, j % 2, t:t + 1], ps[:, s_bank(j, t):s_bank(j, t) + 3, :].rearrange("p a n -> p (a n)"), X, ALU.max,
                                        negate=True).then_inc(mx_done, 1)

                    q_evac(head1(b, h, 0), 0, q1l[:, 0, :], SCALE1, q1h[:, 0, :])
                    for t in range(TT):
                        max1(0, t)
                    q_evac(head1(b, h, 1), 1, q1l[:, 1, :], SCALE1, q1h[:, 1, :])
                    for j in range(R1):
                        u = unit1(b, h, j)
                        for t in range(TT):
                            if j < R1 - 1:
                                max1(j + 1, t)
                            if t == 0:
                                invert(u, rinv[:, j % 2, :, 0], rs[:, j % 2, :, 0], tile1(b, h, j, TT - 1) + 3)
                            for i in range(3):
                                p_split(chunk1(b, h, j, 3 * t + i), TB1[i % NPT], pl1, ph1, i % PT1)
                                if t == 0 and i == 0 and j > 0:
                                    scale_out(u - 1, act[:, j - 1, :], rb1[:, :], chunk1(b, h, j - 1, C1 - 1))
                            if j == R1 - 1 and t < 2:
                                a_split(t, X_WO1 + t, h * R1)
                            if t == 2 and j < R1 - 2:
                                q_evac(head1(b, h, j) + 2, j + 2, q1l[:, j % 2, :], SCALE1, q1h[:, j % 2, :])
                    scale_out(unit1(b, h, R1 - 1), act[:, R1 - 1, :], rb1[:, :], chunk1(b, h, R1 - 1, C1 - 1))
                    for c in range(2, R1):
                        a_split(c, X_WO1 + c, h * R1)
                    add_banks(F_WO1, G_WO1 + 7, h * 7, h * DC)

                added(A_WO1 + 8 * KV1)
                norm(3)
                xt_split(3)
                v.wait_ge(ff_pe, b * NFP + 4)
                v.tensor_copy(q16T[:, :], ps[0:RD1, ROUTER, :]).then_inc(ff_dve, 1)
                v.wait_ge(ff_pe, b * NFP + 5)
                link(v.tensor_copy(sc1[:, :, :], ps[:, ROUTED, 0:TT * E1].rearrange("p (t e) -> p t e", t=TT)))
                for t in range(TT):
                    ins = v.max(m16[:, t, 0:8], sc1[:, t, :])
                link(ins)
                for t in range(TT):
                    ins = v.match_replace(sc2[:, t, :], m16[:, t, 0:8], sc1[:, t, :], LOWEST)
                link(ins)
                for t in range(TT):
                    ins = v.max(m16[:, t, 8:16], sc2[:, t, :])
                link(ins)
                for t in range(TT):
                    ins = v.match_replace(sc3[:, t, :], m16[:, t, 8:16], sc2[:, t, :], LOWEST)
                link(ins)
                link(v.tensor_tensor(sc2[:, :, :], sc3[:, :, :], sc1[:, :, :], ALU.not_equal))
                v.tensor_tensor(sc3[:, :, :], sc1[:, :, :], m16[:, :, 0:1].to_broadcast([P, TT, E1]), ALU.subtract).then_inc(ff_dve, 1)
                v.wait_ge(ff_act, b * NFA + 3)
                link(v.tensor_tensor(sc1[:, :, :], ex1[:, :, :], sc2[:, :, :], ALU.mult))
                link(v.tensor_reduce(t4[:, 0, :], sc1[:, :, :], X, ALU.add))
                link(v.reciprocal(t4[:, 1, :], t4[:, 0, :]))
                link(v.scalar_tensor_tensor(out=sc1[:, :, :], in0=sc1[:, :, :], scalar=GAIN1, in1=t4[:, 1, :].unsqueeze(2).to_broadcast([P, TT, E1]),
                                            op0=ALU.mult, op1=ALU.mult))
                v.tensor_copy(gwide1[:, :, :].rearrange("p t (e r) -> p (t e) r", r=RK1),
                              sc1[:, :, :].rearrange("p t e -> p (t e)").unsqueeze(2).to_broadcast([P, TT * E1, RK1])).then_inc(ff_dve, 1)
                v.wait_ge(ff_act, b * NFA + 4)
                v.wait_ge(g_used, G(b, G_Z + 7))
                for k in range(ZB):
                    v.tensor_tensor(act[:, k, :], ps[:, ZB0 + k, :], act[:, ZB + k, :], ALU.mult).then_inc(ff_dve, 1)
                    if k == 1:
                        a_split(0, X_BW)
                for c in range(1, ZB):
                    a_split(c, X_BW + c)
                add_banks(F_BW, NG - 1)
                assert links[0] == NDV, links[0]


def _layout(np, a):
    t = lambda w: np.ascontiguousarray(w.T)
    return {
        "x_in": a["x"],
        "ctxT": np.ascontiguousarray(a["ctx_4096"].transpose(0, 2, 1)),
        "w_kv0": np.concatenate([a["L0_xattn_wk"].T, a["L0_xattn_wv"].T], axis=1),
        "w_kv1": np.concatenate([a["L1_xattn_Wk"], a["L1_xattn_Wv"]], axis=1),
        "wq0": t(a["L0_xattn_wq"]),
        "wo0": t(a["L0_xattn_wo"]),
        "lnw": t(a["L0_xattn_ln_w"].reshape(DC, P)),
        "wbase": t(a["L0_ffn_W_base"]),
        "bbase": a["L0_ffn_b_base"],
        "a0": t(a["L0_ffn_A"].reshape(E0 * RK0, D)),
        "b0": np.ascontiguousarray(a["L0_ffn_B"].transpose(0, 2, 1)).reshape(E0 * RK0, D),
        "wr0": t(a["L0_ffn_W_router"]),
        "wq1": a["L1_xattn_Wq"],
        "wo1": a["L1_xattn_Wo"],
        "aw": t(a["L1_ffn_A_w"]),
        "bw": t(a["L1_ffn_B_w"]),
        "wr1": t(a["L1_ffn_Wq_w"]),
        "keysT": t(a["L1_ffn_keys"]),
    }


def kernel(**inputs):
    import numpy as _np
    import concourse.bacc as _bacc
    from concourse import mybir as _mybir
    from concourse.bass_utils import run_bass_kernel_spmd as _run

    nc = _bacc.Bacc("TRN2", target_bir_lowering=False, num_devices=1, dynamic_dma_scratch_size=1024)
    arrays, args = {}, []
    for name, a in _layout(_np, {k: _np.asarray(v) for k, v in inputs.items()}).items():
        a = _np.ascontiguousarray(a)
        arrays[f"in_{name}_dram"] = a
        args.append(nc.dram_tensor(f"in_{name}_dram", a.shape, _mybir.dt.from_np(a.dtype), kind="ExternalInput").ap())
    args.append(nc.dram_tensor("out_0_dram", (B, T, D), _mybir.dt.float32, kind="ExternalOutput").ap())
    block_program(nc, *args)
    r = _run(nc, [arrays], core_ids=[0])
    return r.results[0]["out_0_dram"]
```
